# Optimizing a Trainium2 kernel written in Bass

```python
import numpy as np
import jax
import jax.numpy as jnp

def _softmax(x, axis=-1):
    return jax.nn.softmax(x, axis=axis)

def _gelu(x):
    return jax.nn.gelu(x, approximate=True)

def _silu(x):
    return jax.nn.silu(x)

def _sigmoid(x):
    return jax.nn.sigmoid(x)

def _layernorm(x, axis=-1, eps=1e-05):
    m = jnp.mean(x, axis=axis, keepdims=True)
    v = jnp.var(x, axis=axis, keepdims=True)
    return (x - m) / jnp.sqrt(v + eps)

def _scatter_add(tgt, idx, src, axis=0):
    return tgt.at[idx].add(src)

def _segment_sum(src, seg, n):
    return jax.ops.segment_sum(src, seg, n)
kernel_name = 'mk_vit_tower_d1_tok_img1024_r4_e7ac50'

def setup_inputs(seed: int=0):
    np.random.seed(seed)
    _w = jnp.asarray

    def _rec_inputs():
        import jax
        import jax.numpy as jnp
        _rk = jax.random.key(seed)
        x = -7.10856e-05 + 0.999911 * jax.random.normal(jax.random.fold_in(_rk, 1), (4, 1, 1024, 256), jnp.float32)
        return x
    x = _rec_inputs()

    def _L0_tok_setup():
        import jax, jax.numpy as jnp
        import numpy as np
        B, T, X, D, H = (16, 1, 1024, 256, 128)
        key = jax.random.key(seed)
        k0, k1, k2 = jax.random.split(key, 3)
        s1 = 1.0 / np.sqrt(D)
        s2 = 1.0 / np.sqrt(H)
        return {'encoder_outputs': jax.random.normal(k0, (B, T, X, D), dtype=jnp.float32), 'W1': jax.random.uniform(k1, (D, H), minval=-s1, maxval=s1, dtype=jnp.float32), 'b1': jnp.zeros((H,), dtype=jnp.float32), 'W2': jax.random.uniform(k2, (H, 1), minval=-s2, maxval=s2, dtype=jnp.float32), 'b2': jnp.zeros((1,), dtype=jnp.float32)}
    _L0_tok_all = _L0_tok_setup()
    _L0_tok_in = {k: v for k, v in _L0_tok_all.items() if k in ('W1', 'b1', 'W2', 'b2')}
    del _L0_tok_all

    def _L0_attn_setup():
        import jax, jax.numpy as jnp
        import numpy as np
        import math
        B, T, C, FFN = (8, 512, 256, 1024)
        LAYER_ID, N_LAYER = (1, 12)

        def layer_norm(x, g, b, eps=1e-05):
            m = jnp.mean(x, axis=-1, keepdims=True)
            v = jnp.mean(jnp.square(x - m), axis=-1, keepdims=True)
            return (x - m) * jax.lax.rsqrt(v + eps) * g + b

        def token_shift(x):
            return jnp.concatenate([jnp.zeros_like(x[:, :1]), x[:, :-1]], axis=1)

        def wkv(w, u, k, v):
            w = -jnp.exp(w)
            kT = jnp.swapaxes(k, 0, 1)
            vT = jnp.swapaxes(v, 0, 1)

            def step(carry, kv_t):
                aa, bb, pp = carry
                kt, vt = kv_t
                ww = u + kt
                p = jnp.maximum(pp, ww)
                e1 = jnp.exp(pp - p)
                e2 = jnp.exp(ww - p)
                y = (e1 * aa + e2 * vt) / (e1 * bb + e2)
                ww2 = pp + w
                p2 = jnp.maximum(ww2, kt)
                e1b = jnp.exp(ww2 - p2)
                e2b = jnp.exp(kt - p2)
                return ((e1b * aa + e2b * vt, e1b * bb + e2b, p2), y)
            z = jnp.zeros((k.shape[0], k.shape[2]), k.dtype)
            init = (z, z, jnp.full_like(z, -1e+38))
            _, yT = jax.lax.scan(step, init, (kT, vT))
            return jnp.swapaxes(yT, 0, 1)
        key = jax.random.key(seed)
        ks = jax.random.split(key, 8)
        x = jax.random.normal(ks[0], (B, T, C), jnp.float32)
        r0 = LAYER_ID / (N_LAYER - 1)
        r1 = 1.0 - LAYER_ID / N_LAYER
        ddd = (jnp.arange(C, dtype=jnp.float32) / C).reshape(1, 1, C)
        att_mix_k = jnp.power(ddd, r1)
        att_mix_v = jnp.power(ddd, r1) + 0.3 * r0
        att_mix_r = jnp.power(ddd, 0.5 * r1)
        h = jnp.arange(C, dtype=jnp.float32)
        time_decay = -5.0 + 8.0 * jnp.power(h / (C - 1), 0.7 + 1.3 * r0)
        zigzag = ((jnp.arange(C) + 1) % 3 - 1).astype(jnp.float32) * 0.5
        time_first = jnp.full((C,), math.log(0.3), jnp.float32) + zigzag
        ffn_mix_k = jnp.power(ddd, r1)
        ffn_mix_r = jnp.power(ddd, r1)
        s = 0.02
        return {'x': x, 'ln1_g': jnp.ones((C,), jnp.float32), 'ln1_b': jnp.zeros((C,), jnp.float32), 'ln2_g': jnp.ones((C,), jnp.float32), 'ln2_b': jnp.zeros((C,), jnp.float32), 'att_mix_k': att_mix_k, 'att_mix_v': att_mix_v, 'att_mix_r': att_mix_r, 'time_decay': time_decay, 'time_first': time_first, 'Wk': s * jax.random.normal(ks[1], (C, C), jnp.float32), 'Wv': s * jax.random.normal(ks[2], (C, C), jnp.float32), 'Wr': s * jax.random.normal(ks[3], (C, C), jnp.float32), 'Wo': s * jax.random.normal(ks[4], (C, C), jnp.float32), 'ffn_mix_k': ffn_mix_k, 'ffn_mix_r': ffn_mix_r, 'Wk_ffn': s * jax.random.normal(ks[5], (FFN, C), jnp.float32), 'Wr_ffn': s * jax.random.normal(ks[6], (C, C), jnp.float32), 'Wv_ffn': s * jax.random.normal(ks[7], (C, FFN), jnp.float32)}
    _L0_attn_all = _L0_attn_setup()
    _L0_attn_in = {k: v for k, v in _L0_attn_all.items() if k in ('ln1_g', 'ln1_b', 'ln2_g', 'ln2_b', 'att_mix_k', 'att_mix_v', 'att_mix_r', 'time_decay', 'time_first', 'Wk', 'Wv', 'Wr', 'Wo', 'ffn_mix_k', 'ffn_mix_r', 'Wk_ffn', 'Wr_ffn', 'Wv_ffn')}
    del _L0_attn_all

    def _L0_ffn_setup():
        import jax, jax.numpy as jnp
        import numpy as np
        CAPACITY_FACTOR = 0.5
        NUM_HEADS = 16
        key = jax.random.key(seed)
        ks = jax.random.split(key, 6)
        B, N, D = (4, 1024, 256)
        s = 1.0 / np.sqrt(D)
        return {'token_inputs': jax.random.normal(ks[0], (B, N, D), jnp.float32), 'Wg': jax.random.normal(ks[1], (D, 1), jnp.float32) * s, 'Wq': jax.random.normal(ks[2], (D, D), jnp.float32) * s, 'Wk': jax.random.normal(ks[3], (D, D), jnp.float32) * s, 'Wv': jax.random.normal(ks[4], (D, D), jnp.float32) * s, 'Wo': jax.random.normal(ks[5], (D, D), jnp.float32) * s}
    _L0_ffn_all = _L0_ffn_setup()
    _L0_ffn_in = {k: v for k, v in _L0_ffn_all.items() if k in ('Wg', 'Wq', 'Wk', 'Wv', 'Wo')}
    del _L0_ffn_all
    return {'x': x, 'L0_tok_W1': _L0_tok_in['W1'], 'L0_tok_b1': _L0_tok_in['b1'], 'L0_tok_W2': _L0_tok_in['W2'], 'L0_tok_b2': _L0_tok_in['b2'], 'L0_attn_ln1_g': _L0_attn_in['ln1_g'], 'L0_attn_ln1_b': _L0_attn_in['ln1_b'], 'L0_attn_ln2_g': _L0_attn_in['ln2_g'], 'L0_attn_ln2_b': _L0_attn_in['ln2_b'], 'L0_attn_att_mix_k': _L0_attn_in['att_mix_k'], 'L0_attn_att_mix_v': _L0_attn_in['att_mix_v'], 'L0_attn_att_mix_r': _L0_attn_in['att_mix_r'], 'L0_attn_time_decay': _L0_attn_in['time_decay'], 'L0_attn_time_first': _L0_attn_in['time_first'], 'L0_attn_Wk': _L0_attn_in['Wk'], 'L0_attn_Wv': _L0_attn_in['Wv'], 'L0_attn_Wr': _L0_attn_in['Wr'], 'L0_attn_Wo': _L0_attn_in['Wo'], 'L0_attn_ffn_mix_k': _L0_attn_in['ffn_mix_k'], 'L0_attn_ffn_mix_r': _L0_attn_in['ffn_mix_r'], 'L0_attn_Wk_ffn': _L0_attn_in['Wk_ffn'], 'L0_attn_Wr_ffn': _L0_attn_in['Wr_ffn'], 'L0_attn_Wv_ffn': _L0_attn_in['Wv_ffn'], 'L0_ffn_Wg': _L0_ffn_in['Wg'], 'L0_ffn_Wq': _L0_ffn_in['Wq'], 'L0_ffn_Wk': _L0_ffn_in['Wk'], 'L0_ffn_Wv': _L0_ffn_in['Wv'], 'L0_ffn_Wo': _L0_ffn_in['Wo']}

def reference(x, L0_tok_W1, L0_tok_b1, L0_tok_W2, L0_tok_b2, L0_attn_ln1_g, L0_attn_ln1_b, L0_attn_ln2_g, L0_attn_ln2_b, L0_attn_att_mix_k, L0_attn_att_mix_v, L0_attn_att_mix_r, L0_attn_time_decay, L0_attn_time_first, L0_attn_Wk, L0_attn_Wv, L0_attn_Wr, L0_attn_Wo, L0_attn_ffn_mix_k, L0_attn_ffn_mix_r, L0_attn_Wk_ffn, L0_attn_Wr_ffn, L0_attn_Wv_ffn, L0_ffn_Wg, L0_ffn_Wq, L0_ffn_Wk, L0_ffn_Wv, L0_ffn_Wo):
    import jax
    import jax.numpy as jnp

    def _L0_tok_ref(encoder_outputs, W1, b1, W2, b2):
        import jax, jax.numpy as jnp
        import numpy as np
        B, T, X, D, H = (16, 1, 1024, 256, 128)
        h = jnp.tanh(encoder_outputs @ W1 + b1)
        energy = h @ W2 + b2
        energy = jnp.transpose(energy, (0, 3, 2, 1))
        weights = jax.nn.softmax(jnp.squeeze(energy, -1), axis=1)
        out = (encoder_outputs * weights[..., None]).sum(axis=1)
        return out

    def _L0_attn_ref(x, ln1_g, ln1_b, ln2_g, ln2_b, att_mix_k, att_mix_v, att_mix_r, time_decay, time_first, Wk, Wv, Wr, Wo, ffn_mix_k, ffn_mix_r, Wk_ffn, Wr_ffn, Wv_ffn):
        import jax, jax.numpy as jnp
        import numpy as np
        import math
        B, T, C, FFN = (8, 512, 256, 1024)
        LAYER_ID, N_LAYER = (1, 12)

        def layer_norm(x, g, b, eps=1e-05):
            m = jnp.mean(x, axis=-1, keepdims=True)
            v = jnp.mean(jnp.square(x - m), axis=-1, keepdims=True)
            return (x - m) * jax.lax.rsqrt(v + eps) * g + b

        def token_shift(x):
            return jnp.concatenate([jnp.zeros_like(x[:, :1]), x[:, :-1]], axis=1)

        def wkv(w, u, k, v):
            w = -jnp.exp(w)
            kT = jnp.swapaxes(k, 0, 1)
            vT = jnp.swapaxes(v, 0, 1)

            def step(carry, kv_t):
                aa, bb, pp = carry
                kt, vt = kv_t
                ww = u + kt
                p = jnp.maximum(pp, ww)
                e1 = jnp.exp(pp - p)
                e2 = jnp.exp(ww - p)
                y = (e1 * aa + e2 * vt) / (e1 * bb + e2)
                ww2 = pp + w
                p2 = jnp.maximum(ww2, kt)
                e1b = jnp.exp(ww2 - p2)
                e2b = jnp.exp(kt - p2)
                return ((e1b * aa + e2b * vt, e1b * bb + e2b, p2), y)
            z = jnp.zeros((k.shape[0], k.shape[2]), k.dtype)
            init = (z, z, jnp.full_like(z, -1e+38))
            _, yT = jax.lax.scan(step, init, (kT, vT))
            return jnp.swapaxes(yT, 0, 1)
        xn = layer_norm(x, ln1_g, ln1_b)
        xx = token_shift(xn)
        xk = xn * att_mix_k + xx * (1.0 - att_mix_k)
        xv = xn * att_mix_v + xx * (1.0 - att_mix_v)
        xr = xn * att_mix_r + xx * (1.0 - att_mix_r)
        k = jnp.einsum('btc,dc->btd', xk, Wk)
        v = jnp.einsum('btc,dc->btd', xv, Wv)
        sr = jax.nn.sigmoid(jnp.einsum('btc,dc->btd', xr, Wr))
        rwkv = sr * wkv(time_decay, time_first, k, v)
        x = x + jnp.einsum('btd,cd->btc', rwkv, Wo)
        xn2 = layer_norm(x, ln2_g, ln2_b)
        xx2 = token_shift(xn2)
        xk2 = xn2 * ffn_mix_k + xx2 * (1.0 - ffn_mix_k)
        xr2 = xn2 * ffn_mix_r + xx2 * (1.0 - ffn_mix_r)
        kf = jnp.square(jax.nn.relu(jnp.einsum('btc,fc->btf', xk2, Wk_ffn)))
        kv = jnp.einsum('btf,cf->btc', kf, Wv_ffn)
        x = x + jax.nn.sigmoid(jnp.einsum('btc,dc->btd', xr2, Wr_ffn)) * kv
        return x

    def _L0_ffn_ref(token_inputs, Wg, Wq, Wk, Wv, Wo):
        import jax, jax.numpy as jnp
        import numpy as np
        CAPACITY_FACTOR = 0.5
        NUM_HEADS = 16
        B, N, D = token_inputs.shape
        C = int(N * CAPACITY_FACTOR)
        H = NUM_HEADS
        dh = D // H
        gate = jax.nn.sigmoid((token_inputs @ Wg)[..., 0])
        _, idx = jax.lax.top_k(gate, C)
        attn_in = jnp.take_along_axis(token_inputs, idx[..., None], axis=1)
        q = (attn_in @ Wq).reshape(B, C, H, dh)
        k = (attn_in @ Wk).reshape(B, C, H, dh)
        v = (attn_in @ Wv).reshape(B, C, H, dh)
        scores = jnp.einsum('bqhd,bkhd->bhqk', q, k) / jnp.sqrt(jnp.float32(dh))
        attn = jax.nn.softmax(scores, axis=-1)
        o = jnp.einsum('bhqk,bkhd->bqhd', attn, v).reshape(B, C, D) @ Wo
        gate_sel = jnp.take_along_axis(gate, idx, axis=1)
        out = jnp.zeros_like(token_inputs)
        out = out.at[jnp.arange(B)[:, None], idx].set(o * gate_sel[..., None])
        return out
    h = _L0_tok_ref(x, L0_tok_W1, L0_tok_b1, L0_tok_W2, L0_tok_b2)
    h = h + _L0_attn_ref(_layernorm(h, axis=-1), L0_attn_ln1_g, L0_attn_ln1_b, L0_attn_ln2_g, L0_attn_ln2_b, L0_attn_att_mix_k, L0_attn_att_mix_v, L0_attn_att_mix_r, L0_attn_time_decay, L0_attn_time_first, L0_attn_Wk, L0_attn_Wv, L0_attn_Wr, L0_attn_Wo, L0_attn_ffn_mix_k, L0_attn_ffn_mix_r, L0_attn_Wk_ffn, L0_attn_Wr_ffn, L0_attn_Wv_ffn)
    h = h + _L0_ffn_ref(_layernorm(h, axis=-1), L0_ffn_Wg, L0_ffn_Wq, L0_ffn_Wk, L0_ffn_Wv, L0_ffn_Wo)
    return h

_drawn_inputs = setup_inputs


def setup_inputs(seed=0):
    import zlib

    import numpy as np

    out = dict(_drawn_inputs(seed))
    spreads = {'L0_tok_b1': (0.0, 0.1),
     'L0_attn_ln1_g': (1.0, 0.6),
     'L0_attn_ln1_b': (0.0, 0.8),
     'L0_attn_ln2_g': (1.0, 0.6),
     'L0_attn_ln2_b': (0.0, 0.8)}
    factors = {'L0_attn_att_mix_k': 8.0,
     'L0_attn_att_mix_v': 8.0,
     'L0_attn_att_mix_r': 8.0,
     'L0_attn_time_decay': 5.897,
     'L0_attn_time_first': 8.0,
     'L0_attn_Wk': 8.0,
     'L0_attn_Wv': 4.121,
     'L0_attn_Wr': 8.0,
     'L0_attn_Wo': 4.122,
     'L0_attn_ffn_mix_k': 6.046,
     'L0_attn_ffn_mix_r': 8.0,
     'L0_attn_Wk_ffn': 4.053,
     'L0_attn_Wr_ffn': 8.0,
     'L0_attn_Wv_ffn': 3.639,
     'L0_ffn_Wq': 22.28,
     'L0_ffn_Wk': 22.184,
     'L0_ffn_Wg': 8.0,
     'L0_ffn_Wv': 8.0,
     'L0_ffn_Wo': 8.0}
    for name, (base, spread) in spreads.items():
        noise = np.random.default_rng([zlib.crc32(name.encode()), seed]).standard_normal(out[name].shape)
        drawn = base * np.exp(spread * noise) if base else spread * noise
        out[name] = jnp.asarray(drawn.astype(out[name].dtype))
    for name, factor in factors.items():
        out[name] = (out[name] * factor).astype(out[name].dtype)
    return out
```

```python
from contextlib import ExitStack

import numpy as np

import concourse.bass as bass
from concourse import mybir

F32 = mybir.dt.float32
F32R = mybir.dt.float32r
U32 = mybir.dt.uint32
ALU = mybir.AluOpType
ACT = mybir.ActivationFunctionType
AX = mybir.AxisListType

P = 128
B, T, C = 4, 1024, 256
NT = T // P
CH = C // P
TQ = 512
NQ = T // TQ
FFN = 1024
NF = FFN // P
H, DH = 16, 16
CAP = T // 2
KT = CAP // P
NG = 4
EPS = 1e-5
NEG = -1e38

VECTORS = ["ln1_g", "ln1_b", "ln2_g", "ln2_b", "mix_k", "mix_v", "mix_r",
           "decay", "first", "ffn_mix_k", "ffn_mix_r"]


class Lap:

    def __init__(self, plus, register=None):
        self.plus, self.register = plus, register

    def times(self, per, k=0):
        fixed = self.plus * per + k
        return fixed if self.register is None else self.register * per + fixed


def every_batch(recurrence, mlp, attention, eng):
    recurrence(Lap(0))
    mlp(Lap(0))
    with eng.Fori(0, B - 1) as i:
        recurrence(Lap(1, i))
        attention(Lap(0, i))
        mlp(Lap(1, i))
    attention(Lap(B - 1))


def vit_tower(nc, x, vectors, tok_w1, tok_b1, tok_w2, tok_b2, w_k, w_v, w_r, w_o,
              w_kf, w_rf, w_vf, gate_w, w_q2, w_k2, w_v2, w_o2, identity, lower, out):
    nc.disable_value_cache = True
    ctx = ExitStack()
    with ctx:
        def sb(name, shape, dt=F32):
            return ctx.enter_context(nc.sbuf_tensor(name, shape, dt))

        per_batch = {}

        def sem(name, per):
            s = ctx.enter_context(nc.semaphore(name))
            per_batch[name] = per
            return (s, per)

        def upto(b, signal, k):
            return b.times(signal[1], k)

        W1 = sb("W1", [P, CH, P])
        W2 = sb("W2", [P, 1])
        B1 = sb("B1", [P, 1])
        B2 = sb("B2", [P, 1])
        WK = sb("WK", [P, CH, C])
        WV = sb("WV", [P, CH, C])
        WR = sb("WR", [P, CH, C])
        WO = sb("WO", [P, CH, C])
        WKF = sb("WKF", [P, CH, FFN])
        WRF = sb("WRF", [P, CH, C])
        WVF = sb("WVF", [P, NF, C])
        WG = sb("WG", [P, C])
        WQ2 = sb("WQ2", [P, CH, C])
        WK2 = sb("WK2", [P, CH, C])
        WV2 = sb("WV2", [P, CH, C])
        WO2 = sb("WO2", [P, NG, C])
        VEC = sb("VEC", [P, len(VECTORS), CH])
        IDN = sb("IDN", [P, P])
        LOW = sb("LOW", [P, P])

        def vec(name, c):
            i = VECTORS.index(name)
            return VEC[:, i, c:c + 1]

        XIN = sb("XIN", [P, NT, C])
        HX = sb("HX", [P, NT, C])
        XA = sb("XA", [P, NT, C])
        XN = sb("XN", [P, CH, T + 1])
        MA = sb("MA", [P, CH, T])
        MB = sb("MB", [P, CH, T])
        KB = sb("KB", [P, CH, T])
        VR = sb("VR", [P, 2, CH, T])
        PP = sb("PP", [P, T + 1])
        EB = sb("EB", [P, CH, T])
        V2 = sb("V2", [P, T])
        EE = sb("EE", [P, T])
        DEC = sb("DEC", [P, CH])
        DECN = sb("DECN", [P, CH])
        STATS = sb("STATS", [P, NT, 6])
        MV = sb("MV", [P, NT, 2])
        MV2 = sb("MV2", [P, NT, 2])
        MV3 = sb("MV3", [P, NT, 2])
        VE = sb("VE", [P, 2 * NT])
        RS = sb("RS", [P, 2 * NT])
        VE2 = sb("VE2", [P, NT])
        RS2 = sb("RS2", [P, NT])
        VE3 = sb("VE3", [P, NT])
        RS3 = sb("RS3", [P, NT])
        HALF = sb("HALF", [P, 2 * NT])
        HOLD = sb("HOLD", [P, 3])
        SCR = sb("SCR", [P, NT])
        EN = sb("EN", [P, NT, 1])
        ENM = sb("ENM", [P, NT])
        END = sb("END", [P, NT])
        ENE = sb("ENE", [P, NT, 1])
        ENS = sb("ENS", [P, NT])
        ENR = sb("ENR", [P, NT])
        PW = sb("PW", [P, NT])
        ZC = sb("ZC", [P, NT])
        ZE = sb("ZE", [P, NT])
        ZP = sb("ZP", [P, NT])
        GC = sb("GC", [P, NT])
        CNT = sb("CNT", [P, NT, 3])
        RANKF = sb("RANKF", [P, NT])
        H2 = sb("H2", [P, NT, C])
        G2 = sb("G2", [P, NT])
        RANK = sb("RANK", [P, NT], U32)
        SEL = sb("SEL", [P, KT, C])
        AT = sb("AT", [P, CH, CAP])
        QS = sb("QS", [P, H // 2, CAP], F32R)
        KS = sb("KS", [P, H // 2, CAP], F32R)
        VV = sb("VV", [P, KT, H, 32])
        PR = sb("PR", [P, 2, 2, CAP])
        OT = sb("OT", [P, NG, CAP])
        NM = sb("NM", [P, KT, H])
        RSUM = sb("RSUM", [P, NG, KT, 4])

        HID = VR[:, :, :, :].rearrange("p a c t -> p (a c t)").rearrange("p (f t) -> p f t", t=TQ)
        KBT = KB[:, :, :].rearrange("p a t -> p (a t)").rearrange("p (t c) -> p t c", c=C)
        VT = VR[:, 0, :, :].rearrange("p a t -> p (a t)").rearrange("p (t c) -> p t c", c=C)
        E1, E2 = MB[:, 0, :], MB[:, 1, :]
        MHL = AT[0:H, :, :].bitcast(F32R)
        RWIDE = [z[:, :, :].rearrange("p a n -> p (a n)").rearrange("p (g t w) -> p g t w", g=2, t=KT)
                 for z in (AT, SEL)]
        GA = PR[:, :, :, :].rearrange("p a i n -> p (a i n)").rearrange("p (t c) -> p t c", c=C)
        QHL = PR[:, :, :, :].bitcast(F32R)

        kept_d = nc.dram_tensor("kept_d", [CAP, C], F32, kind="Internal").ap()
        qk_d = nc.dram_tensor("qk_d", [4, C, CAP], F32, kind="Internal").ap()
        max_d = nc.dram_tensor("max_d", [2, H, CAP], F32, kind="Internal").ap()
        att_d = nc.dram_tensor("att_d", [T, C], F32, kind="Internal").ap()

        PA = ctx.enter_context(nc.psum_tensor("PA", [P, 3, TQ], F32))
        PC = ctx.enter_context(nc.psum_tensor("PC", [P, 2, 2, TQ], F32))
        PO = ctx.enter_context(nc.psum_tensor("PO", [P, TQ], F32))

        s_w = sem("weights_in", 0)
        s_const = sem("constants_set", 0)
        s_dec = sem("decay_ready", 0)
        s_decn = sem("w_ready", 0)
        s_x = sem("x_in", 16)
        s_pa = sem("bank_filled", 57)
        s_xT = sem("xT_out", 4)
        s_hT = sem("tanh_out", 2)
        s_ee = sem("energy_exp", 1)
        s_xnT = sem("xnT_out", 4)
        s_k = sem("k_out", 4)
        s_v = sem("v_out", 4)
        s_r = sem("r_out", 4)
        s_ex = sem("wkv_exp", 8)
        s_er = sem("r_exp", 4)
        s_y = sem("y_exp", 4)
        s_xn2T = sem("xn2T_out", 4)
        s_r2 = sem("r2_out", 4)
        s_r2e = sem("r2_exp", 8)
        s_relu = sem("relu_out", 16)
        s_hid = sem("hidden_out", 16)
        s_ze = sem("gate_exp", 1)
        s_grow = sem("gate_rows", 2)
        s_en = sem("energy", 3)
        s_pw = sem("pool_weights", 3)
        s_h = sem("pooled", 8)
        s_st = sem("norm_stats", 16)
        s_ve = sem("norm_var", 4)
        s_sc = sem("norm_scale", 1)
        s_xa = sem("xa", 8)
        s_xn = sem("xn", 8)
        s_dx = sem("token_diff", 2)
        s_mk = sem("mixed_k", 2)
        s_mv = sem("mixed_v", 2)
        s_mr = sem("mixed_r", 2)
        s_pp = sem("exponent", 2)
        s_d = sem("exp_args", 10)
        s_rm = sem("min_r", 2)
        s_ev = sem("e2b_v", 2)
        s_ab = sem("scans", 4)
        s_nd = sem("num_den", 14)
        s_rw = sem("rwkv", 2)
        s_x2 = sem("x2", 4)
        s_st2 = sem("norm2_stats", 16)
        s_ve2 = sem("norm2_var", 1)
        s_xn2 = sem("xn2", 8)
        s_dx2 = sem("token_diff2", 2)
        s_mk2 = sem("mixed_k2", 2)
        s_mr2 = sem("mixed_r2", 2)
        s_g2 = sem("r2_arg", 2)
        s_sk = sem("gated_kv", 4)
        s_x3 = sem("x3", 4)
        s_h2 = sem("h2", 4)
        s_st3 = sem("norm3_stats", 16)
        s_ve3 = sem("norm3_var", 1)
        s_ti = sem("router_tokens", 8)
        s_z = sem("gate_logits", 8)
        s_g = sem("gates", 3)
        s_cnt = sem("counts", 24)
        s_rank = sem("ranks", 2)
        s_rs = sem("rstd", 1)
        s_rs2 = sem("rstd2", 1)
        s_rs3 = sem("rstd3", 1)
        s_scat = sem("kept_stored", 16 * NT)
        s_gath = sem("gathered", 16 * NT)
        s_sel = sem("kept_in", 16)
        s_pc = sem("pair_filled", 74)
        s_pv = sem("values_done", 16)
        s_at = sem("aT_out", 1)
        s_qh = sem("qk_high", 2)
        s_ql = sem("qk_low", 2)
        s_qw = sem("qk_stored", 64)
        s_qi = sem("stacks_in", 16 * 12)
        s_vv = sem("v2_out", 1)
        s_nm = sem("maxima", 32)
        s_mh = sem("max_high", 1)
        s_ml = sem("max_low", 1)
        s_mw = sem("max_stored", 32)
        s_mi = sem("max_in", 64)
        s_p = sem("probs", 32)
        s_oT = sem("heads_out", 4)
        s_rsum = sem("sums_inverse", 2)
        s_rw2 = sem("inverse_spread", 2)
        s_on = sem("heads_norm", 2)
        s_o = sem("attention_out", 1)
        s_ow = sem("attention_stored", 16)
        s_fin = sem("result", 8)
        s_out = sem("out_stored", 32)

        emptied = ([(s_xT, i + 1) for i in range(4)] + [(s_hT, i + 1) for i in range(2)] + [(s_en, 1)]
                   + [(s_xnT, i + 1) for i in range(4)] + [(s_k, i + 1) for i in range(4)]
                   + [(s_v, i + 1) for i in range(4)] + [(s_r, i + 1) for i in range(4)]
                   + [(s_x2, i + 1) for i in range(4)] + [(s_xn2T, i + 1) for i in range(4)])
        for q in range(NQ):
            emptied += [(s_r2, 2 * q + i + 1) for i in range(2)]
            emptied += [(s_relu, NF * q + i + 1) for i in range(NF)]
            emptied += [(s_sk, 2 * q + i + 1) for i in range(2)]
        emptied += [(s_grow, i + 1) for i in range(2)]
        assert len(emptied) == s_pa[1] and len(emptied) % 3 == 0
        emptied2 = [(s_at, 1), (s_ql, 1), (s_ql, 2), (s_vv, 1)] + [(s_nm, i + 1) for i in range(32)]
        emptied2 += [(s_ml, 1)] + [(s_p, i + 1) for i in range(32)]
        emptied2 += [(s_rsum, 1), (s_rsum, 2), (s_on, 1), (s_on, 2), (s_o, 1)]
        assert len(emptied2) == s_pc[1] and len(emptied2) % 2 == 0

        MLP_FROM = 23
        block = ctx.enter_context(nc.Block())
        act, dve, pe, pool, sp = nc.scalar, nc.vector, nc.tensor, nc.gpsimd, nc.sync

        LOADS = [(VEC, vectors), (W1, tok_w1), (B1, tok_b1), (W2, tok_w2), (B2, tok_b2), (IDN, identity),
                 (WK, w_k), (WV, w_v), (WR, w_r), (WO, w_o), (WKF, w_kf), (WRF, w_rf), (WVF, w_vf),
                 (WG, gate_w), (LOW, lower), (WQ2, w_q2), (WK2, w_k2), (WV2, w_v2), (WO2, w_o2)]
        ALL_LOADED = 16 * len(LOADS)

        @block.sync
        def _(eng):
            def load_x(b):
                row = b.times(T)
                src = x[bass.ds(row, T), :] if b.register is not None else x[row:row + T, :]
                sp.dma_start(XIN[:, :, :], src.rearrange("(t p) c -> p t c", p=P)).then_inc(s_x[0], 16)

            def recurrence(b):
                eng.wait_ge(s_h[0], upto(b, s_h, 0))
                load_x(b)

            def mlp(b):
                pass

            def attention(b):
                eng.wait_ge(s_scat[0], upto(b, s_scat, 16 * NT))
                sp.dma_start(SEL[:, :, :], kept_d.rearrange("(t p) c -> p t c", p=P)).then_inc(s_sel[0], 16)
                for i in range(2):
                    for part, done in ((0, s_qh), (1, s_ql)):
                        eng.wait_ge(done[0], upto(b, done, i + 1))
                        sp.dma_start(qk_d[2 * i + part].rearrange("(c p) n -> p c n", p=P),
                                     QHL[:, part, :, :].bitcast(F32)).then_inc(s_qw[0], 16)
                for i, (stack, parts) in enumerate(((QS, (0, 0, 1)), (KS, (2, 3, 2)))):
                    eng.wait_ge(s_qw[0], upto(b, s_qw, 32 * (i + 1)))
                    for odd in range(2):
                        for n, part in enumerate(parts):
                            at = 64 * odd + DH * n
                            sp.dma_start(stack[at:at + DH, :, :].bitcast(F32),
                                         qk_d[part].rearrange("(j r d) n -> r d j n", r=2, d=DH)[odd])\
                              .then_inc(s_qi[0], 16)
                for part, done in ((0, s_mh), (1, s_ml)):
                    eng.wait_ge(done[0], upto(b, done, 1))
                    sp.dma_start(max_d[part], MHL[:, part, :].bitcast(F32)).then_inc(s_mw[0], 16)
                eng.wait_ge(s_mw[0], upto(b, s_mw, 32))
                for odd in range(2):
                    for part in range(2):
                        at = 64 * odd + 3 * DH + part
                        sp.dma_start(QS[at:at + 1, :, :].bitcast(F32),
                                     max_d[part:part + 1].rearrange("a (j r) n -> r a j n", r=2)[odd])\
                          .then_inc(s_mi[0], 16)
                eng.wait_ge(s_o[0], upto(b, s_o, 1))
                sp.dma_start(att_d[0:CAP].rearrange("(t p) c -> p t c", p=P), SEL[:, :, :]).then_inc(s_ow[0], 16)
                for half in range(2):
                    eng.wait_ge(s_fin[0], upto(b, s_fin, 4 * (half + 1)))
                    row = b.times(T, 512 * half)
                    dst = out[bass.ds(row, 512), :] if b.register is not None else out[row:row + 512, :]
                    sp.dma_start(dst.rearrange("(t p) c -> p t c", p=P),
                                 H2[:, 4 * half:4 * half + 4, :]).then_inc(s_out[0], 16)

            for buf, src in LOADS:
                sp.dma_start(buf[:], src).then_inc(s_w[0], 16)
            eng.wait_ge(s_const[0], 7)
            sp.dma_start(att_d[CAP:T].rearrange("(t p) c -> p t c", p=P), GA[:, 0:KT, :]).then_inc(s_w[0], 16)
            every_batch(recurrence, mlp, attention, eng)
            eng.wait_ge(s_out[0], 32 * B)
            eng.wait_ge(s_w[0], ALL_LOADED + 16)

        @block.gpsimd
        def _(eng):
            def hold(cell):
                pool.tensor_tensor(HOLD[:, cell:cell + 1], HALF[:, 0:1], HALF[:, 0:1], ALU.mult)

            def power(dst, src, n, need, done, b):
                eng.wait_ge(need[0], upto(b, need, need[1]))
                pool.tensor_tensor(dst[:, 0:n], src[:, 0:n], HALF[:, 0:n], ALU.pow).then_inc(done[0], 1)

            def recurrence(b):
                power(RS, VE, 2 * NT, s_ve, s_rs, b)

            def mlp(b):
                power(RS2, VE2, NT, s_ve2, s_rs2, b)
                power(RS3, VE3, NT, s_ve3, s_rs3, b)
                eng.wait_ge(s_rank[0], upto(b, s_rank, 2))
                eng.wait_ge(s_ti[0], upto(b, s_ti, NT))
                eng.wait_ge(s_sel[0], upto(b, s_sel, 0))
                hold(1)
                for t in range(NT):
                    pool.indirect_dma_start(
                        out=kept_d, out_offset=bass.IndirectOffsetOnAxis(ap=RANK[:, t:t + 1], axis=0),
                        in_=KB[:, :, :].rearrange("p a t -> p (a t)")[:, C * t:C * t + C], in_offset=None,
                        bounds_check=CAP - 1, oob_is_err=False).then_inc(s_scat[0], 16)

            def attention(b):
                eng.wait_ge(s_ow[0], upto(b, s_ow, 16))
                hold(2)
                for t in range(NT):
                    pool.indirect_dma_start(
                        out=GA[:, t, :], out_offset=None, in_=att_d,
                        in_offset=bass.IndirectOffsetOnAxis(ap=RANK[:, t:t + 1], axis=0))\
                        .then_inc(s_gath[0], 16)

            pool.memset(HALF[:], -0.5).then_inc(s_const[0], 1)
            pool.memset(XN[:, :, 0:1], 0.0).then_inc(s_const[0], 1)
            pool.memset(PP[:, 0:1], NEG).then_inc(s_const[0], 1)
            pool.memset(GA, 0.0).then_inc(s_const[0], 1)
            pool.memset(VV[:], 1.0).then_inc(s_const[0], 1)
            pool.memset(QS[:].bitcast(F32), 0.0).then_inc(s_const[0], 1)
            pool.memset(KS[:].bitcast(F32), 1.0).then_inc(s_const[0], 1)
            eng.wait_ge(s_w[0], ALL_LOADED + 16)
            every_batch(recurrence, mlp, attention, eng)

        @block.tensor
        def _(eng):
            def ring(b, first):
                use = [first]

                def bank():
                    u = use[0]
                    use[0] += 1
                    who, k = emptied[u - 3]
                    if u >= 3:
                        eng.wait_ge(who[0], upto(b, who, k))
                    elif b.plus:
                        eng.wait_ge(who[0], upto(b, who, k - who[1]))
                    return PA[:, u % 3, :]

                return use, bank

            def filled(last_instruction):
                last_instruction.then_inc(s_pa[0], 1)

            def to_channels(b, bank, src, need):
                for c in range(CH):
                    for q in range(NQ):
                        dst = bank()
                        for i in range(4):
                            t = 4 * q + i
                            if need is not None:
                                eng.wait_ge(need[0], upto(b, need, t + 1))
                            m = pe.transpose(dst[:, P * i:P * i + P], src(t, c), IDN[:, :])
                        filled(m)

            def recurrence(b):
                use, bank = ring(b, 0)
                eng.wait_ge(s_x[0], upto(b, s_x, 16))
                to_channels(b, bank, lambda t, c: XIN[:, t, P * c:P * c + P], None)
                XT = VR[:, 1, :, :]
                eng.wait_ge(s_xT[0], upto(b, s_xT, 4))
                for q in range(NQ):
                    dst = bank()
                    for c in range(CH):
                        m = pe.matmul(dst, W1[:, c, :], XT[:, c, TQ * q:TQ * q + TQ], start=c == 0, stop=c == CH - 1)
                    filled(m)
                dst = bank()
                eng.wait_ge(s_hT[0], upto(b, s_hT, 2))
                for t in range(NT):
                    m = pe.matmul(dst[:, t:t + 1], V2[:, P * t:P * t + P], W2[:, :], start=True, stop=True)
                filled(m)

                to_channels(b, bank, lambda t, c: KBT[:, t, P * c:P * c + P], s_xn)

                for w, src, need in ((WK, MA, s_mk), (WV, MB, s_mv), (WR, MA, s_mr)):
                    for d in range(CH):
                        for q in range(NQ):
                            dst = bank()
                            for c in range(CH):
                                eng.wait_ge(need[0], upto(b, need, c + 1))
                                m = pe.matmul(dst, w[:, c, P * d:P * d + P], src[:, c, TQ * q:TQ * q + TQ],
                                              start=c == 0, stop=c == CH - 1)
                            filled(m)

                assert use[0] == MLP_FROM

            def mlp(b):
                use, bank = ring(b, MLP_FROM)
                for i in range(4):
                    dst = bank()
                    for j in range(2):
                        t = 2 * i + j
                        for d in range(CH):
                            eng.wait_ge(s_rw[0], upto(b, s_rw, d + 1))
                            m = pe.matmul(dst[:, C * j:C * j + C], KB[:, d, P * t:P * t + P], WO[:, d, :],
                                          start=d == 0, stop=d == CH - 1)
                    filled(m)

                to_channels(b, bank, lambda t, c: VT[:, t, P * c:P * c + P], s_xn2)

                for q in range(NQ):
                    for i in range(2):
                        dst = bank()
                        for j in range(2):
                            t = 4 * q + 2 * i + j
                            for c in range(CH):
                                eng.wait_ge(s_mr2[0], upto(b, s_mr2, c + 1))
                                m = pe.matmul(dst[:, C * j:C * j + C], MB[:, c, P * t:P * t + P], WRF[:, c, :],
                                              start=c == 0, stop=c == CH - 1)
                        filled(m)
                    for f in range(NF):
                        dst = bank()
                        for c in range(CH):
                            eng.wait_ge(s_mk2[0], upto(b, s_mk2, c + 1))
                            m = pe.matmul(dst, WKF[:, c, P * f:P * f + P], MA[:, c, TQ * q:TQ * q + TQ],
                                          start=c == 0, stop=c == CH - 1)
                        filled(m)
                    for i in range(2):
                        dst = bank()
                        for j in range(2):
                            for f in range(NF):
                                eng.wait_ge(s_hid[0], upto(b, s_hid, NF * q + f + 1))
                                t = 2 * i + j
                                m = pe.matmul(dst[:, C * j:C * j + C], HID[:, f, P * t:P * t + P], WVF[:, f, :],
                                              start=f == 0, stop=f == NF - 1)
                        filled(m)

                eng.wait_ge(s_g[0], upto(b, s_g, 2))
                for q in range(2):
                    dst = bank()
                    for i in range(4):
                        t = 4 * q + i
                        m = pe.transpose(dst[:, P * i:P * i + P], GC[:, t:t + 1].broadcast_to([P, P]), IDN[:, :])
                    filled(m)
                assert use[0] == s_pa[1]

            def attention(b):
                use = [0]

                def pair():
                    u = use[0]
                    use[0] += 1
                    if u >= 2:
                        who, k = emptied2[u - 2]
                        eng.wait_ge(who[0], upto(b, who, k))
                    else:
                        who, k = emptied2[u - 2]
                        assert k == who[1]
                        eng.wait_ge(who[0], upto(b, who, 0))
                    return PC[:, u % 2, :, :]

                def filled(last_instruction):
                    last_instruction.then_inc(s_pc[0], 1)

                dst = pair()
                eng.wait_ge(s_sel[0], upto(b, s_sel, 16))
                for c in range(CH):
                    for t in range(KT):
                        m = pe.transpose(dst[:, c, P * t:P * t + P], SEL[:, t, P * c:P * c + P], IDN[:, :])
                filled(m)
                eng.wait_ge(s_at[0], upto(b, s_at, 1))
                for w in (WQ2, WK2):
                    dst = pair()
                    for d in range(CH):
                        for c in range(CH):
                            m = pe.matmul(dst[:, d, :], w[:, c, P * d:P * d + P], AT[:, c, :],
                                          start=c == 0, stop=c == CH - 1)
                    filled(m)
                dst = pair()
                for t in range(KT):
                    for c in range(CH):
                        m = pe.matmul(dst[:, t // 2, C * (t % 2):C * (t % 2) + C], AT[:, c, P * t:P * t + P],
                                      WV2[:, c, :], start=c == 0, stop=c == CH - 1)
                filled(m)
                eng.wait_ge(s_qi[0], upto(b, s_qi, 16 * 12))
                for h in range(H):
                    at, j = 64 * (h % 2), h // 2
                    for n in range(2):
                        dst = pair()
                        for i in range(2):
                            t = 2 * n + i
                            m = pe.matmul(dst[:, i, :], QS[at:at + 3 * DH, j, P * t:P * t + P],
                                          KS[at:at + 3 * DH, j, :], start=True, stop=True)
                        filled(m)
                dst = pair()
                eng.wait_ge(s_nm[0], upto(b, s_nm, 32))
                for t in range(KT):
                    m = pe.transpose(dst[0:H, 0, P * t:P * t + P], NM[:, t, :], IDN[:, :])
                filled(m)
                eng.wait_ge(s_mi[0], upto(b, s_mi, 64))
                eng.wait_ge(s_vv[0], upto(b, s_vv, 1))

                def values(step):
                    g, t = divmod(step, KT)
                    eng.wait_ge(s_p[0], upto(b, s_p, 2 * step + 2))
                    if t == 0:
                        eng.wait_ge(s_oT[0], upto(b, s_oT, g))
                    for i in range(4):
                        m = pe.matmul(PO[32 * i:32 * i + 32, :], VV[:, t, 4 * g + i, :], PR[:, i // 2, i % 2, :],
                                      start=t == 0, stop=t == KT - 1, tile_position=(0, 32 * i))
                    return m

                for step in range(NG * KT + 1):
                    if step < NG * KT:
                        g, t = divmod(step, KT)
                        for n in range(2):
                            dst = pair()
                            j = 2 * g + n
                            for i in range(2):
                                m = pe.matmul(dst[:, i, :], KS[64 * i:64 * i + 64, j, P * t:P * t + P],
                                              QS[64 * i:64 * i + 64, j, :], start=True, stop=True)
                            filled(m)
                    if step > 0:
                        values(step - 1).then_inc(s_pv[0], 1)
                for n in range(2):
                    dst = pair()
                    for i in range(2):
                        g = 2 * n + i
                        eng.wait_ge(s_oT[0], upto(b, s_oT, g + 1))
                        for t in range(KT):
                            m = pe.transpose(dst[:, i, P * t:P * t + P], OT[:, g, P * t:P * t + P], IDN[:, :])
                    filled(m)
                for n in range(2):
                    dst = pair()
                    eng.wait_ge(s_rw2[0], upto(b, s_rw2, n + 1))
                    for i in range(2):
                        g = 2 * n + i
                        for t in range(KT):
                            m = pe.transpose(dst[:, i, P * t:P * t + P],
                                             RWIDE[n][:, i, t, :], IDN[:, :])
                    filled(m)
                dst = pair()
                eng.wait_ge(s_on[0], upto(b, s_on, 2))
                for t in range(KT):
                    for g in range(NG):
                        m = pe.matmul(dst[:, t // 2, C * (t % 2):C * (t % 2) + C], OT[:, g, P * t:P * t + P],
                                      WO2[:, g, :], start=g == 0, stop=g == NG - 1)
                filled(m)
                assert use[0] == s_pc[1]

            eng.wait_ge(s_w[0], ALL_LOADED + 16)
            eng.wait_ge(s_const[0], 7)
            every_batch(recurrence, mlp, attention, eng)

        @block.scalar
        def _(eng):
            def ring(b, first):
                use = [first]

                def bank():
                    u = use[0]
                    use[0] += 1
                    eng.wait_ge(s_pa[0], upto(b, s_pa, u + 1))
                    return PA[:, u % 3, :]

                return use, bank

            def recurrence(b):
                use, bank = ring(b, 0)
                act.preload_act_table_set("exp_and_others")
                XT = VR[:, 1, :, :]
                for c in range(CH):
                    for q in range(NQ):
                        src = bank()
                        act.activation(XT[:, c, TQ * q:TQ * q + TQ], src, ACT.Copy).then_inc(s_xT[0], 1)
                eng.wait_ge(s_cnt[0], upto(b, s_cnt, 0))
                for q in range(NQ):
                    src = bank()
                    act.activation(V2[:, TQ * q:TQ * q + TQ], src, ACT.Tanh, bias=B1[:, :]).then_inc(s_hT[0], 1)
                use[0] += 1
                act.preload_act_table_set("natural_log_exp_and_others")
                eng.wait_ge(s_en[0], upto(b, s_en, 3))
                act.activation(ENE[:, :, 0], END[:, :], ACT.Exp).then_inc(s_ee[0], 1)
                for c in range(CH):
                    for q in range(NQ):
                        src = bank()
                        act.activation(XN[:, c, 1 + TQ * q:1 + TQ * q + TQ], src, ACT.Identity,
                                       scale=vec("ln1_g", c), bias=vec("ln1_b", c)).then_inc(s_xnT[0], 1)
                for dst, done in ((KB, s_k), (VR[:, 0, :, :], s_v), (VR[:, 1, :, :], s_r)):
                    for d in range(CH):
                        for q in range(NQ):
                            src = bank()
                            act.activation(dst[:, d, TQ * q:TQ * q + TQ], src, ACT.Copy).then_inc(done[0], 1)
                for d in range(CH):
                    eng.wait_ge(s_r[0], upto(b, s_r, 2 * d + 2))
                    eng.wait_ge(s_nd[0], upto(b, s_nd, 7 * d))
                    act.activation(EE[:, :], VR[:, 1, d, :], ACT.Abs).then_inc(s_er[0], 1)
                    eng.wait_ge(s_er[0], upto(b, s_er, 2 * d + 1))
                    act.activation(EE[:, :], EE[:, :], ACT.Exp, scale=-1.0).then_inc(s_er[0], 1)
                    for i, (buf, sign, step) in enumerate(((EB[:, 0, :], 1.0, 1), (EB[:, 1, :], 1.0, 2),
                                                           (E1, -1.0, 4), (E2, 1.0, 5))):
                        eng.wait_ge(s_d[0], upto(b, s_d, 5 * d + step))
                        act.activation(buf, buf, ACT.Exp, scale=sign).then_inc(s_ex[0], 1)
                    eng.wait_ge(s_nd[0], upto(b, s_nd, 7 * d + 6))
                    act.activation(EB[:, 0, :], EB[:, 1, :], ACT.Ln).then_inc(s_y[0], 1)
                    eng.wait_ge(s_nd[0], upto(b, s_nd, 7 * d + 7))
                    act.activation(EB[:, 0, :], EB[:, 0, :], ACT.Exp).then_inc(s_y[0], 1)
                assert use[0] == MLP_FROM

            def mlp(b):
                use, bank = ring(b, MLP_FROM + 4)
                for c in range(CH):
                    for q in range(NQ):
                        src = bank()
                        act.activation(XN[:, c, 1 + TQ * q:1 + TQ * q + TQ], src, ACT.Identity,
                                       scale=vec("ln2_g", c), bias=vec("ln2_b", c)).then_inc(s_xn2T[0], 1)
                for q in range(NQ):
                    LG = EB[:, :, :].rearrange("p c t -> p (c t)")[:, 2 * TQ * q:2 * TQ * q + 2 * TQ]
                    eng.wait_ge(s_mk2[0], upto(b, s_mk2, 2))
                    for i in range(2):
                        src = bank()
                        act.activation(LG[:, TQ * i:TQ * i + TQ], src, ACT.Copy).then_inc(s_r2[0], 1)
                    eng.wait_ge(s_r2[0], upto(b, s_r2, 2 * q + 2))
                    eng.wait_ge(s_x3[0], upto(b, s_x3, 2 * q))
                    act.activation(EE[:, :], LG, ACT.Abs).then_inc(s_r2e[0], 1)
                    eng.wait_ge(s_r2e[0], upto(b, s_r2e, 4 * q + 1))
                    act.activation(EE[:, :], EE[:, :], ACT.Exp, scale=-1.0).then_inc(s_r2e[0], 1)
                    eng.wait_ge(s_r2e[0], upto(b, s_r2e, 4 * q + 2))
                    act.activation(EE[:, :], EE[:, :], ACT.Ln, bias=1.0).then_inc(s_r2e[0], 1)
                    for f in range(NF):
                        src = bank()
                        n = NF * q + f
                        tmp = V2[:, TQ * (f % 2):TQ * (f % 2) + TQ]
                        eng.wait_ge(s_hid[0], upto(b, s_hid, n))
                        act.activation(tmp, src, ACT.Relu).then_inc(s_relu[0], 1)
                        eng.wait_ge(s_relu[0], upto(b, s_relu, n + 1))
                        act.activation(HID[:, f, :], tmp, ACT.Square).then_inc(s_hid[0], 1)
                        if f == 1:
                            eng.wait_ge(s_g2[0], upto(b, s_g2, q + 1))
                            act.activation(EE[:, :], EE[:, :], ACT.Exp).then_inc(s_r2e[0], 1)
                    use[0] += 2
                eng.wait_ge(s_z[0], upto(b, s_z, NT))
                act.activation(ZE[:, :], ZC[:, :], ACT.Exp, scale=-1.0).then_inc(s_ze[0], 1)
                for q in range(2):
                    src = bank()
                    act.activation(EB[:, 0, TQ * q:TQ * q + TQ], src, ACT.Copy).then_inc(s_grow[0], 1)
                assert use[0] == s_pa[1]

            def attention(b):
                use = [0]

                def pair(skip=0):
                    use[0] += skip
                    u = use[0]
                    use[0] += 1
                    eng.wait_ge(s_pc[0], upto(b, s_pc, u + 1))
                    return PC[:, u % 2, :, :]

                src = pair()
                eng.wait_ge(s_mw[0], upto(b, s_mw, 0))
                act.activation(AT[:, :, :], src, ACT.Copy).then_inc(s_at[0], 1)
                for i in range(2):
                    src = pair()
                    eng.wait_ge(s_qw[0], upto(b, s_qw, 32 * i))
                    eng.wait_ge(s_fin[0], upto(b, s_fin, 0))
                    act.activation(QHL[:, 0, :, :], src, ACT.Copy).then_inc(s_qh[0], 1)
                src = pair()
                act.activation(VV[:, :, :, 0:DH],
                               src.rearrange("p a (t h d) -> p (a t) h d", t=2, d=DH), ACT.Copy).then_inc(s_vv[0], 1)
                src = pair(skip=32)
                act.activation(MHL[:, 0, :], src[0:H, 0, :], ACT.Copy).then_inc(s_mh[0], 1)
                for step in range(NG * KT):
                    g, t = divmod(step, KT)
                    for n in range(2):
                        src = pair()
                        eng.wait_ge(s_pv[0], upto(b, s_pv, step))
                        if step == 0:
                            eng.wait_ge(s_qw[0], upto(b, s_qw, 64))
                        act.activation(PR[:, n, :, :], src, ACT.Exp, scale=0.25).then_inc(s_p[0], 1)
                    if t == 0 and g > 0:
                        heads_out(b, g - 1)
                heads_out(b, NG - 1)
                src = pair(skip=4)
                act.activation(SEL[:, :, :], src.rearrange("p a (t c) -> p (a t) c", t=2), ACT.Copy)\
                   .then_inc(s_o[0], 1)
                assert use[0] == s_pc[1]

            def heads_out(b, g):
                eng.wait_ge(s_pv[0], upto(b, s_pv, KT * (g + 1)))
                act.activation(OT[:, g, :], PO[:, :], ACT.Copy).then_inc(s_oT[0], 1)

            eng.wait_ge(s_w[0], ALL_LOADED + 16)
            act.activation(DEC[:, :], VEC[:, VECTORS.index("decay"), :], ACT.Exp).then_inc(s_dec[0], 1)
            every_batch(recurrence, mlp, attention, eng)

        @block.vector
        def _(eng):
            def stats(b, src, need, per, st, mv):
                for t in range(NT):
                    eng.wait_ge(need[0], upto(b, need, t // per + 1))
                    dve.bn_stats(STATS[:, t, :], src[:, t, :]).then_inc(st[0], 1)
                eng.wait_ge(st[0], upto(b, st, NT))
                dve.memset(HOLD[:, 0:1], 0.0)
                for t in range(NT):
                    dve.bn_aggr(mv[:, t, :], STATS[:, t, :]).then_inc(st[0], 1)

            def ring(b, first):
                use = [first]

                def bank(skip=0):
                    use[0] += skip
                    u = use[0]
                    use[0] += 1
                    eng.wait_ge(s_pa[0], upto(b, s_pa, u + 1))
                    return PA[:, u % 3, :]

                return use, bank

            def mixed(b, done, dst, name, c):
                dve.scalar_tensor_tensor(dst[:, c, :], EB[:, c, :], vec(name, c), XN[:, c, 0:T],
                                         ALU.mult, ALU.add).then_inc(done[0], 1)

            def recurrence(b):
                use, bank = ring(b, 0)
                src = bank(6)
                dve.tensor_scalar(EN[:, :, 0], src[:, 0:NT], B2[:, :], None, ALU.add).then_inc(s_en[0], 1)
                eng.wait_ge(s_en[0], upto(b, s_en, 1))
                dve.tensor_reduce(ENM[:, :], EN[:, :, :], AX.X, ALU.max).then_inc(s_en[0], 1)
                eng.wait_ge(s_en[0], upto(b, s_en, 2))
                dve.tensor_tensor(END[:, :], EN[:, :, 0], ENM[:, :], ALU.subtract).then_inc(s_en[0], 1)
                eng.wait_ge(s_ee[0], upto(b, s_ee, 1))
                dve.tensor_reduce(ENS[:, :], ENE[:, :, :], AX.X, ALU.add).then_inc(s_pw[0], 1)
                eng.wait_ge(s_pw[0], upto(b, s_pw, 1))
                dve.reciprocal(ENR[:, :], ENS[:, :]).then_inc(s_pw[0], 1)
                eng.wait_ge(s_pw[0], upto(b, s_pw, 2))
                dve.tensor_tensor(PW[:, :], ENE[:, :, 0], ENR[:, :], ALU.mult).then_inc(s_pw[0], 1)
                eng.wait_ge(s_pw[0], upto(b, s_pw, 3))
                eng.wait_ge(s_x[0], upto(b, s_x, 16))
                for t in range(NT):
                    dve.tensor_scalar(HX[:, t, :], XIN[:, t, :], PW[:, t:t + 1], None, ALU.mult).then_inc(s_h[0], 1)
                stats(b, HX, s_h, 1, s_st, MV)
                eng.wait_ge(s_st[0], upto(b, s_st, 2 * NT))
                dve.tensor_scalar(VE[:, 0:NT], MV[:, :, 1], EPS, None, ALU.add).then_inc(s_ve[0], 1)
                eng.wait_ge(s_ve[0], upto(b, s_ve, 1))
                dve.reciprocal(SCR[:, :], VE[:, 0:NT]).then_inc(s_ve[0], 1)
                eng.wait_ge(s_ve[0], upto(b, s_ve, 2))
                dve.tensor_tensor(VE[:, NT:2 * NT], MV[:, :, 1], SCR[:, :], ALU.mult).then_inc(s_ve[0], 1)
                eng.wait_ge(s_ve[0], upto(b, s_ve, 3))
                dve.tensor_scalar(VE[:, NT:2 * NT], VE[:, NT:2 * NT], EPS, None, ALU.add).then_inc(s_ve[0], 1)
                eng.wait_ge(s_rs[0], upto(b, s_rs, 1))
                dve.tensor_tensor(SCR[:, :], RS[:, 0:NT], RS[:, NT:2 * NT], ALU.mult).then_inc(s_sc[0], 1)
                eng.wait_ge(s_sc[0], upto(b, s_sc, 1))
                eng.wait_ge(s_scat[0], upto(b, s_scat, 0))
                for t in range(NT):
                    dve.tensor_scalar(KBT[:, t, :], HX[:, t, :], MV[:, t, 0:1], SCR[:, t:t + 1],
                                      ALU.subtract, ALU.mult).then_inc(s_xn[0], 1)
                for t in range(NT):
                    dve.tensor_scalar(XA[:, t, :], HX[:, t, :], MV[:, t, 0:1], RS[:, t:t + 1],
                                      ALU.subtract, ALU.mult).then_inc(s_xa[0], 1)

                for c in range(CH):
                    eng.wait_ge(s_xnT[0], upto(b, s_xnT, 2 * c + 2))
                    dve.tensor_tensor(EB[:, c, :], XN[:, c, 1:T + 1], XN[:, c, 0:T], ALU.subtract)\
                       .then_inc(s_dx[0], 1)
                for c in range(CH):
                    eng.wait_ge(s_dx[0], upto(b, s_dx, c + 1))
                    mixed(b, s_mk, MA, "mix_k", c)
                for c in range(CH):
                    mixed(b, s_mv, MB, "mix_v", c)
                eng.wait_ge(s_k[0], upto(b, s_k, 4))
                for c in range(CH):
                    mixed(b, s_mr, MA, "mix_r", c)

                for d in range(CH):
                    k, v, r = KB[:, d, :], VR[:, 0, d, :], VR[:, 1, d, :]
                    before, now = PP[:, 0:T], PP[:, 1:T + 1]
                    e1b, e2b = EB[:, 0, :], EB[:, 1, :]
                    AA, BB = XN[:, 0, :], XN[:, 1, :]
                    D, N = 5 * d, 7 * d

                    def exp_arg(i):
                        return upto(b, s_d, D + i)

                    eng.wait_ge(s_k[0], upto(b, s_k, 4))
                    dve.tensor_tensor_scan(now, DECN[:, d:d + 1].broadcast_to([P, T]), k, NEG, ALU.add, ALU.max)\
                       .then_inc(s_pp[0], 1)
                    eng.wait_ge(s_pp[0], upto(b, s_pp, d + 1))
                    eng.wait_ge(s_mr[0], upto(b, s_mr, 2))
                    eng.wait_ge(s_rw[0], upto(b, s_rw, d))
                    dve.scalar_tensor_tensor(e1b, before, DECN[:, d:d + 1], now, ALU.add, ALU.subtract)\
                       .then_inc(s_d[0], 1)
                    dve.tensor_tensor(e2b, k, now, ALU.subtract).then_inc(s_d[0], 1)
                    eng.wait_ge(s_v[0], upto(b, s_v, 4))
                    dve.scalar_tensor_tensor(E2, k, vec("first", d), before, ALU.add, ALU.subtract)\
                       .then_inc(s_d[0], 1)
                    eng.wait_ge(s_d[0], exp_arg(3))
                    dve.tensor_scalar(E1, E2, 0.0, None, ALU.max).then_inc(s_d[0], 1)
                    dve.tensor_scalar(E2, E2, 0.0, None, ALU.min).then_inc(s_d[0], 1)
                    eng.wait_ge(s_r[0], upto(b, s_r, 4))
                    eng.wait_ge(s_er[0], upto(b, s_er, 2 * d + 1))
                    dve.tensor_scalar(r, r, 0.0, None, ALU.min).then_inc(s_rm[0], 1)
                    eng.wait_ge(s_ex[0], upto(b, s_ex, 4 * d + 2))
                    dve.tensor_tensor(V2[:, :], e2b, v, ALU.mult).then_inc(s_ev[0], 1)
                    dve.tensor_tensor_scan(BB[:, 1:T + 1], e1b, e2b, 0.0, ALU.mult, ALU.add).then_inc(s_ab[0], 1)
                    eng.wait_ge(s_ev[0], upto(b, s_ev, d + 1))
                    dve.tensor_tensor_scan(AA[:, 1:T + 1], e1b, V2[:, :], 0.0, ALU.mult, ALU.add)\
                       .then_inc(s_ab[0], 1)
                    eng.wait_ge(s_ex[0], upto(b, s_ex, 4 * d + 4))
                    eng.wait_ge(s_ab[0], upto(b, s_ab, 2 * d + 1))
                    dve.tensor_tensor(e2b, E1, BB[:, 0:T], ALU.mult).then_inc(s_nd[0], 1)
                    eng.wait_ge(s_ab[0], upto(b, s_ab, 2 * d + 2))
                    dve.tensor_tensor(V2[:, :], E1, AA[:, 0:T], ALU.mult).then_inc(s_nd[0], 1)
                    eng.wait_ge(s_nd[0], upto(b, s_nd, N + 1))
                    dve.tensor_tensor(e2b, e2b, E2, ALU.add).then_inc(s_nd[0], 1)
                    eng.wait_ge(s_nd[0], upto(b, s_nd, N + 2))
                    dve.tensor_tensor(E1, E2, v, ALU.mult).then_inc(s_nd[0], 1)
                    eng.wait_ge(s_nd[0], upto(b, s_nd, N + 4))
                    dve.tensor_tensor(V2[:, :], V2[:, :], E1, ALU.add).then_inc(s_nd[0], 1)
                    eng.wait_ge(s_er[0], upto(b, s_er, 2 * d + 2))
                    dve.scalar_tensor_tensor(e2b, EE[:, :], 1.0, e2b, ALU.add, ALU.mult).then_inc(s_nd[0], 1)
                    eng.wait_ge(s_y[0], upto(b, s_y, 2 * d + 1))
                    dve.tensor_tensor(e1b, r, e1b, ALU.subtract).then_inc(s_nd[0], 1)
                    eng.wait_ge(s_y[0], upto(b, s_y, 2 * d + 2))
                    dve.tensor_tensor(KB[:, d, :], V2[:, :], e1b, ALU.mult).then_inc(s_rw[0], 1)

            def mlp(b):
                use, bank = ring(b, MLP_FROM)
                for i in range(4):
                    src = bank()
                    pair = XA[:, 2 * i:2 * i + 2, :].rearrange("p t c -> p (t c)")
                    if i == 0:
                        eng.wait_ge(s_xa[0], upto(b, s_xa, NT))
                    dve.tensor_tensor(pair, pair, src, ALU.add).then_inc(s_x2[0], 1)
                stats(b, XA, s_x2, 2, s_st2, MV2)
                eng.wait_ge(s_st2[0], upto(b, s_st2, 2 * NT))
                dve.tensor_scalar(VE2[:, :], MV2[:, :, 1], EPS, None, ALU.add).then_inc(s_ve2[0], 1)
                eng.wait_ge(s_rs2[0], upto(b, s_rs2, 1))
                for t in range(NT):
                    dve.tensor_scalar(VT[:, t, :], XA[:, t, :], MV2[:, t, 0:1], RS2[:, t:t + 1],
                                      ALU.subtract, ALU.mult).then_inc(s_xn2[0], 1)
                for c in range(CH):
                    eng.wait_ge(s_xn2T[0], upto(b, s_xn2T, 2 * c + 2))
                    dve.tensor_tensor(EB[:, c, :], XN[:, c, 1:T + 1], XN[:, c, 0:T], ALU.subtract)\
                       .then_inc(s_dx2[0], 1)
                for c in range(CH):
                    eng.wait_ge(s_dx2[0], upto(b, s_dx2, c + 1))
                    mixed(b, s_mr2, MB, "ffn_mix_r", c)
                for c in range(CH):
                    mixed(b, s_mk2, MA, "ffn_mix_k", c)
                use[0] += 4
                for q in range(NQ):
                    LG = EB[:, :, :].rearrange("p c t -> p (c t)")[:, 2 * TQ * q:2 * TQ * q + 2 * TQ]
                    eng.wait_ge(s_r2e[0], upto(b, s_r2e, 4 * q + 3))
                    dve.scalar_tensor_tensor(EE[:, :], LG, 0.0, EE[:, :], ALU.min, ALU.subtract)\
                       .then_inc(s_g2[0], 1)
                    for i in range(2):
                        src = bank(10 if i == 0 else 0)
                        n = 2 * q + i
                        two = (slice(None), slice(2 * n, 2 * n + 2), slice(None))
                        flat = lambda z: z[two].rearrange("p t c -> p (t c)")
                        eng.wait_ge(s_r2e[0], upto(b, s_r2e, 4 * q + 4))
                        dve.tensor_tensor(EE[:, TQ * i:TQ * i + TQ], EE[:, TQ * i:TQ * i + TQ], src, ALU.mult)\
                           .then_inc(s_sk[0], 1)
                        eng.wait_ge(s_sk[0], upto(b, s_sk, n + 1))
                        dve.tensor_tensor(flat(XA), flat(XA), EE[:, TQ * i:TQ * i + TQ], ALU.add)\
                           .then_inc(s_x3[0], 1)
                        eng.wait_ge(s_x3[0], upto(b, s_x3, n + 1))
                        if n == 0:
                            eng.wait_ge(s_out[0], upto(b, s_out, 0))
                        dve.tensor_tensor(flat(H2), flat(HX), flat(XA), ALU.add).then_inc(s_h2[0], 1)
                stats(b, H2, s_h2, 2, s_st3, MV3)
                eng.wait_ge(s_st3[0], upto(b, s_st3, 2 * NT))
                dve.tensor_scalar(VE3[:, :], MV3[:, :, 1], EPS, None, ALU.add).then_inc(s_ve3[0], 1)
                eng.wait_ge(s_rs3[0], upto(b, s_rs3, 1))
                for t in range(NT):
                    dve.tensor_scalar(KBT[:, t, :], H2[:, t, :], MV3[:, t, 0:1], RS3[:, t:t + 1],
                                      ALU.subtract, ALU.mult).then_inc(s_ti[0], 1)
                for t in range(NT):
                    eng.wait_ge(s_ti[0], upto(b, s_ti, t + 1))
                    if t:
                        eng.wait_ge(s_z[0], upto(b, s_z, t))
                    dve.tensor_tensor_reduce(out=V2[:, 0:C], in0=KBT[:, t, :], in1=WG[:, :], scale=1.0, scalar=0.0,
                                             op0=ALU.mult, op1=ALU.add, accum_out=ZC[:, t:t + 1]).then_inc(s_z[0], 1)
                eng.wait_ge(s_ze[0], upto(b, s_ze, 1))
                dve.tensor_scalar(ZP[:, :], ZE[:, :], 1.0, None, ALU.add).then_inc(s_g[0], 1)
                eng.wait_ge(s_g[0], upto(b, s_g, 1))
                dve.reciprocal(GC[:, :], ZP[:, :]).then_inc(s_g[0], 1)
                eng.wait_ge(s_g[0], upto(b, s_g, 2))
                eng.wait_ge(s_fin[0], upto(b, s_fin, 0))
                dve.tensor_copy(G2[:, :], GC[:, :]).then_inc(s_g[0], 1)
                use[0] += 2
                eng.wait_ge(s_grow[0], upto(b, s_grow, 2))
                rows, waste = EB[:, 0, :], EB[:, 1, :]
                for t in range(NT):
                    own = GC[:, t:t + 1]
                    eng.wait_ge(s_cnt[0], upto(b, s_cnt, 3 * t))
                    dve.tensor_scalar(waste[:, P * t:T], rows[:, P * t:T], own, None, ALU.is_gt, ALU.add,
                                      accum_out=CNT[:, t, 0:1]).then_inc(s_cnt[0], 1)
                    if t:
                        dve.tensor_scalar(waste[:, 0:P * t], rows[:, 0:P * t], own, None, ALU.is_ge, ALU.add,
                                          accum_out=CNT[:, t, 1:2]).then_inc(s_cnt[0], 1)
                    else:
                        dve.memset(CNT[:, t, 1:2], 0.0).then_inc(s_cnt[0], 1)
                    dve.scalar_tensor_tensor(V2[:, P * t:P * t + P], rows[:, P * t:P * t + P], own, LOW[:, :],
                                             ALU.is_equal, ALU.mult, accum_out=CNT[:, t, 2:3]).then_inc(s_cnt[0], 1)
                eng.wait_ge(s_cnt[0], upto(b, s_cnt, 3 * NT))
                dve.tensor_reduce(RANKF[:, :], CNT[:, :, :], AX.X, ALU.add).then_inc(s_rank[0], 1)
                eng.wait_ge(s_rank[0], upto(b, s_rank, 1))
                eng.wait_ge(s_gath[0], upto(b, s_gath, 0))
                dve.tensor_copy(RANK[:, :], RANKF[:, :]).then_inc(s_rank[0], 1)
                assert use[0] == s_pa[1]

            def attention(b):
                use = [0]

                def pair(skip=0):
                    use[0] += skip
                    u = use[0]
                    use[0] += 1
                    eng.wait_ge(s_pc[0], upto(b, s_pc, u + 1))
                    return PC[:, u % 2, :, :]

                use[0] = 1
                for i in range(2):
                    src = pair()
                    eng.wait_ge(s_qh[0], upto(b, s_qh, i + 1))
                    eng.wait_ge(s_qw[0], upto(b, s_qw, 32 * i))
                    dve.tensor_tensor(QHL[:, 1, :, :], src, QHL[:, 0, :, :].bitcast(F32), ALU.subtract)\
                       .then_inc(s_ql[0], 1)
                use[0] += 1
                for h in range(H):
                    for n in range(2):
                        src = pair()
                        dve.tensor_reduce(NM[:, 2 * n:2 * n + 2, h], src, AX.X, ALU.max, negate=True)\
                           .then_inc(s_nm[0], 1)
                src = pair()
                eng.wait_ge(s_mh[0], upto(b, s_mh, 1))
                dve.tensor_tensor(MHL[:, 1, :], src[0:H, 0, :], MHL[:, 0, :].bitcast(F32), ALU.subtract)\
                   .then_inc(s_ml[0], 1)
                use[0] += 32
                for n in range(2):
                    src = pair()
                    sums = src.rearrange("p g (t i w) -> p g t i w", t=KT, i=4)[:, :, :, :, DH]
                    dve.reciprocal(RSUM[:, 2 * n:2 * n + 2, :, :].rearrange("p g t i -> p (g t) i"),
                                   sums.rearrange("p g t i -> p (g t) i")).then_inc(s_rsum[0], 1)
                for n in range(2):
                    eng.wait_ge(s_rsum[0], upto(b, s_rsum, n + 1))
                    dve.tensor_copy(RWIDE[n].rearrange("p g t (i w) -> p (g t i) w", w=32),
                                    RSUM[:, 2 * n:2 * n + 2, :, :].rearrange("p g t i -> p (g t i)")
                                    .unsqueeze(2).broadcast_to([P, 32, 32])).then_inc(s_rw2[0], 1)
                for n in range(2):
                    src = pair()
                    dve.tensor_tensor(OT[:, 2 * n:2 * n + 2, :], OT[:, 2 * n:2 * n + 2, :], src, ALU.mult)\
                       .then_inc(s_on[0], 1)
                eng.wait_ge(s_gath[0], upto(b, s_gath, 16 * NT))
                for t in range(NT):
                    dve.scalar_tensor_tensor(H2[:, t, :], GA[:, t, :], G2[:, t:t + 1], H2[:, t, :],
                                             ALU.mult, ALU.add).then_inc(s_fin[0], 1)

            eng.wait_ge(s_w[0], ALL_LOADED + 16)
            eng.wait_ge(s_const[0], 7)
            eng.wait_ge(s_dec[0], 1)
            dve.tensor_scalar(DECN[:, :], DEC[:, :], -1.0, None, ALU.mult).then_inc(s_decn[0], 1)
            eng.wait_ge(s_decn[0], 1)
            every_batch(recurrence, mlp, attention, eng)


_ORDER = ["x", "vectors", "tok_w1", "tok_b1", "tok_w2", "tok_b2", "w_k", "w_v", "w_r", "w_o", "w_kf", "w_rf",
          "w_vf", "gate_w", "w_q2", "w_k2", "w_v2", "w_o2", "identity", "lower"]


def kernel(**inputs):
    import concourse.bacc as bacc
    from concourse.bass_utils import run_bass_kernel_spmd

    a = {k: np.asarray(v) for k, v in inputs.items()}

    def rows(w):
        return np.ascontiguousarray(w.reshape(-1, P, w.shape[1]).transpose(1, 0, 2))

    by_name = {
        "ln1_g": "L0_attn_ln1_g", "ln1_b": "L0_attn_ln1_b", "ln2_g": "L0_attn_ln2_g", "ln2_b": "L0_attn_ln2_b",
        "mix_k": "L0_attn_att_mix_k", "mix_v": "L0_attn_att_mix_v", "mix_r": "L0_attn_att_mix_r",
        "decay": "L0_attn_time_decay", "first": "L0_attn_time_first",
        "ffn_mix_k": "L0_attn_ffn_mix_k", "ffn_mix_r": "L0_attn_ffn_mix_r",
    }
    vectors = np.stack([a[by_name[n]].reshape(CH, P) for n in VECTORS]).transpose(2, 0, 1)
    w_o2 = np.zeros((NG, 4, 32, C), np.float32)
    w_o2[:, :, :DH] = a["L0_ffn_Wo"].reshape(NG, 4, DH, C)
    arrays = {
        "x": a["x"].reshape(B * T, C),
        "vectors": np.ascontiguousarray(vectors),
        "tok_w1": rows(a["L0_tok_W1"]),
        "tok_b1": a["L0_tok_b1"].reshape(P, 1),
        "tok_w2": a["L0_tok_W2"].reshape(P, 1),
        "tok_b2": np.ascontiguousarray(np.broadcast_to(a["L0_tok_b2"].reshape(1, 1), (P, 1))),
        "w_k": rows(a["L0_attn_Wk"].T), "w_v": rows(a["L0_attn_Wv"].T), "w_r": rows(a["L0_attn_Wr"].T),
        "w_o": rows(a["L0_attn_Wo"].T), "w_kf": rows(a["L0_attn_Wk_ffn"].T),
        "w_rf": rows(a["L0_attn_Wr_ffn"].T), "w_vf": rows(a["L0_attn_Wv_ffn"].T),
        "gate_w": np.ascontiguousarray(np.broadcast_to(a["L0_ffn_Wg"].reshape(1, C), (P, C))),
        "w_q2": rows(a["L0_ffn_Wq"]), "w_k2": rows(a["L0_ffn_Wk"]), "w_v2": rows(a["L0_ffn_Wv"]),
        "w_o2": np.ascontiguousarray(w_o2.reshape(NG, P, C).transpose(1, 0, 2)),
        "identity": np.eye(P, dtype=np.float32),
        "lower": np.tril(np.ones((P, P), np.float32), -1),
    }
    nc = bacc.Bacc("TRN2", target_bir_lowering=False, num_devices=1)
    args = [nc.dram_tensor(f"in_{n}", arrays[n].shape, mybir.dt.from_np(arrays[n].dtype),
                           kind="ExternalInput").ap() for n in _ORDER]
    result = nc.dram_tensor("out_tokens", (B * T, C), F32, kind="ExternalOutput").ap()
    vit_tower(nc, *args, result)
    r = run_bass_kernel_spmd(nc, [{f"in_{n}": arrays[n] for n in _ORDER}], core_ids=[0])
    return r.results[0]["out_tokens"].reshape(B, T, C)
```

```python
from contextlib import ExitStack

import numpy as np

import concourse.bass as bass
from concourse import mybir

F32 = mybir.dt.float32
F32R = mybir.dt.float32r
U32 = mybir.dt.uint32
ALU = mybir.AluOpType
ACT = mybir.ActivationFunctionType
AX = mybir.AxisListType

P = 128
B, T, C = 4, 1024, 256
NT = T // P
CH = C // P
TQ = 512
NQ = T // TQ
FFN = 1024
NF = FFN // P
H, DH = 16, 16
CAP = T // 2
KT = CAP // P
NG = 4
EPS = 1e-5
NEG = -1e38

VECTORS = ["ln1_g", "ln1_b", "ln2_g", "ln2_b", "mix_k", "mix_v", "mix_r",
           "decay", "first", "ffn_mix_k", "ffn_mix_r"]


class Lap:

    def __init__(self, plus, register=None):
        self.plus, self.register = plus, register

    def times(self, per, k=0):
        fixed = self.plus * per + k
        return fixed if self.register is None else self.register * per + fixed


def every_batch(iteration, eng):
    iteration(Lap(0), None)
    with eng.Fori(0, B - 1) as i:
        iteration(Lap(1, i), Lap(0, i))
    iteration(None, Lap(B - 1))


def vit_tower(nc, x, vectors, tok_w1, tok_b1, tok_w2, tok_b2, w_k, w_v, w_r, w_o,
              w_kf, w_rf, w_vf, gate_w, w_q2, w_k2, w_v2, w_o2, identity, lower, out):
    nc.disable_value_cache = True
    ctx = ExitStack()
    with ctx:
        def sb(name, shape, dt=F32):
            return ctx.enter_context(nc.sbuf_tensor(name, shape, dt))

        per_batch = {}

        def sem(name, per):
            s = ctx.enter_context(nc.semaphore(name))
            per_batch[name] = per
            return (s, per)

        def upto(b, signal, k):
            return b.times(signal[1], k)

        W1 = sb("W1", [P, CH, P])
        W2 = sb("W2", [P, 1])
        B1 = sb("B1", [P, 1])
        B2 = sb("B2", [P, 1])
        WK = sb("WK", [P, CH, C])
        WV = sb("WV", [P, CH, C])
        WR = sb("WR", [P, CH, C])
        WO = sb("WO", [P, CH, C])
        WKF = sb("WKF", [P, CH, FFN])
        WRF = sb("WRF", [P, CH, C])
        WVF = sb("WVF", [P, NF, C])
        WG = sb("WG", [P, C])
        WQ2 = sb("WQ2", [P, CH, C])
        WK2 = sb("WK2", [P, CH, C])
        WV2 = sb("WV2", [P, CH, C])
        WO2 = sb("WO2", [P, NG, C])
        VEC = sb("VEC", [P, len(VECTORS), CH])
        IDN = sb("IDN", [P, P])
        LOW = sb("LOW", [P, P])

        def vec(name, c):
            i = VECTORS.index(name)
            return VEC[:, i, c:c + 1]

        XIN = sb("XIN", [P, NT, C])
        HX = sb("HX", [P, NT, C])
        XA = sb("XA", [P, NT, C])
        XN = sb("XN", [P, CH, T + 1])
        MA = sb("MA", [P, CH, T])
        MB = sb("MB", [P, CH, T])
        KB = sb("KB", [P, CH, T])
        VR = sb("VR", [P, 2, CH, T])
        PP = sb("PP", [P, T + 1])
        EB = sb("EB", [P, CH, T])
        V2 = sb("V2", [P, T])
        EE = sb("EE", [P, T])
        DEC = sb("DEC", [P, CH])
        DECN = sb("DECN", [P, CH])
        STATS = sb("STATS", [P, NT, 6])
        MV = sb("MV", [P, NT, 2])
        MV2 = sb("MV2", [P, NT, 2])
        MV3 = sb("MV3", [P, NT, 2])
        VE = sb("VE", [P, 2 * NT])
        RS = sb("RS", [P, 2 * NT])
        VE2 = sb("VE2", [P, NT])
        RS2 = sb("RS2", [P, NT])
        VE3 = sb("VE3", [P, NT])
        RS3 = sb("RS3", [P, NT])
        HALF = sb("HALF", [P, 2 * NT])
        HOLD = sb("HOLD", [P, 3])
        SCR = sb("SCR", [P, NT])
        EN = sb("EN", [P, NT, 1])
        ENM = sb("ENM", [P, NT])
        END = sb("END", [P, NT])
        ENE = sb("ENE", [P, NT, 1])
        ENS = sb("ENS", [P, NT])
        ENR = sb("ENR", [P, NT])
        PW = sb("PW", [P, NT])
        ZC = sb("ZC", [P, NT])
        ZE = sb("ZE", [P, NT])
        ZP = sb("ZP", [P, NT])
        GC = sb("GC", [P, NT])
        CNT = sb("CNT", [P, NT, 3])
        RANKF = sb("RANKF", [P, NT])
        H2 = sb("H2", [P, NT, C])
        G2 = sb("G2", [P, NT])
        RANK = sb("RANK", [P, NT], U32)
        SEL = sb("SEL", [P, KT, C])
        AT = sb("AT", [P, CH, CAP])
        QS = sb("QS", [P, H // 2, CAP], F32R)
        KS = sb("KS", [P, H // 2, CAP], F32R)
        VV = sb("VV", [P, KT, H, 32])
        PR = sb("PR", [P, 2, 2, CAP])
        OT = sb("OT", [P, NG, CAP])
        NM = sb("NM", [P, KT, H])
        RSUM = sb("RSUM", [P, NG, KT, 4])

        HID = VR[:, :, :, :].rearrange("p a c t -> p (a c t)").rearrange("p (f t) -> p f t", t=TQ)
        KBT = KB[:, :, :].rearrange("p a t -> p (a t)").rearrange("p (t c) -> p t c", c=C)
        VT = VR[:, 0, :, :].rearrange("p a t -> p (a t)").rearrange("p (t c) -> p t c", c=C)
        E1, E2 = MB[:, 0, :], MB[:, 1, :]
        MHL = AT[0:H, :, :].bitcast(F32R)
        RWIDE = [z[:, :, :].rearrange("p a n -> p (a n)").rearrange("p (g t w) -> p g t w", g=2, t=KT)
                 for z in (AT, SEL)]
        GA = PR[:, :, :, :].rearrange("p a i n -> p (a i n)").rearrange("p (t c) -> p t c", c=C)
        QHL = PR[:, :, :, :].bitcast(F32R)

        kept_d = nc.dram_tensor("kept_d", [CAP, C], F32, kind="Internal").ap()
        qk_d = nc.dram_tensor("qk_d", [4, C, CAP], F32, kind="Internal").ap()
        max_d = nc.dram_tensor("max_d", [2, H, CAP], F32, kind="Internal").ap()
        att_d = nc.dram_tensor("att_d", [T, C], F32, kind="Internal").ap()

        PA = ctx.enter_context(nc.psum_tensor("PA", [P, 3, TQ], F32))
        PC = ctx.enter_context(nc.psum_tensor("PC", [P, 2, 2, TQ], F32))
        PO = ctx.enter_context(nc.psum_tensor("PO", [P, TQ], F32))

        s_w = sem("weights_in", 0)
        s_const = sem("constants_set", 0)
        s_dec = sem("decay_ready", 0)
        s_decn = sem("w_ready", 0)
        s_x = sem("x_in", 16)
        s_pa = sem("bank_filled", 57)
        s_xT = sem("xT_out", 4)
        s_hT = sem("tanh_out", 2)
        s_ee = sem("energy_exp", 1)
        s_xnT = sem("xnT_out", 4)
        s_k = sem("k_out", 4)
        s_v = sem("v_out", 4)
        s_r = sem("r_out", 4)
        s_ex = sem("wkv_exp", 8)
        s_er = sem("r_exp", 4)
        s_y = sem("y_exp", 4)
        s_xn2T = sem("xn2T_out", 4)
        s_r2 = sem("r2_out", 4)
        s_r2e = sem("r2_exp", 8)
        s_relu = sem("relu_out", 16)
        s_hid = sem("hidden_out", 16)
        s_ze = sem("gate_exp", 1)
        s_grow = sem("gate_rows", 2)
        s_en = sem("energy", 3)
        s_pw = sem("pool_weights", 3)
        s_h = sem("pooled", 8)
        s_st = sem("norm_stats", 16)
        s_ve = sem("norm_var", 4)
        s_sc = sem("norm_scale", 1)
        s_xa = sem("xa", 8)
        s_xn = sem("xn", 8)
        s_dx = sem("token_diff", 2)
        s_mk = sem("mixed_k", 2)
        s_mv = sem("mixed_v", 2)
        s_mr = sem("mixed_r", 2)
        s_pp = sem("exponent", 2)
        s_d = sem("exp_args", 10)
        s_rm = sem("min_r", 2)
        s_ev = sem("e2b_v", 2)
        s_ab = sem("scans", 4)
        s_nd = sem("num_den", 14)
        s_rw = sem("rwkv", 2)
        s_x2 = sem("x2", 4)
        s_st2 = sem("norm2_stats", 16)
        s_ve2 = sem("norm2_var", 1)
        s_xn2 = sem("xn2", 8)
        s_dx2 = sem("token_diff2", 2)
        s_mk2 = sem("mixed_k2", 2)
        s_mr2 = sem("mixed_r2", 2)
        s_g2 = sem("r2_arg", 2)
        s_sk = sem("gated_kv", 4)
        s_x3 = sem("x3", 4)
        s_h2 = sem("h2", 4)
        s_st3 = sem("norm3_stats", 16)
        s_ve3 = sem("norm3_var", 2)
        s_ti = sem("router_tokens", 8)
        s_z = sem("gate_logits", 8)
        s_g = sem("gates", 3)
        s_cnt = sem("counts", 24)
        s_rank = sem("ranks", 2)
        s_rs = sem("rstd", 1)
        s_rs2 = sem("rstd2", 1)
        s_rs3 = sem("rstd3", 2)
        s_scat = sem("kept_stored", 16 * NT)
        s_gath = sem("gathered", 16 * NT)
        s_sel = sem("kept_in", 16)
        s_pc = sem("pair_filled", 74)
        s_pv = sem("values_done", 16)
        s_at = sem("aT_out", 1)
        s_qh = sem("qk_high", 2)
        s_ql = sem("qk_low", 2)
        s_qw = sem("qk_stored", 64)
        s_qi = sem("stacks_in", 16 * 12)
        s_vv = sem("v2_out", 1)
        s_nm = sem("maxima", 32)
        s_mh = sem("max_high", 1)
        s_ml = sem("max_low", 1)
        s_mw = sem("max_stored", 32)
        s_mi = sem("max_in", 64)
        s_p = sem("probs", 32)
        s_oT = sem("heads_out", 4)
        s_rsum = sem("sums_inverse", 2)
        s_rw2 = sem("inverse_spread", 2)
        s_on = sem("heads_norm", 2)
        s_o = sem("attention_out", 1)
        s_ow = sem("attention_stored", 16)
        s_fin = sem("result", 8)
        s_out = sem("out_stored", 32)

        emptied = ([(s_xT, i + 1) for i in range(4)] + [(s_hT, i + 1) for i in range(2)] + [(s_en, 1)]
                   + [(s_xnT, i + 1) for i in range(4)] + [(s_k, i + 1) for i in range(4)]
                   + [(s_v, i + 1) for i in range(4)] + [(s_r, i + 1) for i in range(4)]
                   + [(s_x2, i + 1) for i in range(4)] + [(s_xn2T, i + 1) for i in range(4)])
        for q in range(NQ):
            emptied += [(s_r2, 2 * q + i + 1) for i in range(2)]
            emptied += [(s_relu, NF * q + i + 1) for i in range(NF)]
            emptied += [(s_sk, 2 * q + i + 1) for i in range(2)]
        emptied += [(s_grow, i + 1) for i in range(2)]
        assert len(emptied) == s_pa[1] and len(emptied) % 3 == 0
        emptied2 = [(s_at, 1), (s_ql, 1), (s_ql, 2), (s_vv, 1)] + [(s_nm, i + 1) for i in range(32)]
        emptied2 += [(s_ml, 1)] + [(s_p, i + 1) for i in range(32)]
        emptied2 += [(s_rsum, 1), (s_rsum, 2), (s_on, 1), (s_on, 2), (s_o, 1)]
        assert len(emptied2) == s_pc[1] and len(emptied2) % 2 == 0

        NORM_FROM, KVR_FROM, MLP_FROM, FFN_FROM = 7, 11, 23, 31
        MAX_FROM, EXP_FROM, SUMS_FROM = 4, 37, 69
        WO_STEP = 12
        block = ctx.enter_context(nc.Block())
        act, dve, pe, pool, sp = nc.scalar, nc.vector, nc.tensor, nc.gpsimd, nc.sync

        LOADS = [(VEC, vectors), (W1, tok_w1), (B1, tok_b1), (W2, tok_w2), (B2, tok_b2), (IDN, identity),
                 (WK, w_k), (WV, w_v), (WR, w_r), (WO, w_o), (WKF, w_kf), (WRF, w_rf), (WVF, w_vf),
                 (WG, gate_w), (LOW, lower), (WQ2, w_q2), (WK2, w_k2), (WV2, w_v2), (WO2, w_o2)]
        ALL_LOADED = 16 * len(LOADS)

        @block.sync
        def _(eng):
            def load_x(b):
                row = b.times(T)
                src = x[bass.ds(row, T), :] if b.register is not None else x[row:row + T, :]
                sp.dma_start(XIN[:, :, :], src.rearrange("(t p) c -> p t c", p=P)).then_inc(s_x[0], 16)

            def iteration(b, a):
                if b:
                    eng.wait_ge(s_h[0], upto(b, s_h, 0))
                    load_x(b)
                if a:
                    attention(a)

            def attention(b):
                eng.wait_ge(s_scat[0], upto(b, s_scat, 16 * NT))
                sp.dma_start(SEL[:, :, :], kept_d.rearrange("(t p) c -> p t c", p=P)).then_inc(s_sel[0], 16)
                for i in range(2):
                    for part, done in ((0, s_qh), (1, s_ql)):
                        eng.wait_ge(done[0], upto(b, done, i + 1))
                        sp.dma_start(qk_d[2 * i + part].rearrange("(c p) n -> p c n", p=P),
                                     QHL[:, part, :, :].bitcast(F32)).then_inc(s_qw[0], 16)
                for i, (stack, parts) in enumerate(((QS, (0, 0, 1)), (KS, (2, 3, 2)))):
                    eng.wait_ge(s_qw[0], upto(b, s_qw, 32 * (i + 1)))
                    for odd in range(2):
                        for n, part in enumerate(parts):
                            at = 64 * odd + DH * n
                            sp.dma_start(stack[at:at + DH, :, :].bitcast(F32),
                                         qk_d[part].rearrange("(j r d) n -> r d j n", r=2, d=DH)[odd])\
                              .then_inc(s_qi[0], 16)
                for part, done in ((0, s_mh), (1, s_ml)):
                    eng.wait_ge(done[0], upto(b, done, 1))
                    sp.dma_start(max_d[part], MHL[:, part, :].bitcast(F32)).then_inc(s_mw[0], 16)
                eng.wait_ge(s_mw[0], upto(b, s_mw, 32))
                for odd in range(2):
                    for part in range(2):
                        at = 64 * odd + 3 * DH + part
                        sp.dma_start(QS[at:at + 1, :, :].bitcast(F32),
                                     max_d[part:part + 1].rearrange("a (j r) n -> r a j n", r=2)[odd])\
                          .then_inc(s_mi[0], 16)
                eng.wait_ge(s_o[0], upto(b, s_o, 1))
                sp.dma_start(att_d[0:CAP].rearrange("(t p) c -> p t c", p=P), SEL[:, :, :]).then_inc(s_ow[0], 16)
                for half in range(2):
                    eng.wait_ge(s_fin[0], upto(b, s_fin, 4 * (half + 1)))
                    row = b.times(T, 512 * half)
                    dst = out[bass.ds(row, 512), :] if b.register is not None else out[row:row + 512, :]
                    sp.dma_start(dst.rearrange("(t p) c -> p t c", p=P),
                                 H2[:, 4 * half:4 * half + 4, :]).then_inc(s_out[0], 16)

            for buf, src in LOADS:
                sp.dma_start(buf[:], src).then_inc(s_w[0], 16)
            eng.wait_ge(s_const[0], 7)
            sp.dma_start(att_d[CAP:T].rearrange("(t p) c -> p t c", p=P), GA[:, 0:KT, :]).then_inc(s_w[0], 16)
            every_batch(iteration, eng)
            eng.wait_ge(s_out[0], 32 * B)
            eng.wait_ge(s_w[0], ALL_LOADED + 16)

        @block.gpsimd
        def _(eng):
            def hold(cell):
                pool.tensor_tensor(HOLD[:, cell:cell + 1], HALF[:, 0:1], HALF[:, 0:1], ALU.mult)

            def power(b, dst, src, n, need, k, done):
                eng.wait_ge(need[0], upto(b, need, k))
                pool.tensor_tensor(dst, src, HALF[:, 0:n], ALU.pow).then_inc(done[0], 1)

            def scatter(b):
                eng.wait_ge(s_rank[0], upto(b, s_rank, 2))
                eng.wait_ge(s_ti[0], upto(b, s_ti, NT))
                eng.wait_ge(s_sel[0], upto(b, s_sel, 0))
                hold(1)
                for t in range(NT):
                    pool.indirect_dma_start(
                        out=kept_d, out_offset=bass.IndirectOffsetOnAxis(ap=RANK[:, t:t + 1], axis=0),
                        in_=KB[:, :, :].rearrange("p a t -> p (a t)")[:, C * t:C * t + C], in_offset=None,
                        bounds_check=CAP - 1, oob_is_err=False).then_inc(s_scat[0], 16)

            def gather(b):
                eng.wait_ge(s_ow[0], upto(b, s_ow, 16))
                hold(2)
                for t in range(NT):
                    pool.indirect_dma_start(
                        out=GA[:, t, :], out_offset=None, in_=att_d,
                        in_offset=bass.IndirectOffsetOnAxis(ap=RANK[:, t:t + 1], axis=0))\
                        .then_inc(s_gath[0], 16)

            def iteration(b, a):
                if b:
                    power(b, RS[:, :], VE[:, :], 2 * NT, s_ve, 4, s_rs)
                    power(b, RS2[:, :], VE2[:, :], NT, s_ve2, 1, s_rs2)
                if a:
                    gather(a)
                if b:
                    for q in range(NQ):
                        n = NT // NQ
                        power(b, RS3[:, n * q:n * q + n], VE3[:, n * q:n * q + n], n, s_ve3, q + 1, s_rs3)
                    scatter(b)

            pool.memset(HALF[:], -0.5).then_inc(s_const[0], 1)
            pool.memset(XN[:, :, 0:1], 0.0).then_inc(s_const[0], 1)
            pool.memset(PP[:, 0:1], NEG).then_inc(s_const[0], 1)
            pool.memset(GA, 0.0).then_inc(s_const[0], 1)
            pool.memset(VV[:], 1.0).then_inc(s_const[0], 1)
            pool.memset(QS[:].bitcast(F32), 0.0).then_inc(s_const[0], 1)
            pool.memset(KS[:].bitcast(F32), 1.0).then_inc(s_const[0], 1)
            eng.wait_ge(s_w[0], ALL_LOADED + 16)
            every_batch(iteration, eng)

        @block.tensor
        def _(eng):
            def ring(b, first):
                use = [first]

                def bank():
                    u = use[0]
                    use[0] += 1
                    who, k = emptied[u - 3]
                    if u >= 3:
                        eng.wait_ge(who[0], upto(b, who, k))
                    elif b.plus:
                        eng.wait_ge(who[0], upto(b, who, k - who[1]))
                    return PA[:, u % 3, :]

                return use, bank

            def filled(last_instruction):
                last_instruction.then_inc(s_pa[0], 1)

            def to_channels(b, bank, src, need):
                for c in range(CH):
                    for q in range(NQ):
                        dst = bank()
                        for i in range(4):
                            t = 4 * q + i
                            if need is not None:
                                eng.wait_ge(need[0], upto(b, need, t + 1))
                            m = pe.transpose(dst[:, P * i:P * i + P], src(t, c), IDN[:, :])
                        filled(m)

            def pooling(b):
                use, bank = ring(b, 0)
                eng.wait_ge(s_x[0], upto(b, s_x, 16))
                to_channels(b, bank, lambda t, c: XIN[:, t, P * c:P * c + P], None)
                XT = VR[:, 1, :, :]
                eng.wait_ge(s_xT[0], upto(b, s_xT, 4))
                for q in range(NQ):
                    dst = bank()
                    for c in range(CH):
                        m = pe.matmul(dst, W1[:, c, :], XT[:, c, TQ * q:TQ * q + TQ], start=c == 0, stop=c == CH - 1)
                    filled(m)
                dst = bank()
                eng.wait_ge(s_hT[0], upto(b, s_hT, 2))
                for t in range(NT):
                    m = pe.matmul(dst[:, t:t + 1], V2[:, P * t:P * t + P], W2[:, :], start=True, stop=True)
                filled(m)

            def norm(b):
                use, bank = ring(b, NORM_FROM)
                to_channels(b, bank, lambda t, c: KBT[:, t, P * c:P * c + P], s_xn)

            def project(b, i):
                use, bank = ring(b, KVR_FROM + i)
                w, src, need = ((WK, MA, s_mk), (WV, MB, s_mv), (WR, MA, s_mr))[i // 4]
                d, q = divmod(i % 4, NQ)
                dst = bank()
                for c in range(CH):
                    eng.wait_ge(need[0], upto(b, need, c + 1))
                    m = pe.matmul(dst, w[:, c, P * d:P * d + P], src[:, c, TQ * q:TQ * q + TQ],
                                  start=c == 0, stop=c == CH - 1)
                filled(m)

            def output(b):
                use, bank = ring(b, MLP_FROM)
                for i in range(4):
                    dst = bank()
                    for j in range(2):
                        t = 2 * i + j
                        for d in range(CH):
                            eng.wait_ge(s_rw[0], upto(b, s_rw, d + 1))
                            m = pe.matmul(dst[:, C * j:C * j + C], KB[:, d, P * t:P * t + P], WO[:, d, :],
                                          start=d == 0, stop=d == CH - 1)
                    filled(m)

            def norm2(b):
                use, bank = ring(b, MLP_FROM + 4)
                to_channels(b, bank, lambda t, c: VT[:, t, P * c:P * c + P], s_xn2)

            def ffn_gate(b, q):
                use, bank = ring(b, FFN_FROM + 12 * q)
                for i in range(2):
                    dst = bank()
                    for j in range(2):
                        t = 4 * q + 2 * i + j
                        for c in range(CH):
                            eng.wait_ge(s_mr2[0], upto(b, s_mr2, c + 1))
                            m = pe.matmul(dst[:, C * j:C * j + C], MB[:, c, P * t:P * t + P], WRF[:, c, :],
                                          start=c == 0, stop=c == CH - 1)
                    filled(m)

            def ffn(b, q):
                use, bank = ring(b, FFN_FROM + 12 * q + 2)
                for f in range(NF):
                    dst = bank()
                    for c in range(CH):
                        eng.wait_ge(s_mk2[0], upto(b, s_mk2, c + 1))
                        m = pe.matmul(dst, WKF[:, c, P * f:P * f + P], MA[:, c, TQ * q:TQ * q + TQ],
                                      start=c == 0, stop=c == CH - 1)
                    filled(m)
                for i in range(2):
                    dst = bank()
                    for j in range(2):
                        for f in range(NF):
                            eng.wait_ge(s_hid[0], upto(b, s_hid, NF * q + f + 1))
                            t = 2 * i + j
                            m = pe.matmul(dst[:, C * j:C * j + C], HID[:, f, P * t:P * t + P], WVF[:, f, :],
                                          start=f == 0, stop=f == NF - 1)
                    filled(m)

            def gate_rows(b):
                use, bank = ring(b, s_pa[1] - 2)
                eng.wait_ge(s_g[0], upto(b, s_g, 2))
                for q in range(2):
                    dst = bank()
                    for i in range(4):
                        t = 4 * q + i
                        m = pe.transpose(dst[:, P * i:P * i + P], GC[:, t:t + 1].broadcast_to([P, P]), IDN[:, :])
                    filled(m)
                assert use[0] == s_pa[1]

            def pair(b, u):
                who, k = emptied2[u - 2]
                eng.wait_ge(who[0], upto(b, who, k if u >= 2 else k - who[1]))
                return PC[:, u % 2, :, :]

            def pair_filled(last_instruction):
                last_instruction.then_inc(s_pc[0], 1)

            def kept(b):
                dst = pair(b, 0)
                eng.wait_ge(s_sel[0], upto(b, s_sel, 16))
                for c in range(CH):
                    for t in range(KT):
                        m = pe.transpose(dst[:, c, P * t:P * t + P], SEL[:, t, P * c:P * c + P], IDN[:, :])
                pair_filled(m)
                eng.wait_ge(s_at[0], upto(b, s_at, 1))
                for n, w in enumerate((WQ2, WK2)):
                    dst = pair(b, 1 + n)
                    for d in range(CH):
                        for c in range(CH):
                            m = pe.matmul(dst[:, d, :], w[:, c, P * d:P * d + P], AT[:, c, :],
                                          start=c == 0, stop=c == CH - 1)
                    pair_filled(m)
                dst = pair(b, 3)
                for t in range(KT):
                    for c in range(CH):
                        m = pe.matmul(dst[:, t // 2, C * (t % 2):C * (t % 2) + C], AT[:, c, P * t:P * t + P],
                                      WV2[:, c, :], start=c == 0, stop=c == CH - 1)
                pair_filled(m)

            def query_scores(b, h):
                if h == 0:
                    eng.wait_ge(s_qi[0], upto(b, s_qi, 16 * 12))
                at, j = 64 * (h % 2), h // 2
                for n in range(2):
                    dst = pair(b, MAX_FROM + 2 * h + n)
                    for i in range(2):
                        t = 2 * n + i
                        m = pe.matmul(dst[:, i, :], QS[at:at + 3 * DH, j, P * t:P * t + P],
                                      KS[at:at + 3 * DH, j, :], start=True, stop=True)
                    pair_filled(m)

            def maxima_rows(b):
                dst = pair(b, EXP_FROM - 1)
                eng.wait_ge(s_nm[0], upto(b, s_nm, 32))
                for t in range(KT):
                    m = pe.transpose(dst[0:H, 0, P * t:P * t + P], NM[:, t, :], IDN[:, :])
                pair_filled(m)

            def key_scores(b, step):
                if step == 0:
                    eng.wait_ge(s_mi[0], upto(b, s_mi, 64))
                g, t = divmod(step, KT)
                for n in range(2):
                    dst = pair(b, EXP_FROM + 2 * step + n)
                    j = 2 * g + n
                    for i in range(2):
                        m = pe.matmul(dst[:, i, :], KS[64 * i:64 * i + 64, j, P * t:P * t + P],
                                      QS[64 * i:64 * i + 64, j, :], start=True, stop=True)
                    pair_filled(m)

            def values(b, step):
                g, t = divmod(step, KT)
                if step == 0:
                    eng.wait_ge(s_vv[0], upto(b, s_vv, 1))
                eng.wait_ge(s_p[0], upto(b, s_p, 2 * step + 2))
                if t == 0:
                    eng.wait_ge(s_oT[0], upto(b, s_oT, g))
                for i in range(4):
                    m = pe.matmul(PO[32 * i:32 * i + 32, :], VV[:, t, 4 * g + i, :], PR[:, i // 2, i % 2, :],
                                  start=t == 0, stop=t == KT - 1, tile_position=(0, 32 * i))
                m.then_inc(s_pv[0], 1)

            def sums(b):
                for n in range(2):
                    dst = pair(b, SUMS_FROM + n)
                    for i in range(2):
                        g = 2 * n + i
                        eng.wait_ge(s_oT[0], upto(b, s_oT, g + 1))
                        for t in range(KT):
                            m = pe.transpose(dst[:, i, P * t:P * t + P], OT[:, g, P * t:P * t + P], IDN[:, :])
                    pair_filled(m)

            def inverse_sums(b):
                for n in range(2):
                    dst = pair(b, SUMS_FROM + 2 + n)
                    eng.wait_ge(s_rw2[0], upto(b, s_rw2, n + 1))
                    for i in range(2):
                        for t in range(KT):
                            m = pe.transpose(dst[:, i, P * t:P * t + P],
                                             RWIDE[n][:, i, t, :], IDN[:, :])
                    pair_filled(m)

            def head_output(b):
                dst = pair(b, SUMS_FROM + 4)
                eng.wait_ge(s_on[0], upto(b, s_on, 2))
                for t in range(KT):
                    for g in range(NG):
                        m = pe.matmul(dst[:, t // 2, C * (t % 2):C * (t % 2) + C], OT[:, g, P * t:P * t + P],
                                      WO2[:, g, :], start=g == 0, stop=g == NG - 1)
                pair_filled(m)

            def iteration(b, a):
                if b:
                    pooling(b)
                if a:
                    kept(a)
                if b:
                    norm(b)
                    for i in range(4):
                        project(b, i)
                for h in range(H):
                    if a:
                        query_scores(a, h)
                    if b and h % 2:
                        project(b, 4 + h // 2)
                if a:
                    maxima_rows(a)
                for step in range(NG * KT):
                    if a:
                        key_scores(a, step)
                        if step:
                            values(a, step - 1)
                    if b and step == WO_STEP:
                        output(b)
                if a:
                    values(a, NG * KT - 1)
                    sums(a)
                if b:
                    norm2(b)
                if a:
                    inverse_sums(a)
                if b:
                    ffn_gate(b, 0)
                if a:
                    head_output(a)
                if b:
                    ffn(b, 0)
                    ffn_gate(b, 1)
                    ffn(b, 1)
                    gate_rows(b)

            eng.wait_ge(s_w[0], ALL_LOADED + 16)
            eng.wait_ge(s_const[0], 7)
            every_batch(iteration, eng)

        @block.scalar
        def _(eng):
            def ring(b, first):
                use = [first]

                def bank():
                    u = use[0]
                    use[0] += 1
                    eng.wait_ge(s_pa[0], upto(b, s_pa, u + 1))
                    return PA[:, u % 3, :]

                return use, bank

            def pooling(b):
                use, bank = ring(b, 0)
                act.preload_act_table_set("exp_and_others")
                XT = VR[:, 1, :, :]
                for c in range(CH):
                    for q in range(NQ):
                        src = bank()
                        act.activation(XT[:, c, TQ * q:TQ * q + TQ], src, ACT.Copy).then_inc(s_xT[0], 1)
                eng.wait_ge(s_cnt[0], upto(b, s_cnt, 0))
                for q in range(NQ):
                    src = bank()
                    act.activation(V2[:, TQ * q:TQ * q + TQ], src, ACT.Tanh, bias=B1[:, :]).then_inc(s_hT[0], 1)
                act.preload_act_table_set("natural_log_exp_and_others")
                eng.wait_ge(s_en[0], upto(b, s_en, 3))
                act.activation(ENE[:, :, 0], END[:, :], ACT.Exp).then_inc(s_ee[0], 1)

            def norm(b):
                use, bank = ring(b, NORM_FROM)
                for c in range(CH):
                    for q in range(NQ):
                        src = bank()
                        act.activation(XN[:, c, 1 + TQ * q:1 + TQ * q + TQ], src, ACT.Identity,
                                       scale=vec("ln1_g", c), bias=vec("ln1_b", c)).then_inc(s_xnT[0], 1)

            def project(b):
                use, bank = ring(b, KVR_FROM)
                for dst, done in ((KB, s_k), (VR[:, 0, :, :], s_v), (VR[:, 1, :, :], s_r)):
                    for d in range(CH):
                        for q in range(NQ):
                            src = bank()
                            act.activation(dst[:, d, TQ * q:TQ * q + TQ], src, ACT.Copy).then_inc(done[0], 1)

            def r_exp(b, d):
                eng.wait_ge(s_r[0], upto(b, s_r, 2 * d + 2))
                eng.wait_ge(s_nd[0], upto(b, s_nd, 7 * d))
                act.activation(EE[:, :], VR[:, 1, d, :], ACT.Abs).then_inc(s_er[0], 1)
                eng.wait_ge(s_er[0], upto(b, s_er, 2 * d + 1))
                act.activation(EE[:, :], EE[:, :], ACT.Exp, scale=-1.0).then_inc(s_er[0], 1)

            def wkv_exp(b, d, i):
                buf, sign, step = ((EB[:, 0, :], 1.0, 1), (EB[:, 1, :], 1.0, 2), (E1, -1.0, 4), (E2, 1.0, 5))[i]
                eng.wait_ge(s_d[0], upto(b, s_d, 5 * d + step))
                act.activation(buf, buf, ACT.Exp, scale=sign).then_inc(s_ex[0], 1)

            def wkv_quotient(b, d):
                eng.wait_ge(s_nd[0], upto(b, s_nd, 7 * d + 6))
                act.activation(EB[:, 0, :], EB[:, 1, :], ACT.Ln).then_inc(s_y[0], 1)
                eng.wait_ge(s_nd[0], upto(b, s_nd, 7 * d + 7))
                act.activation(EB[:, 0, :], EB[:, 0, :], ACT.Exp).then_inc(s_y[0], 1)

            def norm2(b):
                use, bank = ring(b, MLP_FROM + 4)
                for c in range(CH):
                    for q in range(NQ):
                        src = bank()
                        act.activation(XN[:, c, 1 + TQ * q:1 + TQ * q + TQ], src, ACT.Identity,
                                       scale=vec("ln2_g", c), bias=vec("ln2_b", c)).then_inc(s_xn2T[0], 1)

            def ffn_gate(b, q):
                use, bank = ring(b, FFN_FROM + 12 * q)
                LG = EB[:, :, :].rearrange("p c t -> p (c t)")[:, 2 * TQ * q:2 * TQ * q + 2 * TQ]
                eng.wait_ge(s_mk2[0], upto(b, s_mk2, 2))
                for i in range(2):
                    src = bank()
                    act.activation(LG[:, TQ * i:TQ * i + TQ], src, ACT.Copy).then_inc(s_r2[0], 1)

            def ffn(b, q):
                use, bank = ring(b, FFN_FROM + 12 * q + 2)
                LG = EB[:, :, :].rearrange("p c t -> p (c t)")[:, 2 * TQ * q:2 * TQ * q + 2 * TQ]
                eng.wait_ge(s_r2[0], upto(b, s_r2, 2 * q + 2))
                eng.wait_ge(s_x3[0], upto(b, s_x3, 2 * q))
                act.activation(EE[:, :], LG, ACT.Abs).then_inc(s_r2e[0], 1)
                eng.wait_ge(s_r2e[0], upto(b, s_r2e, 4 * q + 1))
                act.activation(EE[:, :], EE[:, :], ACT.Exp, scale=-1.0).then_inc(s_r2e[0], 1)
                eng.wait_ge(s_r2e[0], upto(b, s_r2e, 4 * q + 2))
                act.activation(EE[:, :], EE[:, :], ACT.Ln, bias=1.0).then_inc(s_r2e[0], 1)
                for f in range(NF):
                    src = bank()
                    n = NF * q + f
                    tmp = V2[:, TQ * (f % 2):TQ * (f % 2) + TQ]
                    eng.wait_ge(s_hid[0], upto(b, s_hid, n))
                    act.activation(tmp, src, ACT.Relu).then_inc(s_relu[0], 1)
                    eng.wait_ge(s_relu[0], upto(b, s_relu, n + 1))
                    act.activation(HID[:, f, :], tmp, ACT.Square).then_inc(s_hid[0], 1)
                    if f == 1:
                        eng.wait_ge(s_g2[0], upto(b, s_g2, q + 1))
                        act.activation(EE[:, :], EE[:, :], ACT.Exp).then_inc(s_r2e[0], 1)

            def gate(b):
                use, bank = ring(b, s_pa[1] - 2)
                eng.wait_ge(s_z[0], upto(b, s_z, NT))
                act.activation(ZE[:, :], ZC[:, :], ACT.Exp, scale=-1.0).then_inc(s_ze[0], 1)
                for q in range(2):
                    src = bank()
                    act.activation(EB[:, 0, TQ * q:TQ * q + TQ], src, ACT.Copy).then_inc(s_grow[0], 1)

            def pair(b, u):
                eng.wait_ge(s_pc[0], upto(b, s_pc, u + 1))
                return PC[:, u % 2, :, :]

            def kept(b):
                src = pair(b, 0)
                eng.wait_ge(s_mw[0], upto(b, s_mw, 0))
                act.activation(AT[:, :, :], src, ACT.Copy).then_inc(s_at[0], 1)
                for i in range(2):
                    src = pair(b, 1 + i)
                    eng.wait_ge(s_qw[0], upto(b, s_qw, 32 * i))
                    eng.wait_ge(s_fin[0], upto(b, s_fin, 0))
                    act.activation(QHL[:, 0, :, :], src, ACT.Copy).then_inc(s_qh[0], 1)
                src = pair(b, 3)
                act.activation(VV[:, :, :, 0:DH],
                               src.rearrange("p a (t h d) -> p (a t) h d", t=2, d=DH), ACT.Copy).then_inc(s_vv[0], 1)

            def maxima_rows(b):
                src = pair(b, EXP_FROM - 1)
                act.activation(MHL[:, 0, :], src[0:H, 0, :], ACT.Copy).then_inc(s_mh[0], 1)

            def exps(b, step):
                for n in range(2):
                    src = pair(b, EXP_FROM + 2 * step + n)
                    eng.wait_ge(s_pv[0], upto(b, s_pv, step))
                    if step == 0:
                        eng.wait_ge(s_qw[0], upto(b, s_qw, 64))
                    act.activation(PR[:, n, :, :], src, ACT.Exp, scale=0.25).then_inc(s_p[0], 1)
                g, t = divmod(step, KT)
                if t == 0 and g > 0:
                    heads_out(b, g - 1)

            def attention_out(b):
                src = pair(b, SUMS_FROM + 4)
                act.activation(SEL[:, :, :], src.rearrange("p a (t c) -> p (a t) c", t=2), ACT.Copy)\
                   .then_inc(s_o[0], 1)

            def heads_out(b, g):
                eng.wait_ge(s_pv[0], upto(b, s_pv, KT * (g + 1)))
                act.activation(OT[:, g, :], PO[:, :], ACT.Copy).then_inc(s_oT[0], 1)

            def iteration(b, a):
                if b:
                    pooling(b)
                if a:
                    kept(a)
                if b:
                    norm(b)
                    project(b)
                if a:
                    maxima_rows(a)
                for step in range(NG * KT):
                    if b:
                        if step in (0, 6):
                            r_exp(b, step // 6)
                        if step in (0, 1, 6, 7):
                            for i in range(2):
                                wkv_exp(b, step // 6, 2 * (step % 6) + i)
                        if step in (4, 10):
                            wkv_quotient(b, step // 6)
                    if a:
                        exps(a, step)
                if a:
                    heads_out(a, NG - 1)
                if b:
                    norm2(b)
                    ffn_gate(b, 0)
                if a:
                    attention_out(a)
                if b:
                    ffn(b, 0)
                    ffn_gate(b, 1)
                    ffn(b, 1)
                    gate(b)

            eng.wait_ge(s_w[0], ALL_LOADED + 16)
            act.activation(DEC[:, :], VEC[:, VECTORS.index("decay"), :], ACT.Exp).then_inc(s_dec[0], 1)
            every_batch(iteration, eng)

        @block.vector
        def _(eng):
            def stats(b, src, need, per, st, mv, tiles=range(NT)):
                first, n = tiles[0], len(tiles)
                for t in tiles:
                    eng.wait_ge(need[0], upto(b, need, t // per + 1))
                    dve.bn_stats(STATS[:, t, :], src[:, t, :]).then_inc(st[0], 1)
                eng.wait_ge(st[0], upto(b, st, 2 * first + n))
                dve.memset(HOLD[:, 0:1], 0.0)
                for t in tiles:
                    dve.bn_aggr(mv[:, t, :], STATS[:, t, :]).then_inc(st[0], 1)

            def ring(b, first):
                use = [first]

                def bank(skip=0):
                    use[0] += skip
                    u = use[0]
                    use[0] += 1
                    eng.wait_ge(s_pa[0], upto(b, s_pa, u + 1))
                    return PA[:, u % 3, :]

                return use, bank

            def mixed(b, done, dst, name, c):
                dve.scalar_tensor_tensor(dst[:, c, :], EB[:, c, :], vec(name, c), XN[:, c, 0:T],
                                         ALU.mult, ALU.add).then_inc(done[0], 1)

            def pooling(b):
                use, bank = ring(b, 0)
                src = bank(6)
                dve.tensor_scalar(EN[:, :, 0], src[:, 0:NT], B2[:, :], None, ALU.add).then_inc(s_en[0], 1)
                eng.wait_ge(s_en[0], upto(b, s_en, 1))
                dve.tensor_reduce(ENM[:, :], EN[:, :, :], AX.X, ALU.max).then_inc(s_en[0], 1)
                eng.wait_ge(s_en[0], upto(b, s_en, 2))
                dve.tensor_tensor(END[:, :], EN[:, :, 0], ENM[:, :], ALU.subtract).then_inc(s_en[0], 1)
                eng.wait_ge(s_ee[0], upto(b, s_ee, 1))
                dve.tensor_reduce(ENS[:, :], ENE[:, :, :], AX.X, ALU.add).then_inc(s_pw[0], 1)
                eng.wait_ge(s_pw[0], upto(b, s_pw, 1))
                dve.reciprocal(ENR[:, :], ENS[:, :]).then_inc(s_pw[0], 1)
                eng.wait_ge(s_pw[0], upto(b, s_pw, 2))
                dve.tensor_tensor(PW[:, :], ENE[:, :, 0], ENR[:, :], ALU.mult).then_inc(s_pw[0], 1)
                eng.wait_ge(s_pw[0], upto(b, s_pw, 3))
                eng.wait_ge(s_x[0], upto(b, s_x, 16))
                for t in range(NT):
                    dve.tensor_scalar(HX[:, t, :], XIN[:, t, :], PW[:, t:t + 1], None, ALU.mult).then_inc(s_h[0], 1)
                stats(b, HX, s_h, 1, s_st, MV)
                eng.wait_ge(s_st[0], upto(b, s_st, 2 * NT))
                dve.tensor_scalar(VE[:, 0:NT], MV[:, :, 1], EPS, None, ALU.add).then_inc(s_ve[0], 1)
                eng.wait_ge(s_ve[0], upto(b, s_ve, 1))
                dve.reciprocal(SCR[:, :], VE[:, 0:NT]).then_inc(s_ve[0], 1)
                eng.wait_ge(s_ve[0], upto(b, s_ve, 2))
                dve.tensor_tensor(VE[:, NT:2 * NT], MV[:, :, 1], SCR[:, :], ALU.mult).then_inc(s_ve[0], 1)
                eng.wait_ge(s_ve[0], upto(b, s_ve, 3))
                dve.tensor_scalar(VE[:, NT:2 * NT], VE[:, NT:2 * NT], EPS, None, ALU.add).then_inc(s_ve[0], 1)
                eng.wait_ge(s_rs[0], upto(b, s_rs, 1))
                dve.tensor_tensor(SCR[:, :], RS[:, 0:NT], RS[:, NT:2 * NT], ALU.mult).then_inc(s_sc[0], 1)
                eng.wait_ge(s_sc[0], upto(b, s_sc, 1))
                eng.wait_ge(s_scat[0], upto(b, s_scat, 0))
                for t in range(NT):
                    dve.tensor_scalar(KBT[:, t, :], HX[:, t, :], MV[:, t, 0:1], SCR[:, t:t + 1],
                                      ALU.subtract, ALU.mult).then_inc(s_xn[0], 1)
                for t in range(NT):
                    dve.tensor_scalar(XA[:, t, :], HX[:, t, :], MV[:, t, 0:1], RS[:, t:t + 1],
                                      ALU.subtract, ALU.mult).then_inc(s_xa[0], 1)

            def mix(b):
                for c in range(CH):
                    eng.wait_ge(s_xnT[0], upto(b, s_xnT, 2 * c + 2))
                    dve.tensor_tensor(EB[:, c, :], XN[:, c, 1:T + 1], XN[:, c, 0:T], ALU.subtract)\
                       .then_inc(s_dx[0], 1)
                for c in range(CH):
                    eng.wait_ge(s_dx[0], upto(b, s_dx, c + 1))
                    mixed(b, s_mk, MA, "mix_k", c)
                for c in range(CH):
                    mixed(b, s_mv, MB, "mix_v", c)

            def mix_r(b):
                eng.wait_ge(s_k[0], upto(b, s_k, 4))
                for c in range(CH):
                    mixed(b, s_mr, MA, "mix_r", c)

            def wkv(b):
                for d in range(CH):
                    k, v, r = KB[:, d, :], VR[:, 0, d, :], VR[:, 1, d, :]
                    before, now = PP[:, 0:T], PP[:, 1:T + 1]
                    e1b, e2b = EB[:, 0, :], EB[:, 1, :]
                    AA, BB = XN[:, 0, :], XN[:, 1, :]
                    D, N = 5 * d, 7 * d

                    def exp_arg(i):
                        return upto(b, s_d, D + i)

                    eng.wait_ge(s_k[0], upto(b, s_k, 4))
                    dve.tensor_tensor_scan(now, DECN[:, d:d + 1].broadcast_to([P, T]), k, NEG, ALU.add, ALU.max)\
                       .then_inc(s_pp[0], 1)
                    eng.wait_ge(s_pp[0], upto(b, s_pp, d + 1))
                    eng.wait_ge(s_mr[0], upto(b, s_mr, 2))
                    eng.wait_ge(s_rw[0], upto(b, s_rw, d))
                    dve.scalar_tensor_tensor(e1b, before, DECN[:, d:d + 1], now, ALU.add, ALU.subtract)\
                       .then_inc(s_d[0], 1)
                    dve.tensor_tensor(e2b, k, now, ALU.subtract).then_inc(s_d[0], 1)
                    eng.wait_ge(s_v[0], upto(b, s_v, 4))
                    dve.scalar_tensor_tensor(E2, k, vec("first", d), before, ALU.add, ALU.subtract)\
                       .then_inc(s_d[0], 1)
                    eng.wait_ge(s_d[0], exp_arg(3))
                    dve.tensor_scalar(E1, E2, 0.0, None, ALU.max).then_inc(s_d[0], 1)
                    dve.tensor_scalar(E2, E2, 0.0, None, ALU.min).then_inc(s_d[0], 1)
                    eng.wait_ge(s_r[0], upto(b, s_r, 4))
                    eng.wait_ge(s_er[0], upto(b, s_er, 2 * d + 1))
                    dve.tensor_scalar(r, r, 0.0, None, ALU.min).then_inc(s_rm[0], 1)
                    eng.wait_ge(s_ex[0], upto(b, s_ex, 4 * d + 2))
                    dve.tensor_tensor(V2[:, :], e2b, v, ALU.mult).then_inc(s_ev[0], 1)
                    dve.tensor_tensor_scan(BB[:, 1:T + 1], e1b, e2b, 0.0, ALU.mult, ALU.add).then_inc(s_ab[0], 1)
                    eng.wait_ge(s_ev[0], upto(b, s_ev, d + 1))
                    dve.tensor_tensor_scan(AA[:, 1:T + 1], e1b, V2[:, :], 0.0, ALU.mult, ALU.add)\
                       .then_inc(s_ab[0], 1)
                    eng.wait_ge(s_ex[0], upto(b, s_ex, 4 * d + 4))
                    eng.wait_ge(s_ab[0], upto(b, s_ab, 2 * d + 1))
                    dve.tensor_tensor(e2b, E1, BB[:, 0:T], ALU.mult).then_inc(s_nd[0], 1)
                    eng.wait_ge(s_ab[0], upto(b, s_ab, 2 * d + 2))
                    dve.tensor_tensor(V2[:, :], E1, AA[:, 0:T], ALU.mult).then_inc(s_nd[0], 1)
                    eng.wait_ge(s_nd[0], upto(b, s_nd, N + 1))
                    dve.tensor_tensor(e2b, e2b, E2, ALU.add).then_inc(s_nd[0], 1)
                    eng.wait_ge(s_nd[0], upto(b, s_nd, N + 2))
                    dve.tensor_tensor(E1, E2, v, ALU.mult).then_inc(s_nd[0], 1)
                    eng.wait_ge(s_nd[0], upto(b, s_nd, N + 4))
                    dve.tensor_tensor(V2[:, :], V2[:, :], E1, ALU.add).then_inc(s_nd[0], 1)
                    eng.wait_ge(s_er[0], upto(b, s_er, 2 * d + 2))
                    dve.scalar_tensor_tensor(e2b, EE[:, :], 1.0, e2b, ALU.add, ALU.mult).then_inc(s_nd[0], 1)
                    eng.wait_ge(s_y[0], upto(b, s_y, 2 * d + 1))
                    dve.tensor_tensor(e1b, r, e1b, ALU.subtract).then_inc(s_nd[0], 1)
                    eng.wait_ge(s_y[0], upto(b, s_y, 2 * d + 2))
                    dve.tensor_tensor(KB[:, d, :], V2[:, :], e1b, ALU.mult).then_inc(s_rw[0], 1)

            def norm2(b):
                use, bank = ring(b, MLP_FROM)
                for i in range(4):
                    src = bank()
                    pair = XA[:, 2 * i:2 * i + 2, :].rearrange("p t c -> p (t c)")
                    if i == 0:
                        eng.wait_ge(s_xa[0], upto(b, s_xa, NT))
                    dve.tensor_tensor(pair, pair, src, ALU.add).then_inc(s_x2[0], 1)
                stats(b, XA, s_x2, 2, s_st2, MV2)
                eng.wait_ge(s_st2[0], upto(b, s_st2, 2 * NT))
                dve.tensor_scalar(VE2[:, :], MV2[:, :, 1], EPS, None, ALU.add).then_inc(s_ve2[0], 1)
                eng.wait_ge(s_rs2[0], upto(b, s_rs2, 1))
                for t in range(NT):
                    dve.tensor_scalar(VT[:, t, :], XA[:, t, :], MV2[:, t, 0:1], RS2[:, t:t + 1],
                                      ALU.subtract, ALU.mult).then_inc(s_xn2[0], 1)

            def mix2(b):
                for c in range(CH):
                    eng.wait_ge(s_xn2T[0], upto(b, s_xn2T, 2 * c + 2))
                    dve.tensor_tensor(EB[:, c, :], XN[:, c, 1:T + 1], XN[:, c, 0:T], ALU.subtract)\
                       .then_inc(s_dx2[0], 1)
                for c in range(CH):
                    eng.wait_ge(s_dx2[0], upto(b, s_dx2, c + 1))
                    mixed(b, s_mr2, MB, "ffn_mix_r", c)
                for c in range(CH):
                    mixed(b, s_mk2, MA, "ffn_mix_k", c)

            def ffn_gate(b, q):
                LG = EB[:, :, :].rearrange("p c t -> p (c t)")[:, 2 * TQ * q:2 * TQ * q + 2 * TQ]
                eng.wait_ge(s_r2e[0], upto(b, s_r2e, 4 * q + 3))
                dve.scalar_tensor_tensor(EE[:, :], LG, 0.0, EE[:, :], ALU.min, ALU.subtract)\
                   .then_inc(s_g2[0], 1)

            def ffn(b, q):
                use, bank = ring(b, FFN_FROM + 12 * q + 10)
                for i in range(2):
                    src = bank()
                    n = 2 * q + i
                    two = (slice(None), slice(2 * n, 2 * n + 2), slice(None))
                    flat = lambda z: z[two].rearrange("p t c -> p (t c)")
                    eng.wait_ge(s_r2e[0], upto(b, s_r2e, 4 * q + 4))
                    dve.tensor_tensor(EE[:, TQ * i:TQ * i + TQ], EE[:, TQ * i:TQ * i + TQ], src, ALU.mult)\
                       .then_inc(s_sk[0], 1)
                    eng.wait_ge(s_sk[0], upto(b, s_sk, n + 1))
                    dve.tensor_tensor(flat(XA), flat(XA), EE[:, TQ * i:TQ * i + TQ], ALU.add)\
                       .then_inc(s_x3[0], 1)
                    eng.wait_ge(s_x3[0], upto(b, s_x3, n + 1))
                    if n == 0:
                        eng.wait_ge(s_out[0], upto(b, s_out, 0))
                    dve.tensor_tensor(flat(H2), flat(HX), flat(XA), ALU.add).then_inc(s_h2[0], 1)

            def router(b, q):
                tiles = range(NT // NQ * q, NT // NQ * (q + 1))
                lo, hi = tiles[0], tiles[-1] + 1
                stats(b, H2, s_h2, 2, s_st3, MV3, tiles)
                eng.wait_ge(s_st3[0], upto(b, s_st3, 2 * hi))
                dve.tensor_scalar(VE3[:, lo:hi], MV3[:, lo:hi, 1], EPS, None, ALU.add).then_inc(s_ve3[0], 1)
                eng.wait_ge(s_rs3[0], upto(b, s_rs3, q + 1))
                for t in tiles:
                    dve.tensor_scalar(KBT[:, t, :], H2[:, t, :], MV3[:, t, 0:1], RS3[:, t:t + 1],
                                      ALU.subtract, ALU.mult).then_inc(s_ti[0], 1)
                for t in tiles:
                    eng.wait_ge(s_ti[0], upto(b, s_ti, t + 1))
                    if t:
                        eng.wait_ge(s_z[0], upto(b, s_z, t))
                    dve.tensor_tensor_reduce(out=EB[:, 0, 0:C], in0=KBT[:, t, :], in1=WG[:, :], scale=1.0, scalar=0.0,
                                             op0=ALU.mult, op1=ALU.add, accum_out=ZC[:, t:t + 1]).then_inc(s_z[0], 1)

            def rank(b):
                eng.wait_ge(s_ze[0], upto(b, s_ze, 1))
                dve.tensor_scalar(ZP[:, :], ZE[:, :], 1.0, None, ALU.add).then_inc(s_g[0], 1)
                eng.wait_ge(s_g[0], upto(b, s_g, 1))
                dve.reciprocal(GC[:, :], ZP[:, :]).then_inc(s_g[0], 1)
                eng.wait_ge(s_g[0], upto(b, s_g, 2))
                eng.wait_ge(s_fin[0], upto(b, s_fin, 0))
                dve.tensor_copy(G2[:, :], GC[:, :]).then_inc(s_g[0], 1)
                eng.wait_ge(s_grow[0], upto(b, s_grow, 2))
                rows, waste = EB[:, 0, :], EB[:, 1, :]
                for t in range(NT):
                    own = GC[:, t:t + 1]
                    eng.wait_ge(s_cnt[0], upto(b, s_cnt, 3 * t))
                    dve.tensor_scalar(waste[:, P * t:T], rows[:, P * t:T], own, None, ALU.is_gt, ALU.add,
                                      accum_out=CNT[:, t, 0:1]).then_inc(s_cnt[0], 1)
                    if t:
                        dve.tensor_scalar(waste[:, 0:P * t], rows[:, 0:P * t], own, None, ALU.is_ge, ALU.add,
                                          accum_out=CNT[:, t, 1:2]).then_inc(s_cnt[0], 1)
                    else:
                        dve.memset(CNT[:, t, 1:2], 0.0).then_inc(s_cnt[0], 1)
                    dve.scalar_tensor_tensor(V2[:, P * t:P * t + P], rows[:, P * t:P * t + P], own, LOW[:, :],
                                             ALU.is_equal, ALU.mult, accum_out=CNT[:, t, 2:3]).then_inc(s_cnt[0], 1)
                eng.wait_ge(s_cnt[0], upto(b, s_cnt, 3 * NT))
                dve.tensor_reduce(RANKF[:, :], CNT[:, :, :], AX.X, ALU.add).then_inc(s_rank[0], 1)
                eng.wait_ge(s_rank[0], upto(b, s_rank, 1))
                eng.wait_ge(s_gath[0], upto(b, s_gath, 0))
                dve.tensor_copy(RANK[:, :], RANKF[:, :]).then_inc(s_rank[0], 1)

            def pair(b, u):
                eng.wait_ge(s_pc[0], upto(b, s_pc, u + 1))
                return PC[:, u % 2, :, :]

            def qk_low(b):
                for i in range(2):
                    src = pair(b, 1 + i)
                    eng.wait_ge(s_qh[0], upto(b, s_qh, i + 1))
                    eng.wait_ge(s_qw[0], upto(b, s_qw, 32 * i))
                    dve.tensor_tensor(QHL[:, 1, :, :], src, QHL[:, 0, :, :].bitcast(F32), ALU.subtract)\
                       .then_inc(s_ql[0], 1)

            def maxima(b, h):
                for n in range(2):
                    src = pair(b, MAX_FROM + 2 * h + n)
                    dve.tensor_reduce(NM[:, 2 * n:2 * n + 2, h], src, AX.X, ALU.max, negate=True)\
                       .then_inc(s_nm[0], 1)

            def max_low(b):
                src = pair(b, EXP_FROM - 1)
                eng.wait_ge(s_mh[0], upto(b, s_mh, 1))
                dve.tensor_tensor(MHL[:, 1, :], src[0:H, 0, :], MHL[:, 0, :].bitcast(F32), ALU.subtract)\
                   .then_inc(s_ml[0], 1)

            def inverse_sums(b):
                for n in range(2):
                    src = pair(b, SUMS_FROM + n)
                    sums = src.rearrange("p g (t i w) -> p g t i w", t=KT, i=4)[:, :, :, :, DH]
                    dve.reciprocal(RSUM[:, 2 * n:2 * n + 2, :, :].rearrange("p g t i -> p (g t) i"),
                                   sums.rearrange("p g t i -> p (g t) i")).then_inc(s_rsum[0], 1)
                for n in range(2):
                    eng.wait_ge(s_rsum[0], upto(b, s_rsum, n + 1))
                    dve.tensor_copy(RWIDE[n].rearrange("p g t (i w) -> p (g t i) w", w=32),
                                    RSUM[:, 2 * n:2 * n + 2, :, :].rearrange("p g t i -> p (g t i)")
                                    .unsqueeze(2).broadcast_to([P, 32, 32])).then_inc(s_rw2[0], 1)

            def normalise(b):
                for n in range(2):
                    src = pair(b, SUMS_FROM + 2 + n)
                    dve.tensor_tensor(OT[:, 2 * n:2 * n + 2, :], OT[:, 2 * n:2 * n + 2, :], src, ALU.mult)\
                       .then_inc(s_on[0], 1)

            def finish(b):
                eng.wait_ge(s_gath[0], upto(b, s_gath, 16 * NT))
                for t in range(NT):
                    dve.scalar_tensor_tensor(H2[:, t, :], GA[:, t, :], G2[:, t:t + 1], H2[:, t, :],
                                             ALU.mult, ALU.add).then_inc(s_fin[0], 1)

            def iteration(b, a):
                if b:
                    pooling(b)
                if a:
                    qk_low(a)
                if b:
                    mix(b)
                for h in range(H):
                    if a:
                        maxima(a, h)
                    if b and h == 1:
                        mix_r(b)
                if a:
                    max_low(a)
                if b:
                    wkv(b)
                    norm2(b)
                if a:
                    inverse_sums(a)
                if b:
                    mix2(b)
                if a:
                    normalise(a)
                if b:
                    ffn_gate(b, 0)
                if a:
                    finish(a)
                if b:
                    ffn(b, 0)
                    ffn_gate(b, 1)
                    router(b, 0)
                    ffn(b, 1)
                    router(b, 1)
                    rank(b)

            eng.wait_ge(s_w[0], ALL_LOADED + 16)
            eng.wait_ge(s_const[0], 7)
            eng.wait_ge(s_dec[0], 1)
            dve.tensor_scalar(DECN[:, :], DEC[:, :], -1.0, None, ALU.mult).then_inc(s_decn[0], 1)
            eng.wait_ge(s_decn[0], 1)
            every_batch(iteration, eng)


_ORDER = ["x", "vectors", "tok_w1", "tok_b1", "tok_w2", "tok_b2", "w_k", "w_v", "w_r", "w_o", "w_kf", "w_rf",
          "w_vf", "gate_w", "w_q2", "w_k2", "w_v2", "w_o2", "identity", "lower"]


def kernel(**inputs):
    import concourse.bacc as bacc
    from concourse.bass_utils import run_bass_kernel_spmd

    a = {k: np.asarray(v) for k, v in inputs.items()}

    def rows(w):
        return np.ascontiguousarray(w.reshape(-1, P, w.shape[1]).transpose(1, 0, 2))

    by_name = {
        "ln1_g": "L0_attn_ln1_g", "ln1_b": "L0_attn_ln1_b", "ln2_g": "L0_attn_ln2_g", "ln2_b": "L0_attn_ln2_b",
        "mix_k": "L0_attn_att_mix_k", "mix_v": "L0_attn_att_mix_v", "mix_r": "L0_attn_att_mix_r",
        "decay": "L0_attn_time_decay", "first": "L0_attn_time_first",
        "ffn_mix_k": "L0_attn_ffn_mix_k", "ffn_mix_r": "L0_attn_ffn_mix_r",
    }
    vectors = np.stack([a[by_name[n]].reshape(CH, P) for n in VECTORS]).transpose(2, 0, 1)
    w_o2 = np.zeros((NG, 4, 32, C), np.float32)
    w_o2[:, :, :DH] = a["L0_ffn_Wo"].reshape(NG, 4, DH, C)
    arrays = {
        "x": a["x"].reshape(B * T, C),
        "vectors": np.ascontiguousarray(vectors),
        "tok_w1": rows(a["L0_tok_W1"]),
        "tok_b1": a["L0_tok_b1"].reshape(P, 1),
        "tok_w2": a["L0_tok_W2"].reshape(P, 1),
        "tok_b2": np.ascontiguousarray(np.broadcast_to(a["L0_tok_b2"].reshape(1, 1), (P, 1))),
        "w_k": rows(a["L0_attn_Wk"].T), "w_v": rows(a["L0_attn_Wv"].T), "w_r": rows(a["L0_attn_Wr"].T),
        "w_o": rows(a["L0_attn_Wo"].T), "w_kf": rows(a["L0_attn_Wk_ffn"].T),
        "w_rf": rows(a["L0_attn_Wr_ffn"].T), "w_vf": rows(a["L0_attn_Wv_ffn"].T),
        "gate_w": np.ascontiguousarray(np.broadcast_to(a["L0_ffn_Wg"].reshape(1, C), (P, C))),
        "w_q2": rows(a["L0_ffn_Wq"]), "w_k2": rows(a["L0_ffn_Wk"]), "w_v2": rows(a["L0_ffn_Wv"]),
        "w_o2": np.ascontiguousarray(w_o2.reshape(NG, P, C).transpose(1, 0, 2)),
        "identity": np.eye(P, dtype=np.float32),
        "lower": np.tril(np.ones((P, P), np.float32), -1),
    }
    nc = bacc.Bacc("TRN2", target_bir_lowering=False, num_devices=1)
    args = [nc.dram_tensor(f"in_{n}", arrays[n].shape, mybir.dt.from_np(arrays[n].dtype),
                           kind="ExternalInput").ap() for n in _ORDER]
    result = nc.dram_tensor("out_tokens", (B * T, C), F32, kind="ExternalOutput").ap()
    vit_tower(nc, *args, result)
    r = run_bass_kernel_spmd(nc, [{f"in_{n}": arrays[n] for n in _ORDER}], core_ids=[0])
    return r.results[0]["out_tokens"].reshape(B, T, C)
```

```python
from contextlib import ExitStack

import numpy as np

import concourse.bass as bass
from concourse import mybir

F32 = mybir.dt.float32
F32R = mybir.dt.float32r
U32 = mybir.dt.uint32
ALU = mybir.AluOpType
ACT = mybir.ActivationFunctionType
AX = mybir.AxisListType

P = 128
B, T, C = 4, 1024, 256
NT = T // P
CH = C // P
TQ = 512
NQ = T // TQ
FFN = 1024
NF = FFN // P
H, DH = 16, 16
CAP = T // 2
KT = CAP // P
NG = 4
EPS = 1e-5
NEG = -1e38

VECTORS = ["ln1_g", "ln1_b", "ln2_g", "ln2_b", "mix_k", "mix_v", "mix_r",
           "decay", "first", "ffn_mix_k", "ffn_mix_r"]


BESIDE = {0: (8, 9), 1: (10, 11), 2: (12, 13), 3: (14, 15)}
EARLY = 3
R_BESIDE = (0, 2, 4, 6)
ROWS_STEP = 4
WO_STEP = 10


class Lap:

    def __init__(self, plus, register=None):
        self.plus, self.register = plus, register

    def times(self, per, k=0):
        fixed = self.plus * per + k
        return fixed if self.register is None else self.register * per + fixed


def every_batch(first_norm, iteration, eng):
    first_norm(Lap(0))
    iteration(Lap(0), None, Lap(1))
    with eng.Fori(0, B - 2) as i:
        iteration(Lap(1, i), Lap(0, i), Lap(2, i))
    iteration(Lap(B - 1), Lap(B - 2), None)
    iteration(None, Lap(B - 1), None)


def vit_tower(nc, x, vectors, tok_w1, tok_b1, tok_w2, tok_b2, w_k, w_v, w_r, w_o,
              w_kf, w_rf, w_vf, gate_w, w_q2, w_k2, w_v2, w_o2, identity, lower, out):
    nc.disable_value_cache = True
    ctx = ExitStack()
    with ctx:
        def sb(name, shape, dt=F32):
            return ctx.enter_context(nc.sbuf_tensor(name, shape, dt))

        per_batch = {}

        def sem(name, per):
            s = ctx.enter_context(nc.semaphore(name))
            per_batch[name] = per
            return (s, per)

        def upto(b, signal, k):
            return b.times(signal[1], k)

        W1 = sb("W1", [P, CH, P])
        W2 = sb("W2", [P, 1])
        B1 = sb("B1", [P, 1])
        B2 = sb("B2", [P, 1])
        WK = sb("WK", [P, CH, C])
        WV = sb("WV", [P, CH, C])
        WR = sb("WR", [P, CH, C])
        WO = sb("WO", [P, CH, C])
        WKF = sb("WKF", [P, CH, FFN])
        WRF = sb("WRF", [P, CH, C])
        WVF = sb("WVF", [P, NF, C])
        WG = sb("WG", [P, C])
        WQ2 = sb("WQ2", [P, CH, C])
        WK2 = sb("WK2", [P, CH, C])
        WV2 = sb("WV2", [P, CH, C])
        WO2 = sb("WO2", [P, NG, C])
        VEC = sb("VEC", [P, len(VECTORS), CH])
        IDN = sb("IDN", [P, P])
        LOW = sb("LOW", [P, P])

        def vec(name, c):
            i = VECTORS.index(name)
            return VEC[:, i, c:c + 1]

        with nc.sbuf_tensor("FIRST_STACKS", [P, H // 2, CAP], F32), nc.sbuf_tensor("XIN", [P, NT, C], F32) as XIN, \
                nc.sbuf_tensor("MA", [P, CH, T], F32) as MA:
            pass
        KS = sb("KS", [P, H, CAP], F32R)

        HX = sb("HX", [P, NT, C])
        XA = sb("XA", [P, NT, C])
        XN = sb("XN", [P, CH, T + 1])
        MB = sb("MB", [P, CH, T])
        KB = sb("KB", [P, CH, T])
        VR = sb("VR", [P, 2, CH, T])
        PP = sb("PP", [P, T + 1])
        EB = sb("EB", [P, CH, T])
        V2 = sb("V2", [P, T])
        EE = sb("EE", [P, T])
        DEC = sb("DEC", [P, CH])
        DECN = sb("DECN", [P, CH])
        STATS = sb("STATS", [P, NT, 6])
        MV = sb("MV", [P, NT, 2])
        MV2 = sb("MV2", [P, NT, 2])
        MV3 = sb("MV3", [P, NT, 2])
        VE = sb("VE", [P, 2 * NT])
        RS = sb("RS", [P, 2 * NT])
        VE2 = sb("VE2", [P, NT])
        RS2 = sb("RS2", [P, NT])
        VE3 = sb("VE3", [P, NT])
        RS3 = sb("RS3", [P, NT])
        HALF = sb("HALF", [P, 2 * NT])
        HOLD = sb("HOLD", [P, 8])
        SCR = sb("SCR", [P, NT])
        EN = sb("EN", [P, NT, 1])
        ENM = sb("ENM", [P, NT])
        END = sb("END", [P, NT])
        ENE = sb("ENE", [P, NT, 1])
        ENS = sb("ENS", [P, NT])
        ENR = sb("ENR", [P, NT])
        PW = sb("PW", [P, NT])
        ZC = sb("ZC", [P, NT])
        ZE = sb("ZE", [P, NT])
        ZP = sb("ZP", [P, NT])
        GC = sb("GC", [P, NT])
        CNT = sb("CNT", [P, NT, 3])
        RANKF = sb("RANKF", [P, NT])
        H2 = sb("H2", [P, NT, C])
        G2 = sb("G2", [P, NT])
        RANK = sb("RANK", [P, NT], U32)
        SEL = sb("SEL", [P, KT, C])
        AT = sb("AT", [P, CH, CAP])
        QS = sb("QS", [P, H // 2, CAP], F32R)
        VV = sb("VV", [P, KT, H, 32])
        PR = sb("PR", [P, 2, 2, CAP])
        OT = sb("OT", [P, NG, CAP])
        NM = sb("NM", [P, KT, H])
        RSUM = sb("RSUM", [P, NG, KT, 4])

        HID = VR[:, :, :, :].rearrange("p a c t -> p (a c t)").rearrange("p (f t) -> p f t", t=TQ)
        KBT = KB[:, :, :].rearrange("p a t -> p (a t)").rearrange("p (t c) -> p t c", c=C)
        VT = VR[:, 0, :, :].rearrange("p a t -> p (a t)").rearrange("p (t c) -> p t c", c=C)
        E1, E2 = MB[:, 0, :], MB[:, 1, :]
        XT = XN[:, :, 1:T + 1]
        HT = MB[:, 0, :]
        GROWS = EE
        SLOTS = [PR[:, 0, :, :], PR[:, 1, :, :], AT[:, :, :],
                 SEL[:, :, :].rearrange("p t c -> p (t c)").rearrange("p (i n) -> p i n", n=CAP)]
        MHL = OT[0:H // 2, 2:4, :].bitcast(F32R)
        RWIDE = [z[:, :, :].rearrange("p a n -> p (a n)").rearrange("p (g t w) -> p g t w", g=2, t=KT)
                 for z in (AT, SEL)]
        GA = PR[:, :, :, :].rearrange("p a i n -> p (a i n)").rearrange("p (t c) -> p t c", c=C)
        QHL = [PR[:, :, :, :].bitcast(F32R),
               OT[:, :, :].rearrange("p (a i) n -> p a i n", a=2).bitcast(F32R)]

        kept_d = nc.dram_tensor("kept_d", [CAP, C], F32, kind="Internal").ap()
        qk_d = nc.dram_tensor("qk_d", [4, C, CAP], F32, kind="Internal").ap()
        max_d = nc.dram_tensor("max_d", [2, H // 2, 2, CAP], F32, kind="Internal").ap()
        att_d = nc.dram_tensor("att_d", [T, C], F32, kind="Internal").ap()

        PA = ctx.enter_context(nc.psum_tensor("PA", [P, 3, TQ], F32))
        PC = ctx.enter_context(nc.psum_tensor("PC", [P, 2, 2, TQ], F32))
        PO = ctx.enter_context(nc.psum_tensor("PO", [P, TQ], F32))

        s_w0 = sem("first_weights_in", 0)
        s_w = sem("weights_in", 0)
        s_zero = sem("zeros_set", 0)
        s_room = sem("stacks_cleared", 0)
        s_const = sem("constants_set", 0)
        s_dec = sem("decay_ready", 0)
        s_decn = sem("w_ready", 0)
        s_x = sem("x_in", 16)
        s_pa = sem("bank_filled", 48)
        s_pp2 = sem("pooling_filled", 4)
        s_gf = sem("gate_rows_filled", 2)
        s_xT = sem("xT_out", 2)
        s_hT = sem("tanh_out", 1)
        s_ee = sem("energy_exp", 1)
        s_xnT = sem("xnT_out", 4)
        s_k = sem("k_out", 4)
        s_v = sem("v_out", 4)
        s_r = sem("r_out", 4)
        s_ex = sem("wkv_exp", 8)
        s_er = sem("r_exp", 4)
        s_y = sem("y_exp", 4)
        s_xn2T = sem("xn2T_out", 4)
        s_r2 = sem("r2_out", 4)
        s_r2e = sem("r2_exp", 8)
        s_relu = sem("relu_out", 16)
        s_hid = sem("hidden_out", 16)
        s_ze = sem("gate_exp", 1)
        s_grow = sem("gate_rows", 2)
        s_en = sem("energy", 3)
        s_pw = sem("pool_weights", 3)
        s_h = sem("pooled", 8)
        s_st = sem("norm_stats", 16)
        s_ve = sem("norm_var", 4)
        s_sc = sem("norm_scale", 1)
        s_xa = sem("xa", 8)
        s_xn = sem("xn", 8)
        s_dx = sem("token_diff", 2)
        s_mk = sem("mixed_k", 2)
        s_mv = sem("mixed_v", 2)
        s_mr = sem("mixed_r", 2)
        s_pp = sem("exponent", 2)
        s_d = sem("exp_args", 10)
        s_ev = sem("e2b_v", 2)
        s_ab = sem("scans", 4)
        s_nd = sem("num_den", 14)
        s_rw = sem("rwkv", 2)
        s_x2 = sem("x2", 4)
        s_st2 = sem("norm2_stats", 16)
        s_ve2 = sem("norm2_var", 1)
        s_xn2 = sem("xn2", 8)
        s_dx2 = sem("token_diff2", 2)
        s_mk2 = sem("mixed_k2", 2)
        s_mr2 = sem("mixed_r2", 2)
        s_g2 = sem("r2_arg", 2)
        s_sk = sem("gated_kv", 4)
        s_x3 = sem("x3", 4)
        s_h2 = sem("h2", 4)
        s_st3 = sem("norm3_stats", 16)
        s_ve3 = sem("norm3_var", 2)
        s_ti = sem("router_tokens", 8)
        s_z = sem("gate_logits", 8)
        s_g = sem("gates", 3)
        s_cnt = sem("counts", 24)
        s_rank = sem("ranks", 4)
        s_rs = sem("rstd", 1)
        s_rs2 = sem("rstd2", 1)
        s_rs3 = sem("rstd3", 2)
        s_scat = sem("kept_stored", 16 * NT)
        s_gath = [sem("gathered", 16 * KT), sem("later_gathered", 16 * KT)]
        s_sel = sem("kept_in", 16)
        s_pc = sem("pair_filled", 60)
        s_pm = sem("max_bank_filled", 33)
        s_pv = sem("values_done", 16)
        s_at = sem("aT_out", 1)
        s_qh = sem("qk_high", 2)
        s_ql = sem("qk_low", 2)
        s_qw = sem("q_stored", 32)
        s_kw = sem("k_stored", 32)
        s_xz = sem("x_room_cleared", 4)
        s_kz = sem("k_room_cleared", 4)
        s_qz = sem("max_rows_cleared", 32)
        s_qi = sem("q_stack_in", 16 * 6)
        s_ki = sem("k_stack_in", 16 * 6)
        s_vv = sem("v2_out", 2)
        s_nm = sem("maxima", 48)
        s_mh = sem("max_high", 2)
        s_ml = sem("max_low", 2)
        s_mw = sem("max_stored", 32)
        s_mi = sem("max_in", 64)
        s_p = sem("probs", 32)
        s_oT = sem("heads_out", 4)
        s_rsum = sem("sums_inverse", 2)
        s_rw2 = sem("inverse_spread", 2)
        s_on = sem("heads_norm", 2)
        s_o = sem("attention_out", 2)
        s_ow = sem("attention_stored", 16)
        s_fin = sem("result", 8)
        s_out = sem("out_stored", 32)

        emptied = ([(s_xnT, i + 1) for i in range(4)] + [(s_k, i + 1) for i in range(4)]
                   + [(s_v, i + 1) for i in range(4)] + [(s_r, i + 1) for i in range(4)]
                   + [(s_x2, i + 1) for i in range(4)] + [(s_xn2T, i + 1) for i in range(4)])
        for q in range(NQ):
            emptied += [(s_r2, 2 * q + i + 1) for i in range(2)]
            emptied += [(s_relu, NF * q + i + 1) for i in range(NF)]
            emptied += [(s_sk, 2 * q + i + 1) for i in range(2)]
        assert len(emptied) == s_pa[1] and len(emptied) % 3 == 0
        pairs = {"kept": (s_at, 1), "q": (s_ql, 1), "k": (s_ql, 2),
                 ("v", 0): (s_vv, 1), ("v", 1): (s_vv, 2)}
        for h in range(H // 2):
            pairs.update({("max", h, n): (s_nm, 2 * h + n + 1) for n in range(2)})
        pairs["rows", 0] = (s_ml, 1)
        for step in range(NG * KT):
            pairs.update({("exp", step, n): (s_p, 2 * step + n + 1) for n in range(2)})
        pairs.update({("sums", 0): (s_rsum, 1), ("sums", 1): (s_rsum, 2), ("inverse", 0): (s_on, 1),
                      ("inverse", 1): (s_on, 2), ("out", 0): (s_o, 1), ("out", 1): (s_o, 2)})
        pair_use = {name: u for u, name in enumerate(pairs)}
        emptied2 = list(pairs.values())
        assert len(emptied2) == s_pc[1] and len(emptied2) % 2 == 0

        emptied3 = [(s_nm, 16 + i + 1) for i in range(2 * H)] + [(s_ml, 2)]
        assert len(emptied3) == s_pm[1] and len(emptied3) % 3 == 0
        NORM_FROM, KVR_FROM, MLP_FROM, FFN_FROM = 0, 4, 16, 24
        block = ctx.enter_context(nc.Block())
        act, dve, pe, pool, sp = nc.scalar, nc.vector, nc.tensor, nc.gpsimd, nc.sync

        FIRST = [(IDN, identity), (W1, tok_w1), (B1, tok_b1), (W2, tok_w2), (B2, tok_b2), (VEC, vectors)]
        LOADS = [(WK, w_k), (WV, w_v), (WR, w_r), (WO, w_o), (WKF, w_kf), (WRF, w_rf), (WVF, w_vf),
                 (WG, gate_w), (LOW, lower), (WQ2, w_q2), (WK2, w_k2), (WV2, w_v2), (WO2, w_o2)]
        FIRST_LOADED = 16 * len(FIRST)
        ALL_LOADED = 16 * (len(LOADS) + 1)

        def restack(queue, eng, b, i, stored, stack, planes, carry=lambda cell: None):
            for part, done in ((0, s_qh), (1, s_ql)):
                eng.wait_ge(done[0], upto(b, done, i + 1))
                carry(part)
                queue.dma_start(qk_d[2 * i + part].rearrange("(c p) n -> p c n", p=P),
                                QHL[i][:, part, :, :].bitcast(F32)).then_inc(stored[0], 16)
            eng.wait_ge(stored[0], upto(b, stored, 32))
            carry(2)
            for row, plane in enumerate(planes):
                for odd in range(2):
                    at = 64 * odd + DH * row
                    heads = slice(odd, H, 2) if i else slice(None)
                    queue.dma_start(stack[at:at + DH, heads, :].bitcast(F32),
                                    qk_d[plane].rearrange("(j r d) n -> r d j n", r=2, d=DH)[odd])\
                         .then_inc((s_ki if i else s_qi)[0], 16)

        def clear(heads, done):
            for odd in range(2):
                own, other = 64 * odd, 64 - 64 * odd
                mine = slice(heads[0] + odd, heads[-1] + 1, 2)
                dve.memset(KS[other:other + 64, mine, :].bitcast(F32), 0.0).then_inc(done[0], 1)
                dve.memset(KS[own + 32:own + 64, mine, :].bitcast(F32), 1.0).then_inc(done[0], 1)

        @block.sync
        def _(eng):
            def load_x(b):
                row = b.times(T)
                src = x[bass.ds(row, T), :] if b.register is not None else x[row:row + T, :]
                sp.dma_start(XIN[:, :, :], src.rearrange("(t p) c -> p t c", p=P)).then_inc(s_x[0], 16)

            def iteration(b, a, n):
                if a:
                    stacks(a)
                    if n:
                        eng.wait_ge(s_pv[0], upto(a, s_pv, 16))
                        load_x(n)
                    results(a)
                elif n:
                    eng.wait_ge(s_h[0], upto(n, s_h, 0))
                    load_x(n)

            def stacks(b):
                eng.wait_ge(s_scat[0], upto(b, s_scat, 16 * NT))
                sp.dma_start(SEL[:, :, :], kept_d.rearrange("(t p) c -> p t c", p=P)).then_inc(s_sel[0], 16)
                for odd in range(2):
                    at = 64 * odd + 3 * DH
                    sp.dma_start(QS[at:at + 2, :, :].bitcast(F32),
                                 att_d[CAP:CAP + 32].rearrange("(a j r) c -> a j (r c)", a=2, r=2))\
                      .then_inc(s_qz[0], 16)
                restack(sp, eng, b, 1, s_kw, KS, (2, 3, 2))
                for half in range(2):
                    eng.wait_ge(s_ml[0], upto(b, s_ml, half + 1))
                    sp.dma_start(max_d[half], MHL.bitcast(F32)).then_inc(s_mw[0], 16)
                    eng.wait_ge(s_mw[0], upto(b, s_mw, 16 * (half + 1)))
                    for odd in range(2):
                        at = 64 * odd + 3 * DH
                        sp.dma_start(QS[at:at + 2, 4 * half:4 * half + 4, :].bitcast(F32),
                                     max_d[half].rearrange("(j r) a n -> r a j n", r=2)[odd])\
                          .then_inc(s_mi[0], 16)

            def results(b):
                eng.wait_ge(s_o[0], upto(b, s_o, 2))
                sp.dma_start(att_d[0:CAP].rearrange("(t p) c -> p t c", p=P), SEL[:, :, :]).then_inc(s_ow[0], 16)
                for half in range(2):
                    eng.wait_ge(s_fin[0], upto(b, s_fin, 4 * (half + 1)))
                    row = b.times(T, 512 * half)
                    dst = out[bass.ds(row, 512), :] if b.register is not None else out[row:row + 512, :]
                    sp.dma_start(dst.rearrange("(t p) c -> p t c", p=P),
                                 H2[:, 4 * half:4 * half + 4, :]).then_inc(s_out[0], 16)

            sp.dma_start(IDN[:], identity).then_inc(s_w0[0], 16)
            load_x(Lap(0))
            for buf, src in FIRST[1:]:
                sp.dma_start(buf[:], src).then_inc(s_w0[0], 16)
            for buf, src in LOADS:
                sp.dma_start(buf[:], src).then_inc(s_w[0], 16)
            eng.wait_ge(s_zero[0], 1)
            sp.dma_start(att_d[CAP:T].rearrange("(t p) c -> p t c", p=P), GA[:, 0:KT, :]).then_inc(s_w[0], 16)
            every_batch(lambda n: None, iteration, eng)
            eng.wait_ge(s_out[0], 32 * B)
            eng.wait_ge(s_w[0], ALL_LOADED)

        @block.gpsimd
        def _(eng):
            def hold(cell):
                pool.tensor_tensor(HOLD[:, cell:cell + 1], HALF[:, 0:1], HALF[:, 0:1], ALU.mult)

            def power(b, dst, src, n, need, k, done):
                eng.wait_ge(need[0], upto(b, need, k))
                pool.tensor_tensor(dst, src, HALF[:, 0:n], ALU.pow).then_inc(done[0], 1)

            def scatter(b, half):
                eng.wait_ge(s_rank[0], upto(b, s_rank, 2 * half + 2))
                if half == 0:
                    eng.wait_ge(s_ti[0], upto(b, s_ti, NT))
                    eng.wait_ge(s_sel[0], upto(b, s_sel, 0))
                hold(1 + half)
                for t in range(4 * half, 4 * half + 4):
                    pool.indirect_dma_start(
                        out=kept_d, out_offset=bass.IndirectOffsetOnAxis(ap=RANK[:, t:t + 1], axis=0),
                        in_=KB[:, :, :].rearrange("p a t -> p (a t)")[:, C * t:C * t + C], in_offset=None,
                        bounds_check=CAP - 1, oob_is_err=False).then_inc(s_scat[0], 16)

            def gather(b):
                eng.wait_ge(s_ow[0], upto(b, s_ow, 16))
                hold(3)
                for t in range(NT):
                    pool.indirect_dma_start(
                        out=GA[:, t, :], out_offset=None, in_=att_d,
                        in_offset=bass.IndirectOffsetOnAxis(ap=RANK[:, t:t + 1], axis=0))\
                        .then_inc(s_gath[t // KT][0], 16)

            def first_norm(n):
                power(n, RS[:, :], VE[:, :], 2 * NT, s_ve, 4, s_rs)

            def third_norm(b, q):
                n = NT // NQ
                power(b, RS3[:, n * q:n * q + n], VE3[:, n * q:n * q + n], n, s_ve3, q + 1, s_rs3)

            def iteration(b, a, n):
                if a:
                    restack(pool, eng, a, 0, s_qw, QS, (0, 0, 1), lambda cell: hold(5 + cell))
                if b:
                    power(b, RS2[:, :], VE2[:, :], NT, s_ve2, 1, s_rs2)
                if a:
                    gather(a)
                if b:
                    third_norm(b, 0)
                    third_norm(b, 1)
                if n:
                    first_norm(n)
                if b:
                    scatter(b, 0)
                    scatter(b, 1)

            pool.memset(HALF[:], -0.5).then_inc(s_const[0], 1)
            pool.memset(XN[:, :, 0:1], 0.0).then_inc(s_const[0], 1)
            pool.memset(PP[:, 0:1], NEG).then_inc(s_const[0], 1)
            pool.memset(GA, 0.0).then_inc(s_zero[0], 1)
            pool.memset(VV[:], 1.0).then_inc(s_room[0], 1)
            pool.memset(QS[:].bitcast(F32), 0.0).then_inc(s_room[0], 1)
            eng.wait_ge(s_const[0], 3)
            hold(4)
            every_batch(first_norm, iteration, eng)

        @block.tensor
        def _(eng):
            def ring(b, first):
                use = [first]

                def bank(a=None):
                    u = use[0]
                    use[0] += 1
                    who, k = emptied[u - 3]
                    if a:
                        who, k = emptied3[u % 3 - 3]
                        eng.wait_ge(who[0], upto(a, who, k))
                    elif u >= 3:
                        eng.wait_ge(who[0], upto(b, who, k))
                    elif b.plus:
                        eng.wait_ge(who[0], upto(b, who, k - who[1]))
                    return PA[:, u % 3, :]

                return use, bank

            def filled(last_instruction):
                last_instruction.then_inc(s_pa[0], 1)

            def to_channels(b, bank, src, need):
                for c in range(CH):
                    for q in range(NQ):
                        dst = bank()
                        for i in range(4):
                            t = 4 * q + i
                            if need is not None:
                                eng.wait_ge(need[0], upto(b, need, t + 1))
                            m = pe.transpose(dst[:, P * i:P * i + P], src(t, c), IDN[:, :])
                        filled(m)

            def pooling_filled(last_instruction):
                last_instruction.then_inc(s_pp2[0], 1)

            def turn_x(n, a):
                eng.wait_ge(s_x[0], upto(n, s_x, 16))
                for c in range(CH):
                    if a:
                        who, k = emptied2[c - 2]
                        eng.wait_ge(who[0], upto(a, who, k))
                    elif n.plus:
                        who = (s_hT, s_en)[c]
                        eng.wait_ge(who[0], upto(n, who, 1 - who[1]))
                    for t in range(NT):
                        m = pe.transpose(PC[:, c, t // 4, P * (t % 4):P * (t % 4) + P],
                                         XIN[:, t, P * c:P * c + P], IDN[:, :])
                    pooling_filled(m)

            def tanh_layer(n):
                eng.wait_ge(s_xT[0], upto(n, s_xT, 2))
                for q in range(NQ):
                    for c in range(CH):
                        m = pe.matmul(PC[:, 0, q, :], W1[:, c, :], XT[:, c, TQ * q:TQ * q + TQ],
                                      start=c == 0, stop=c == CH - 1)
                pooling_filled(m)

            def energies(n):
                eng.wait_ge(s_hT[0], upto(n, s_hT, 1))
                for t in range(NT):
                    m = pe.matmul(PC[:, 1, 0, t:t + 1], HT[:, P * t:P * t + P], W2[:, :], start=True, stop=True)
                pooling_filled(m)

            def gate_rows(b, a, n):
                eng.wait_ge(s_g[0], upto(b, s_g, 2))
                for q in range(2):
                    if n:
                        who = (s_hT, s_en)[q]
                        eng.wait_ge(who[0], upto(n, who, 1))
                    else:
                        who, k = emptied2[q - 2]
                        eng.wait_ge(who[0], upto(a, who, k))
                    for i in range(4):
                        t = 4 * q + i
                        m = pe.transpose(PC[:, q, 0, P * i:P * i + P], GC[:, t:t + 1].broadcast_to([P, P]), IDN[:, :])
                    m.then_inc(s_gf[0], 1)

            def norm(b):
                use, bank = ring(b, NORM_FROM)
                to_channels(b, bank, lambda t, c: VT[:, t, P * c:P * c + P], s_xn)

            def project(b, i):
                use, bank = ring(b, KVR_FROM + i)
                w, src, need = ((WK, MB, s_mk), (WV, VR[:, 1, :, :], s_mv), (WR, EB, s_mr))[i // 4]
                d, q = divmod(i % 4, NQ)
                dst = bank()
                for c in range(CH):
                    eng.wait_ge(need[0], upto(b, need, c + 1))
                    m = pe.matmul(dst, w[:, c, P * d:P * d + P], src[:, c, TQ * q:TQ * q + TQ],
                                  start=c == 0, stop=c == CH - 1)
                filled(m)

            def output(b, a):
                use, bank = ring(b, MLP_FROM)
                assert MLP_FROM % 3 == KVR_FROM % 3
                for i in range(4):
                    dst = bank(a if i < 3 else None)
                    for j in range(2):
                        t = 2 * i + j
                        for d in range(CH):
                            eng.wait_ge(s_rw[0], upto(b, s_rw, d + 1))
                            m = pe.matmul(dst[:, C * j:C * j + C], KB[:, d, P * t:P * t + P], WO[:, d, :],
                                          start=d == 0, stop=d == CH - 1)
                    filled(m)

            def norm2(b):
                use, bank = ring(b, MLP_FROM + 4)
                to_channels(b, bank, lambda t, c: VT[:, t, P * c:P * c + P], s_xn2)

            def ffn_gate(b, q):
                use, bank = ring(b, FFN_FROM + 12 * q)
                for i in range(2):
                    dst = bank()
                    for j in range(2):
                        t = 4 * q + 2 * i + j
                        for c in range(CH):
                            eng.wait_ge(s_mr2[0], upto(b, s_mr2, c + 1))
                            m = pe.matmul(dst[:, C * j:C * j + C], MB[:, c, P * t:P * t + P], WRF[:, c, :],
                                          start=c == 0, stop=c == CH - 1)
                    filled(m)

            def hidden(b, q, blocks):
                use, bank = ring(b, FFN_FROM + 12 * q + 2 + blocks[0])
                for f in blocks:
                    dst = bank()
                    for c in range(CH):
                        eng.wait_ge(s_mk2[0], upto(b, s_mk2, c + 1))
                        m = pe.matmul(dst, WKF[:, c, P * f:P * f + P], MA[:, c, TQ * q:TQ * q + TQ],
                                      start=c == 0, stop=c == CH - 1)
                    filled(m)

            def hidden_products(b, q):
                use, bank = ring(b, FFN_FROM + 12 * q + 10)
                for i in range(2):
                    dst = bank()
                    for j in range(2):
                        for f in range(NF):
                            eng.wait_ge(s_hid[0], upto(b, s_hid, NF * q + f + 1))
                            t = 2 * i + j
                            m = pe.matmul(dst[:, C * j:C * j + C], HID[:, f, P * t:P * t + P], WVF[:, f, :],
                                          start=f == 0, stop=f == NF - 1)
                    filled(m)

            def pair(b, name):
                u = pair_use[name]
                who, k = emptied2[u - 2] if u >= 2 else (s_grow, u + 1)
                eng.wait_ge(who[0], upto(b, who, k))
                return PC[:, u % 2, :, :]

            def pair_filled(last_instruction):
                last_instruction.then_inc(s_pc[0], 1)

            def kept(b):
                dst = pair(b, "kept")
                eng.wait_ge(s_sel[0], upto(b, s_sel, 16))
                for c in range(CH):
                    for t in range(KT):
                        m = pe.transpose(dst[:, c, P * t:P * t + P], SEL[:, t, P * c:P * c + P], IDN[:, :])
                pair_filled(m)
                eng.wait_ge(s_at[0], upto(b, s_at, 1))
                for n, w in enumerate((WQ2, WK2)):
                    dst = pair(b, "qk"[n])
                    for d in range(CH):
                        for c in range(CH):
                            m = pe.matmul(dst[:, d, :], w[:, c, P * d:P * d + P], AT[:, c, :],
                                          start=c == 0, stop=c == CH - 1)
                    pair_filled(m)
                for n in range(2):
                    dst = pair(b, ("v", n))
                    for i in range(2):
                        t = 2 * n + i
                        for c in range(CH):
                            m = pe.matmul(dst[:, 0, C * i:C * i + C], AT[:, c, P * t:P * t + P],
                                          WV2[:, c, :], start=c == 0, stop=c == CH - 1)
                    pair_filled(m)

            def query_scores(b, h):
                if h == 0:
                    eng.wait_ge(s_qz[0], upto(b, s_qz, 32))
                    eng.wait_ge(s_qi[0], upto(b, s_qi, 16 * 6))
                    eng.wait_ge(s_ki[0], upto(b, s_ki, 16 * 6))
                for n in range(2):
                    dst = pair(b, ("max", h, n))
                    for i in range(2):
                        t = 2 * n + i
                        m = pe.matmul(dst[:, i, :], QS[:, h // 2, P * t:P * t + P], KS[:, h, :],
                                      start=True, stop=True)
                    pair_filled(m)

            def max_bank(a, b, u):
                if u >= 3:
                    who, k = emptied3[u - 3]
                    eng.wait_ge(who[0], upto(a, who, k))
                elif b:
                    who, k = emptied[MLP_FROM - 3 + u]
                    eng.wait_ge(who[0], upto(b, who, k))
                else:
                    who, k = emptied[u - 3]
                    eng.wait_ge(who[0], upto(a, who, k))
                return PA[:, (MLP_FROM + u) % 3, :]

            def later_query_scores(a, b, h):
                for t in range(KT):
                    dst = max_bank(a, b, 4 * (h - 8) + t)
                    pe.matmul(dst, QS[:, h // 2, P * t:P * t + P], KS[:, h, :],
                              start=True, stop=True).then_inc(s_pm[0], 1)

            def maxima_rows(a, b, half):
                dst = max_bank(a, b, s_pm[1] - 1) if half else pair(a, ("rows", 0))[:, 0, :]
                eng.wait_ge(s_nm[0], upto(a, s_nm, 48 if half else 16))
                for t in range(KT):
                    m = pe.transpose(dst[0:8, P * t:P * t + P], NM[:, t, 8 * half:8 * half + 8], IDN[:, :])
                m.then_inc((s_pm if half else s_pc)[0], 1)

            def key_scores(b, step):
                if step in (0, 8):
                    eng.wait_ge(s_mi[0], upto(b, s_mi, 32 if step == 0 else 64))
                g, t = divmod(step, KT)
                for n in range(2):
                    dst = pair(b, ("exp", step, n))
                    j = 2 * g + n
                    for i in range(2):
                        m = pe.matmul(dst[:, i, :], KS[:, 2 * j + i, P * t:P * t + P], QS[:, j, :],
                                      start=True, stop=True)
                    pair_filled(m)

            def values(b, step):
                g, t = divmod(step, KT)
                if step == 0:
                    eng.wait_ge(s_vv[0], upto(b, s_vv, 2))
                eng.wait_ge(s_p[0], upto(b, s_p, 2 * step + 2))
                if t == 0:
                    eng.wait_ge(s_oT[0], upto(b, s_oT, g))
                for i in range(4):
                    probs = SLOTS[(2 * step + i // 2) % 4]
                    m = pe.matmul(PO[32 * i:32 * i + 32, :], VV[:, t, 4 * g + i, :], probs[:, i % 2, :],
                                  start=t == 0, stop=t == KT - 1, tile_position=(0, 32 * i))
                m.then_inc(s_pv[0], 1)

            def sums(b):
                for n in range(2):
                    dst = pair(b, ("sums", n))
                    for i in range(2):
                        g = 2 * n + i
                        eng.wait_ge(s_oT[0], upto(b, s_oT, g + 1))
                        for t in range(KT):
                            m = pe.transpose(dst[:, i, P * t:P * t + P], OT[:, g, P * t:P * t + P], IDN[:, :])
                    pair_filled(m)

            def inverse_sums(b):
                for n in range(2):
                    dst = pair(b, ("inverse", n))
                    eng.wait_ge(s_rw2[0], upto(b, s_rw2, n + 1))
                    for i in range(2):
                        for t in range(KT):
                            m = pe.transpose(dst[:, i, P * t:P * t + P],
                                             RWIDE[n][:, i, t, :], IDN[:, :])
                    pair_filled(m)

            def head_output(b):
                eng.wait_ge(s_on[0], upto(b, s_on, 2))
                for n in range(2):
                    dst = pair(b, ("out", n))
                    for i in range(2):
                        t = 2 * n + i
                        for g in range(NG):
                            m = pe.matmul(dst[:, 0, C * i:C * i + C], OT[:, g, P * t:P * t + P],
                                          WO2[:, g, :], start=g == 0, stop=g == NG - 1)
                    pair_filled(m)

            def first_norm(n):
                turn_x(n, None)
                tanh_layer(n)
                energies(n)
                norm(n)
                eng.wait_ge(s_w[0], ALL_LOADED)
                eng.wait_ge(s_room[0], 6)

            def iteration(b, a, n):
                if b:
                    for i in range(EARLY):
                        project(b, i)
                if a:
                    kept(a)
                if b:
                    for i in range(EARLY, 8):
                        project(b, i)
                for h in range(H // 2):
                    if a:
                        query_scores(a, h)
                    if b and h in R_BESIDE:
                        project(b, 8 + R_BESIDE.index(h))
                if a:
                    maxima_rows(a, b, 0)
                for step in range(NG * KT):
                    if a:
                        key_scores(a, step)
                        if step:
                            values(a, step - 1)
                        for h in BESIDE.get(step, ()):
                            later_query_scores(a, b, h)
                        if step == ROWS_STEP:
                            maxima_rows(a, b, 1)
                    if b and step == WO_STEP:
                        output(b, a)
                if a:
                    values(a, NG * KT - 1)
                    sums(a)
                if b:
                    norm2(b)
                if a:
                    inverse_sums(a)
                if b:
                    ffn_gate(b, 0)
                if a:
                    head_output(a)
                if b:
                    hidden(b, 0, range(NF))
                    hidden_products(b, 0)
                    ffn_gate(b, 1)
                if n:
                    turn_x(n, a)
                if b:
                    hidden(b, 1, range(4))
                if n:
                    tanh_layer(n)
                if b:
                    hidden(b, 1, range(4, NF))
                if n:
                    energies(n)
                if b:
                    hidden_products(b, 1)
                if b:
                    gate_rows(b, a, n)
                if n:
                    norm(n)

            eng.wait_ge(s_w0[0], FIRST_LOADED)
            eng.wait_ge(s_const[0], 3)
            every_batch(first_norm, iteration, eng)

        @block.scalar
        def _(eng):
            def ring(b, first):
                use = [first]

                def bank():
                    u = use[0]
                    use[0] += 1
                    eng.wait_ge(s_pa[0], upto(b, s_pa, u + 1))
                    return PA[:, u % 3, :]

                return use, bank

            def x_turned(n):
                eng.wait_ge(s_mk2[0], upto(n, s_mk2, 0))
                for c in range(CH):
                    eng.wait_ge(s_pp2[0], upto(n, s_pp2, c + 1))
                    act.activation(XT[:, c, :], PC[:, c, :, :].rearrange("p i t -> p (i t)"), ACT.Copy)\
                       .then_inc(s_xT[0], 1)

            def tanh_layer(n):
                act.preload_act_table_set("exp_and_others")
                eng.wait_ge(s_pp2[0], upto(n, s_pp2, 3))
                act.activation(HT, PC[:, 0, :, :].rearrange("p i t -> p (i t)"), ACT.Tanh, bias=B1[:, :])\
                   .then_inc(s_hT[0], 1)

            def energies(n):
                eng.wait_ge(s_en[0], upto(n, s_en, 3))
                act.activation(ENE[:, :, 0], END[:, :], ACT.Exp).then_inc(s_ee[0], 1)

            def norm(b):
                use, bank = ring(b, NORM_FROM)
                for c in range(CH):
                    for q in range(NQ):
                        src = bank()
                        act.activation(XN[:, c, 1 + TQ * q:1 + TQ * q + TQ], src, ACT.Identity,
                                       scale=vec("ln1_g", c), bias=vec("ln1_b", c)).then_inc(s_xnT[0], 1)

            def copy_banks(b, dst, first, done):
                use, bank = ring(b, first)
                for d in range(CH):
                    for q in range(NQ):
                        src = bank()
                        act.activation(dst[:, d, TQ * q:TQ * q + TQ], src, ACT.Copy).then_inc(done[0], 1)

            def project_v(b):
                copy_banks(b, VR[:, 0, :, :], KVR_FROM + 4, s_v)

            def project_k(b):
                eng.wait_ge(s_scat[0], upto(b, s_scat, 0))
                copy_banks(b, KB, KVR_FROM, s_k)

            def project_r(b):
                copy_banks(b, VR[:, 1, :, :], KVR_FROM + 8, s_r)

            def r_exp(b, d):
                eng.wait_ge(s_r[0], upto(b, s_r, 2 * d + 2))
                eng.wait_ge(s_nd[0], upto(b, s_nd, 6 * d))
                if d == 0:
                    eng.wait_ge(s_cnt[0], upto(b, s_cnt, 0))
                act.activation(EE[:, :], VR[:, 1, d, :], ACT.Abs).then_inc(s_er[0], 1)
                eng.wait_ge(s_er[0], upto(b, s_er, 2 * d + 1))
                act.activation(EE[:, :], EE[:, :], ACT.Exp, scale=-1.0).then_inc(s_er[0], 1)

            def wkv_exp(b, d, i):
                buf, sign, step = ((E1, -1.0, 2), (E2, 1.0, 3), (EB[:, 0, :], 1.0, 4), (EB[:, 1, :], 1.0, 5))[i]
                eng.wait_ge(s_d[0], upto(b, s_d, 5 * d + step))
                act.activation(buf, buf, ACT.Exp, scale=sign).then_inc(s_ex[0], 1)

            def wkv_quotient(b, d, i):
                if i == 0:
                    eng.wait_ge(s_nd[0], upto(b, s_nd, 7 * d + 6))
                    act.activation(EB[:, 0, :], EB[:, 1, :], ACT.Ln).then_inc(s_y[0], 1)
                else:
                    eng.wait_ge(s_nd[0], upto(b, s_nd, 7 * d + 7))
                    act.activation(EB[:, 0, :], EB[:, 0, :], ACT.Exp).then_inc(s_y[0], 1)

            def norm2(b):
                use, bank = ring(b, MLP_FROM + 4)
                for c in range(CH):
                    for q in range(NQ):
                        src = bank()
                        act.activation(XN[:, c, 1 + TQ * q:1 + TQ * q + TQ], src, ACT.Identity,
                                       scale=vec("ln2_g", c), bias=vec("ln2_b", c)).then_inc(s_xn2T[0], 1)

            def ffn_gate(b, q):
                use, bank = ring(b, FFN_FROM + 12 * q)
                LG = EB[:, :, :].rearrange("p c t -> p (c t)")[:, 2 * TQ * q:2 * TQ * q + 2 * TQ]
                eng.wait_ge(s_mk2[0], upto(b, s_mk2, 2))
                for i in range(2):
                    src = bank()
                    act.activation(LG[:, TQ * i:TQ * i + TQ], src, ACT.Copy).then_inc(s_r2[0], 1)

            def log_gate(b, q):
                LG = EB[:, :, :].rearrange("p c t -> p (c t)")[:, 2 * TQ * q:2 * TQ * q + 2 * TQ]
                eng.wait_ge(s_r2[0], upto(b, s_r2, 2 * q + 2))
                eng.wait_ge(s_x3[0], upto(b, s_x3, 2 * q))
                act.activation(EE[:, :], LG, ACT.Abs).then_inc(s_r2e[0], 1)
                eng.wait_ge(s_r2e[0], upto(b, s_r2e, 4 * q + 1))
                act.activation(EE[:, :], EE[:, :], ACT.Exp, scale=-1.0).then_inc(s_r2e[0], 1)
                eng.wait_ge(s_r2e[0], upto(b, s_r2e, 4 * q + 2))
                act.activation(EE[:, :], EE[:, :], ACT.Ln, bias=1.0).then_inc(s_r2e[0], 1)

            def hidden(b, q, blocks):
                use, bank = ring(b, FFN_FROM + 12 * q + 2 + blocks[0])
                for f in blocks:
                    src = bank()
                    n = NF * q + f
                    tmp = V2[:, TQ * (f % 2):TQ * (f % 2) + TQ]
                    eng.wait_ge(s_hid[0], upto(b, s_hid, n))
                    act.activation(tmp, src, ACT.Relu).then_inc(s_relu[0], 1)
                    eng.wait_ge(s_relu[0], upto(b, s_relu, n + 1))
                    act.activation(HID[:, f, :], tmp, ACT.Square).then_inc(s_hid[0], 1)
                    if f == 1:
                        eng.wait_ge(s_g2[0], upto(b, s_g2, q + 1))
                        act.activation(EE[:, :], EE[:, :], ACT.Exp).then_inc(s_r2e[0], 1)

            def gate(b):
                eng.wait_ge(s_z[0], upto(b, s_z, NT))
                act.activation(ZE[:, :], ZC[:, :], ACT.Exp, scale=-1.0).then_inc(s_ze[0], 1)
                for q in range(2):
                    eng.wait_ge(s_gf[0], upto(b, s_gf, q + 1))
                    act.activation(GROWS[:, TQ * q:TQ * q + TQ], PC[:, q, 0, :], ACT.Copy).then_inc(s_grow[0], 1)

            def pair(b, name):
                u = pair_use[name]
                eng.wait_ge(s_pc[0], upto(b, s_pc, u + 1))
                return PC[:, u % 2, :, :]

            def kept(b):
                src = pair(b, "kept")
                act.activation(AT[:, :, :], src, ACT.Copy).then_inc(s_at[0], 1)
                for i in range(2):
                    src = pair(b, "qk"[i])
                    if i == 0:
                        eng.wait_ge(s_fin[0], upto(b, s_fin, 0))
                    act.activation(QHL[i][:, 0, :, :], src, ACT.Copy).then_inc(s_qh[0], 1)
                for n in range(2):
                    src = pair(b, ("v", n))
                    act.activation(VV[:, 2 * n:2 * n + 2, :, 0:DH],
                                   src[:, 0, :].rearrange("p (t h d) -> p t h d", t=2, d=DH), ACT.Copy)\
                       .then_inc(s_vv[0], 1)

            def maxima_rows(b, half):
                if half:
                    eng.wait_ge(s_pm[0], upto(b, s_pm, s_pm[1]))
                    src = PA[:, (MLP_FROM - 1) % 3, :]
                else:
                    src = pair(b, ("rows", 0))[:, 0, :]
                    eng.wait_ge(s_kw[0], upto(b, s_kw, 32))
                if half:
                    eng.wait_ge(s_mw[0], upto(b, s_mw, 16))
                act.activation(MHL[:, 0, :], src[0:8, :], ACT.Copy).then_inc(s_mh[0], 1)

            def exps(b, step):
                for n in range(2):
                    src = pair(b, ("exp", step, n))
                    if step > 1:
                        eng.wait_ge(s_pv[0], upto(b, s_pv, step - 1))
                    elif step == 0:
                        eng.wait_ge(s_qw[0], upto(b, s_qw, 32))
                    act.activation(SLOTS[(2 * step + n) % 4], src, ACT.Exp, scale=0.25).then_inc(s_p[0], 1)
                g, t = divmod(step, KT)
                if t == 0 and g > 0:
                    heads_out(b, g - 1)

            def attention_out(b):
                for n in range(2):
                    src = pair(b, ("out", n))
                    act.activation(SEL[:, 2 * n:2 * n + 2, :], src[:, 0, :].rearrange("p (t c) -> p t c", c=C),
                                   ACT.Copy).then_inc(s_o[0], 1)

            def heads_out(b, g):
                eng.wait_ge(s_pv[0], upto(b, s_pv, KT * (g + 1)))
                act.activation(OT[:, g, :], PO[:, :], ACT.Copy).then_inc(s_oT[0], 1)

            def first_norm(n):
                x_turned(n)
                tanh_layer(n)
                energies(n)
                norm(n)

            def iteration(b, a, n):
                if a:
                    kept(a)
                if b:
                    project_k(b)
                    project_v(b)
                    act.preload_act_table_set("natural_log_exp_and_others")
                    wkv_exp(b, 0, 0)
                    wkv_exp(b, 0, 1)
                    project_r(b)
                if a:
                    maxima_rows(a, 0)
                if b:
                    r_exp(b, 0)
                    wkv_exp(b, 0, 2)
                    wkv_exp(b, 0, 3)
                for step in range(NG * KT):
                    if b:
                        if step == 1:
                            wkv_quotient(b, 0, 0)
                            r_exp(b, 1)
                        elif step == 2:
                            wkv_quotient(b, 0, 1)
                            wkv_exp(b, 1, 0)
                            wkv_exp(b, 1, 1)
                        elif step == 3:
                            wkv_exp(b, 1, 2)
                            wkv_exp(b, 1, 3)
                        elif step in (7, 8):
                            wkv_quotient(b, 1, step - 7)
                    if a:
                        exps(a, step)
                        if step == ROWS_STEP:
                            maxima_rows(a, 1)
                if a:
                    heads_out(a, NG - 1)
                if b:
                    norm2(b)
                    ffn_gate(b, 0)
                if a:
                    attention_out(a)
                if b:
                    log_gate(b, 0)
                    hidden(b, 0, range(NF))
                    ffn_gate(b, 1)
                    log_gate(b, 1)
                if n:
                    x_turned(n)
                if b:
                    hidden(b, 1, range(4))
                if n:
                    tanh_layer(n)
                if b:
                    hidden(b, 1, range(4, NF))
                if n:
                    energies(n)
                if b:
                    gate(b)
                if n:
                    norm(n)

            eng.wait_ge(s_w0[0], FIRST_LOADED)
            act.activation(DEC[:, :], VEC[:, VECTORS.index("decay"), :], ACT.Exp).then_inc(s_dec[0], 1)
            every_batch(first_norm, iteration, eng)

        @block.vector
        def _(eng):
            def stats(b, src, need, per, st, mv, tiles=range(NT)):
                first, n = tiles[0], len(tiles)
                for t in tiles:
                    eng.wait_ge(need[0], upto(b, need, t // per + 1))
                    dve.bn_stats(STATS[:, t, :], src[:, t, :]).then_inc(st[0], 1)
                eng.wait_ge(st[0], upto(b, st, 2 * first + n))
                dve.memset(HOLD[:, 0:1], 0.0)
                for t in tiles:
                    dve.bn_aggr(mv[:, t, :], STATS[:, t, :]).then_inc(st[0], 1)

            def ring(b, first):
                use = [first]

                def bank(skip=0):
                    use[0] += skip
                    u = use[0]
                    use[0] += 1
                    eng.wait_ge(s_pa[0], upto(b, s_pa, u + 1))
                    return PA[:, u % 3, :]

                return use, bank

            def mixed(b, done, dst, name, c):
                dve.scalar_tensor_tensor(dst[:, c, :], EB[:, c, :], vec(name, c), XN[:, c, 0:T],
                                         ALU.mult, ALU.add).then_inc(done[0], 1)

            def pooling(b):
                eng.wait_ge(s_pp2[0], upto(b, s_pp2, 4))
                dve.tensor_scalar(EN[:, :, 0], PC[:, 1, 0, 0:NT], B2[:, :], None, ALU.add).then_inc(s_en[0], 1)
                eng.wait_ge(s_en[0], upto(b, s_en, 1))
                dve.tensor_reduce(ENM[:, :], EN[:, :, :], AX.X, ALU.max).then_inc(s_en[0], 1)
                eng.wait_ge(s_en[0], upto(b, s_en, 2))
                dve.tensor_tensor(END[:, :], EN[:, :, 0], ENM[:, :], ALU.subtract).then_inc(s_en[0], 1)
                eng.wait_ge(s_ee[0], upto(b, s_ee, 1))
                dve.tensor_reduce(ENS[:, :], ENE[:, :, :], AX.X, ALU.add).then_inc(s_pw[0], 1)
                eng.wait_ge(s_pw[0], upto(b, s_pw, 1))
                dve.reciprocal(ENR[:, :], ENS[:, :]).then_inc(s_pw[0], 1)
                eng.wait_ge(s_pw[0], upto(b, s_pw, 2))
                dve.tensor_tensor(PW[:, :], ENE[:, :, 0], ENR[:, :], ALU.mult).then_inc(s_pw[0], 1)

            def pool(b):
                eng.wait_ge(s_h2[0], upto(b, s_h2, 0))
                eng.wait_ge(s_pw[0], upto(b, s_pw, 3))
                eng.wait_ge(s_x[0], upto(b, s_x, 16))
                for t in range(NT):
                    dve.tensor_scalar(HX[:, t, :], XIN[:, t, :], PW[:, t:t + 1], None, ALU.mult).then_inc(s_h[0], 1)

            def pooled_stats(b):
                stats(b, HX, s_h, 1, s_st, MV)
                eng.wait_ge(s_st[0], upto(b, s_st, 2 * NT))
                dve.tensor_scalar(VE[:, 0:NT], MV[:, :, 1], EPS, None, ALU.add).then_inc(s_ve[0], 1)
                eng.wait_ge(s_ve[0], upto(b, s_ve, 1))
                dve.reciprocal(SCR[:, :], VE[:, 0:NT]).then_inc(s_ve[0], 1)
                eng.wait_ge(s_ve[0], upto(b, s_ve, 2))
                dve.tensor_tensor(VE[:, NT:2 * NT], MV[:, :, 1], SCR[:, :], ALU.mult).then_inc(s_ve[0], 1)
                eng.wait_ge(s_ve[0], upto(b, s_ve, 3))
                dve.tensor_scalar(VE[:, NT:2 * NT], VE[:, NT:2 * NT], EPS, None, ALU.add).then_inc(s_ve[0], 1)

            def norm(b):
                eng.wait_ge(s_rs[0], upto(b, s_rs, 1))
                dve.tensor_tensor(SCR[:, :], RS[:, 0:NT], RS[:, NT:2 * NT], ALU.mult).then_inc(s_sc[0], 1)
                eng.wait_ge(s_sc[0], upto(b, s_sc, 1))
                for t in range(NT):
                    dve.tensor_scalar(VT[:, t, :], HX[:, t, :], MV[:, t, 0:1], SCR[:, t:t + 1],
                                      ALU.subtract, ALU.mult).then_inc(s_xn[0], 1)

            def residual(b):
                for t in range(NT):
                    dve.tensor_scalar(XA[:, t, :], HX[:, t, :], MV[:, t, 0:1], RS[:, t:t + 1],
                                      ALU.subtract, ALU.mult).then_inc(s_xa[0], 1)

            def mix(b):
                for c in range(CH):
                    eng.wait_ge(s_xnT[0], upto(b, s_xnT, 2 * c + 2))
                    dve.tensor_tensor(EB[:, c, :], XN[:, c, 1:T + 1], XN[:, c, 0:T], ALU.subtract)\
                       .then_inc(s_dx[0], 1)
                for c in range(CH):
                    eng.wait_ge(s_dx[0], upto(b, s_dx, c + 1))
                    mixed(b, s_mk, MB, "mix_k", c)

            def mix_v(b):
                for c in range(CH):
                    mixed(b, s_mv, VR[:, 1, :, :], "mix_v", c)

            def mix_r(b):
                for c in range(CH):
                    eng.wait_ge(s_mv[0], upto(b, s_mv, 2))
                    mixed(b, s_mr, EB, "mix_r", c)

            def wkv(b, d, steps):
                k, v, r = KB[:, d, :], VR[:, 0, d, :], VR[:, 1, d, :]
                before, now = PP[:, 0:T], PP[:, 1:T + 1]
                e1b, e2b = EB[:, 0, :], EB[:, 1, :]
                AA, BB = XN[:, 0, :], XN[:, 1, :]
                D, N = 5 * d, 7 * d
                if 0 in steps:
                    eng.wait_ge(s_k[0], upto(b, s_k, 4))
                    if d:
                        eng.wait_ge(s_d[0], upto(b, s_d, 5))
                    dve.tensor_tensor_scan(now, DECN[:, d:d + 1].broadcast_to([P, T]), k, NEG, ALU.add, ALU.max)\
                       .then_inc(s_pp[0], 1)
                if 1 in steps:
                    eng.wait_ge(s_pp[0], upto(b, s_pp, d + 1))
                    eng.wait_ge(s_k[0], upto(b, s_k, 4))
                    if d:
                        eng.wait_ge(s_nd[0], upto(b, s_nd, 5))
                    dve.scalar_tensor_tensor(E2, k, vec("first", d), before, ALU.add, ALU.subtract)\
                       .then_inc(s_d[0], 1)
                if 2 in steps:
                    eng.wait_ge(s_d[0], upto(b, s_d, D + 1))
                    dve.tensor_scalar(E1, E2, 0.0, None, ALU.max).then_inc(s_d[0], 1)
                if 3 in steps:
                    dve.tensor_scalar(E2, E2, 0.0, None, ALU.min).then_inc(s_d[0], 1)
                if 4 in steps:
                    eng.wait_ge(s_r[0], upto(b, s_r, 4))
                    eng.wait_ge(s_rw[0], upto(b, s_rw, d))
                    dve.scalar_tensor_tensor(e1b, before, DECN[:, d:d + 1], now, ALU.add, ALU.subtract)\
                       .then_inc(s_d[0], 1)
                if 5 in steps:
                    dve.tensor_tensor(e2b, k, now, ALU.subtract).then_inc(s_d[0], 1)
                if 7 in steps:
                    eng.wait_ge(s_v[0], upto(b, s_v, 4))
                    eng.wait_ge(s_ex[0], upto(b, s_ex, 4 * d + 4))
                    dve.tensor_tensor(V2[:, :], e2b, v, ALU.mult).then_inc(s_ev[0], 1)
                if 8 in steps:
                    dve.tensor_tensor_scan(BB[:, 1:T + 1], e1b, e2b, 0.0, ALU.mult, ALU.add).then_inc(s_ab[0], 1)
                if 9 in steps:
                    eng.wait_ge(s_ev[0], upto(b, s_ev, d + 1))
                    dve.tensor_tensor_scan(AA[:, 1:T + 1], e1b, V2[:, :], 0.0, ALU.mult, ALU.add)\
                       .then_inc(s_ab[0], 1)
                if 10 in steps:
                    eng.wait_ge(s_ex[0], upto(b, s_ex, 4 * d + 4))
                    eng.wait_ge(s_ab[0], upto(b, s_ab, 2 * d + 1))
                    dve.tensor_tensor(e2b, E1, BB[:, 0:T], ALU.mult).then_inc(s_nd[0], 1)
                if 11 in steps:
                    eng.wait_ge(s_ab[0], upto(b, s_ab, 2 * d + 2))
                    dve.tensor_tensor(V2[:, :], E1, AA[:, 0:T], ALU.mult).then_inc(s_nd[0], 1)
                if 12 in steps:
                    eng.wait_ge(s_nd[0], upto(b, s_nd, N + 1))
                    dve.tensor_tensor(e2b, e2b, E2, ALU.add).then_inc(s_nd[0], 1)
                if 13 in steps:
                    eng.wait_ge(s_nd[0], upto(b, s_nd, N + 2))
                    dve.tensor_tensor(E1, E2, v, ALU.mult).then_inc(s_nd[0], 1)
                if 14 in steps:
                    eng.wait_ge(s_nd[0], upto(b, s_nd, N + 4))
                    dve.tensor_tensor(V2[:, :], V2[:, :], E1, ALU.add).then_inc(s_nd[0], 1)
                if 15 in steps:
                    eng.wait_ge(s_er[0], upto(b, s_er, 2 * d + 2))
                    dve.scalar_tensor_tensor(e2b, EE[:, :], 1.0, e2b, ALU.add, ALU.mult).then_inc(s_nd[0], 1)
                if 16 in steps:
                    eng.wait_ge(s_y[0], upto(b, s_y, 2 * d + 1))
                    dve.scalar_tensor_tensor(e1b, r, 0.0, e1b, ALU.min, ALU.subtract).then_inc(s_nd[0], 1)
                if 17 in steps:
                    eng.wait_ge(s_y[0], upto(b, s_y, 2 * d + 2))
                    dve.tensor_tensor(KB[:, d, :], V2[:, :], e1b, ALU.mult).then_inc(s_rw[0], 1)

            def norm2(b):
                use, bank = ring(b, MLP_FROM)
                for i in range(4):
                    src = bank()
                    pair = XA[:, 2 * i:2 * i + 2, :].rearrange("p t c -> p (t c)")
                    if i == 0:
                        eng.wait_ge(s_xa[0], upto(b, s_xa, NT))
                    dve.tensor_tensor(pair, pair, src, ALU.add).then_inc(s_x2[0], 1)
                stats(b, XA, s_x2, 2, s_st2, MV2)
                eng.wait_ge(s_st2[0], upto(b, s_st2, 2 * NT))
                dve.tensor_scalar(VE2[:, :], MV2[:, :, 1], EPS, None, ALU.add).then_inc(s_ve2[0], 1)
                eng.wait_ge(s_rs2[0], upto(b, s_rs2, 1))
                for t in range(NT):
                    dve.tensor_scalar(VT[:, t, :], XA[:, t, :], MV2[:, t, 0:1], RS2[:, t:t + 1],
                                      ALU.subtract, ALU.mult).then_inc(s_xn2[0], 1)

            def mix2(b):
                for c in range(CH):
                    eng.wait_ge(s_xn2T[0], upto(b, s_xn2T, 2 * c + 2))
                    dve.tensor_tensor(EB[:, c, :], XN[:, c, 1:T + 1], XN[:, c, 0:T], ALU.subtract)\
                       .then_inc(s_dx2[0], 1)
                for c in range(CH):
                    eng.wait_ge(s_dx2[0], upto(b, s_dx2, c + 1))
                    mixed(b, s_mr2, MB, "ffn_mix_r", c)
                for c in range(CH):
                    mixed(b, s_mk2, MA, "ffn_mix_k", c)

            def ffn_gate(b, q):
                LG = EB[:, :, :].rearrange("p c t -> p (c t)")[:, 2 * TQ * q:2 * TQ * q + 2 * TQ]
                eng.wait_ge(s_r2e[0], upto(b, s_r2e, 4 * q + 3))
                dve.scalar_tensor_tensor(EE[:, :], LG, 0.0, EE[:, :], ALU.min, ALU.subtract)\
                   .then_inc(s_g2[0], 1)

            def ffn(b, q):
                use, bank = ring(b, FFN_FROM + 12 * q + 10)
                for i in range(2):
                    src = bank()
                    n = 2 * q + i
                    two = (slice(None), slice(2 * n, 2 * n + 2), slice(None))
                    flat = lambda z: z[two].rearrange("p t c -> p (t c)")
                    eng.wait_ge(s_r2e[0], upto(b, s_r2e, 4 * q + 4))
                    dve.tensor_tensor(EE[:, TQ * i:TQ * i + TQ], EE[:, TQ * i:TQ * i + TQ], src, ALU.mult)\
                       .then_inc(s_sk[0], 1)
                    eng.wait_ge(s_sk[0], upto(b, s_sk, n + 1))
                    dve.tensor_tensor(flat(XA), flat(XA), EE[:, TQ * i:TQ * i + TQ], ALU.add)\
                       .then_inc(s_x3[0], 1)
                    eng.wait_ge(s_x3[0], upto(b, s_x3, n + 1))
                    if n == 0:
                        eng.wait_ge(s_out[0], upto(b, s_out, 0))
                    dve.tensor_tensor(flat(H2), flat(HX), flat(XA), ALU.add).then_inc(s_h2[0], 1)

            def router(b, q):
                tiles = range(NT // NQ * q, NT // NQ * (q + 1))
                hi = tiles[-1] + 1
                lo = tiles[0]
                stats(b, H2, s_h2, 2, s_st3, MV3, tiles)
                eng.wait_ge(s_st3[0], upto(b, s_st3, 2 * hi))
                dve.tensor_scalar(VE3[:, lo:hi], MV3[:, lo:hi, 1], EPS, None, ALU.add).then_inc(s_ve3[0], 1)

            def router_logits(b, q):
                tiles = range(NT // NQ * q, NT // NQ * (q + 1))
                eng.wait_ge(s_rs3[0], upto(b, s_rs3, q + 1))
                for t in tiles:
                    dve.tensor_scalar(KBT[:, t, :], H2[:, t, :], MV3[:, t, 0:1], RS3[:, t:t + 1],
                                      ALU.subtract, ALU.mult).then_inc(s_ti[0], 1)
                for t in tiles:
                    eng.wait_ge(s_ti[0], upto(b, s_ti, t + 1))
                    if t:
                        eng.wait_ge(s_z[0], upto(b, s_z, t))
                    dve.tensor_tensor_reduce(out=EB[:, 0, 0:C], in0=KBT[:, t, :], in1=WG[:, :], scale=1.0, scalar=0.0,
                                             op0=ALU.mult, op1=ALU.add, accum_out=ZC[:, t:t + 1]).then_inc(s_z[0], 1)

            def gates(b):
                eng.wait_ge(s_ze[0], upto(b, s_ze, 1))
                dve.tensor_scalar(ZP[:, :], ZE[:, :], 1.0, None, ALU.add).then_inc(s_g[0], 1)
                eng.wait_ge(s_g[0], upto(b, s_g, 1))
                dve.reciprocal(GC[:, :], ZP[:, :]).then_inc(s_g[0], 1)
                eng.wait_ge(s_g[0], upto(b, s_g, 2))
                eng.wait_ge(s_fin[0], upto(b, s_fin, 0))
                dve.tensor_copy(G2[:, :], GC[:, :]).then_inc(s_g[0], 1)

            def rank(b, half):
                eng.wait_ge(s_grow[0], upto(b, s_grow, 2))
                rows, waste = GROWS, V2
                tiles = range(4 * half, 4 * half + 4)
                for t in tiles:
                    own = GC[:, t:t + 1]
                    eng.wait_ge(s_cnt[0], upto(b, s_cnt, 3 * t))
                    dve.tensor_scalar(waste[:, P * t:T], rows[:, P * t:T], own, None, ALU.is_gt, ALU.add,
                                      accum_out=CNT[:, t, 0:1]).then_inc(s_cnt[0], 1)
                    if t:
                        dve.tensor_scalar(waste[:, 0:P * t], rows[:, 0:P * t], own, None, ALU.is_ge, ALU.add,
                                          accum_out=CNT[:, t, 1:2]).then_inc(s_cnt[0], 1)
                    else:
                        dve.memset(CNT[:, t, 1:2], 0.0).then_inc(s_cnt[0], 1)
                    dve.scalar_tensor_tensor(MA[:, 0, 0:P], rows[:, P * t:P * t + P], own, LOW[:, :],
                                             ALU.is_equal, ALU.mult, accum_out=CNT[:, t, 2:3]).then_inc(s_cnt[0], 1)
                half_of = slice(4 * half, 4 * half + 4)
                eng.wait_ge(s_cnt[0], upto(b, s_cnt, 12 * half + 12))
                dve.tensor_reduce(RANKF[:, half_of], CNT[:, half_of, :], AX.X, ALU.add).then_inc(s_rank[0], 1)
                eng.wait_ge(s_rank[0], upto(b, s_rank, 2 * half + 1))
                if half == 0:
                    eng.wait_ge(s_gath[0][0], upto(b, s_gath[0], 0))
                    eng.wait_ge(s_gath[1][0], upto(b, s_gath[1], 0))
                dve.tensor_copy(RANK[:, half_of], RANKF[:, half_of]).then_inc(s_rank[0], 1)

            def pair(b, name):
                u = pair_use[name]
                eng.wait_ge(s_pc[0], upto(b, s_pc, u + 1))
                return PC[:, u % 2, :, :]

            def qk_low(b, i):
                src = pair(b, "qk"[i])
                eng.wait_ge(s_qh[0], upto(b, s_qh, i + 1))
                dve.tensor_tensor(QHL[i][:, 1, :, :], src, QHL[i][:, 0, :, :].bitcast(F32), ALU.subtract)\
                   .then_inc(s_ql[0], 1)

            def maxima(b, h, n):
                src = pair(b, ("max", h, n))
                dve.tensor_reduce(NM[:, 2 * n:2 * n + 2, h], src, AX.X, ALU.max, negate=True)\
                   .then_inc(s_nm[0], 1)

            def later_maxima(b, h, t):
                u = 4 * (h - 8) + t
                eng.wait_ge(s_pm[0], upto(b, s_pm, u + 1))
                dve.tensor_reduce(NM[:, t, h:h + 1], PA[:, (MLP_FROM + u) % 3, :], AX.X, ALU.max, negate=True)\
                   .then_inc(s_nm[0], 1)

            def max_low(b, half):
                if half:
                    eng.wait_ge(s_pm[0], upto(b, s_pm, s_pm[1]))
                    src = PA[:, (MLP_FROM - 1) % 3, :]
                else:
                    src = pair(b, ("rows", 0))[:, 0, :]
                eng.wait_ge(s_mh[0], upto(b, s_mh, half + 1))
                dve.tensor_tensor(MHL[:, 1, :], src[0:8, :], MHL[:, 0, :].bitcast(F32), ALU.subtract)\
                   .then_inc(s_ml[0], 1)

            def inverse_sums(b):
                for n in range(2):
                    src = pair(b, ("sums", n))
                    sums = src.rearrange("p g (t i w) -> p g t i w", t=KT, i=4)[:, :, :, :, DH]
                    dve.reciprocal(RSUM[:, 2 * n:2 * n + 2, :, :].rearrange("p g t i -> p (g t) i"),
                                   sums.rearrange("p g t i -> p (g t) i")).then_inc(s_rsum[0], 1)
                for n in range(2):
                    eng.wait_ge(s_rsum[0], upto(b, s_rsum, n + 1))
                    dve.tensor_copy(RWIDE[n].rearrange("p g t (i w) -> p (g t i) w", w=32),
                                    RSUM[:, 2 * n:2 * n + 2, :, :].rearrange("p g t i -> p (g t i)")
                                    .unsqueeze(2).broadcast_to([P, 32, 32])).then_inc(s_rw2[0], 1)

            def normalise(b):
                for n in range(2):
                    src = pair(b, ("inverse", n))
                    dve.tensor_tensor(OT[:, 2 * n:2 * n + 2, :], OT[:, 2 * n:2 * n + 2, :], src, ALU.mult)\
                       .then_inc(s_on[0], 1)

            def finish(b):
                for t in range(NT):
                    if t % KT == 0:
                        eng.wait_ge(s_gath[t // KT][0], upto(b, s_gath[t // KT], 16 * KT))
                    dve.scalar_tensor_tensor(H2[:, t, :], GA[:, t, :], G2[:, t:t + 1], H2[:, t, :],
                                             ALU.mult, ALU.add).then_inc(s_fin[0], 1)

            def first_norm(n):
                pooling(n)
                pool(n)
                pooled_stats(n)
                norm(n)
                mix(n)
                mix_v(n)
                mix_r(n)
                eng.wait_ge(s_w[0], ALL_LOADED)
                eng.wait_ge(s_room[0], 6)

            def iteration(b, a, n):
                if a:
                    if b:
                        eng.wait_ge(s_xz[0], upto(a, s_xz, 4))
                    clear(range(12, H), s_kz)
                    qk_low(a, 0)
                    eng.wait_ge(s_kz[0], upto(a, s_kz, 4))
                    qk_low(a, 1)
                if b:
                    residual(b)
                    wkv(b, 0, range(4))
                if a:
                    for h in range(H // 2):
                        for k in range(2):
                            maxima(a, h, k)
                    max_low(a, 0)
                if b:
                    wkv(b, 0, range(4, 13))
                beside = ((0, (13,)), (0, (14,)), (0, (15,)), (1, (0,)), (1, (1,)), (1, (2, 3)), (0, (16,)),
                          (0, (17,)), (1, (4,)), (1, (5,)), (1, ()), (1, (7,)), (1, (8,)), (1, (9,)), (1, (10,)),
                          (1, (11,)))
                for k in range(H):
                    if a:
                        for t in range(2):
                            later_maxima(a, H // 2 + k // 2, 2 * (k % 2) + t)
                    if b:
                        d, steps = beside[k]
                        wkv(b, d, steps)
                if b:
                    wkv(b, 1, (12,))
                if a:
                    max_low(a, 1)
                if b:
                    wkv(b, 1, range(13, 18))
                if b:
                    norm2(b)
                if a:
                    inverse_sums(a)
                if b:
                    mix2(b)
                if a:
                    normalise(a)
                if b:
                    ffn_gate(b, 0)
                if a:
                    finish(a)
                if b:
                    ffn(b, 0)
                    router(b, 0)
                    ffn_gate(b, 1)
                    router_logits(b, 0)
                if n:
                    pooling(n)
                if b:
                    ffn(b, 1)
                    router(b, 1)
                if n:
                    pool(n)
                if b:
                    router_logits(b, 1)
                if b:
                    gates(b)
                if n:
                    pooled_stats(n)
                if b:
                    rank(b, 0)
                if n:
                    norm(n)
                if b:
                    rank(b, 1)
                if n:
                    mix(n)
                    mix_v(n)
                    mix_r(n)
                    clear(range(8, 12), s_xz)

            eng.wait_ge(s_w0[0], FIRST_LOADED)
            eng.wait_ge(s_const[0], 3)
            eng.wait_ge(s_dec[0], 1)
            dve.tensor_scalar(DECN[:, :], DEC[:, :], -1.0, None, ALU.mult).then_inc(s_decn[0], 1)
            eng.wait_ge(s_decn[0], 1)
            clear(range(8), s_room)
            every_batch(first_norm, iteration, eng)


_ORDER = ["x", "vectors", "tok_w1", "tok_b1", "tok_w2", "tok_b2", "w_k", "w_v", "w_r", "w_o", "w_kf", "w_rf",
          "w_vf", "gate_w", "w_q2", "w_k2", "w_v2", "w_o2", "identity", "lower"]


def kernel(**inputs):
    import concourse.bacc as bacc
    from concourse.bass_utils import run_bass_kernel_spmd

    a = {k: np.asarray(v) for k, v in inputs.items()}

    def rows(w):
        return np.ascontiguousarray(w.reshape(-1, P, w.shape[1]).transpose(1, 0, 2))

    by_name = {
        "ln1_g": "L0_attn_ln1_g", "ln1_b": "L0_attn_ln1_b", "ln2_g": "L0_attn_ln2_g", "ln2_b": "L0_attn_ln2_b",
        "mix_k": "L0_attn_att_mix_k", "mix_v": "L0_attn_att_mix_v", "mix_r": "L0_attn_att_mix_r",
        "decay": "L0_attn_time_decay", "first": "L0_attn_time_first",
        "ffn_mix_k": "L0_attn_ffn_mix_k", "ffn_mix_r": "L0_attn_ffn_mix_r",
    }
    vectors = np.stack([a[by_name[n]].reshape(CH, P) for n in VECTORS]).transpose(2, 0, 1)
    w_o2 = np.zeros((NG, 4, 32, C), np.float32)
    w_o2[:, :, :DH] = a["L0_ffn_Wo"].reshape(NG, 4, DH, C)
    arrays = {
        "x": a["x"].reshape(B * T, C),
        "vectors": np.ascontiguousarray(vectors),
        "tok_w1": rows(a["L0_tok_W1"]),
        "tok_b1": a["L0_tok_b1"].reshape(P, 1),
        "tok_w2": a["L0_tok_W2"].reshape(P, 1),
        "tok_b2": np.ascontiguousarray(np.broadcast_to(a["L0_tok_b2"].reshape(1, 1), (P, 1))),
        "w_k": rows(a["L0_attn_Wk"].T), "w_v": rows(a["L0_attn_Wv"].T), "w_r": rows(a["L0_attn_Wr"].T),
        "w_o": rows(a["L0_attn_Wo"].T), "w_kf": rows(a["L0_attn_Wk_ffn"].T),
        "w_rf": rows(a["L0_attn_Wr_ffn"].T), "w_vf": rows(a["L0_attn_Wv_ffn"].T),
        "gate_w": np.ascontiguousarray(np.broadcast_to(a["L0_ffn_Wg"].reshape(1, C), (P, C))),
        "w_q2": rows(a["L0_ffn_Wq"]), "w_k2": rows(a["L0_ffn_Wk"]), "w_v2": rows(a["L0_ffn_Wv"]),
        "w_o2": np.ascontiguousarray(w_o2.reshape(NG, P, C).transpose(1, 0, 2)),
        "identity": np.eye(P, dtype=np.float32),
        "lower": np.tril(np.ones((P, P), np.float32), -1),
    }
    nc = bacc.Bacc("TRN2", target_bir_lowering=False, num_devices=1)
    args = [nc.dram_tensor(f"in_{n}", arrays[n].shape, mybir.dt.from_np(arrays[n].dtype),
                           kind="ExternalInput").ap() for n in _ORDER]
    result = nc.dram_tensor("out_tokens", (B * T, C), F32, kind="ExternalOutput").ap()
    vit_tower(nc, *args, result)
    r = run_bass_kernel_spmd(nc, [{f"in_{n}": arrays[n] for n in _ORDER}], core_ids=[0])
    return r.results[0]["out_tokens"].reshape(B, T, C)
```
